# Optimizing a Trainium2 kernel written in Bass

```python
import numpy as np
import jax
import jax.numpy as jnp

def _softmax(x, axis=-1):
    return jax.nn.softmax(x, axis=axis)

def _gelu(x):
    return jax.nn.gelu(x, approximate=True)

def _silu(x):
    return jax.nn.silu(x)

def _sigmoid(x):
    return jax.nn.sigmoid(x)

def _layernorm(x, axis=-1, eps=1e-05):
    m = jnp.mean(x, axis=axis, keepdims=True)
    v = jnp.var(x, axis=axis, keepdims=True)
    return (x - m) / jnp.sqrt(v + eps)

def _scatter_add(tgt, idx, src, axis=0):
    return tgt.at[idx].add(src)

def _segment_sum(src, seg, n):
    return jax.ops.segment_sum(src, seg, n)
kernel_name = 'mk_gnn_ffn_d1_gnn_r32_93b463'

def setup_inputs(seed: int=0):
    np.random.seed(seed)
    _w = jnp.asarray

    def _rec_inputs():
        import jax
        import jax.numpy as jnp
        _gk = jax.random.key(seed)
        x = -0.0003713 + 1 * jax.random.normal(jax.random.fold_in(_gk, 1), (3125, 256), jnp.float32)
        src = jax.random.randint(jax.random.fold_in(_gk, 2), (50000,), 0, 3125, jnp.int32)
        dst = jax.random.randint(jax.random.fold_in(_gk, 3), (50000,), 0, 3125, jnp.int32)
        _o = jnp.argsort(dst, stable=True)
        src = src[_o]
        dst = dst[_o]
        edge_attr_18 = 0.00023367 + 0.999922 * jax.random.normal(jax.random.fold_in(_gk, 11), (50000, 18), jnp.float32)
        return (x, src, dst, edge_attr_18)
    x, src, dst, edge_attr_18 = _rec_inputs()

    def _L0_gnn_setup():
        import jax, jax.numpy as jnp
        import numpy as np
        N, E = (50000, 25000)
        DIM, H, D = (256, 16, 8)
        DH = D * H
        IN_RPE = 18
        SCALE = D ** (-0.5)
        EPS = 1e-16

        def _segment_softmax(compat, s, num_nodes):
            m = jax.ops.segment_max(compat, s, num_segments=num_nodes)
            ex = jnp.exp(compat - m[s])
            den = jax.ops.segment_sum(ex, s, num_segments=num_nodes)
            return ex / (den[s] + EPS)
        key = jax.random.key(seed)
        ks = jax.random.split(key, 10)
        x = jax.random.normal(ks[0], (N, DIM), dtype=jnp.float32)
        edge_index = jax.random.randint(ks[1], (2, E), 0, N, dtype=jnp.int64)
        edge_attr = jax.random.normal(ks[2], (E, IN_RPE), dtype=jnp.float32)
        Wqkv = jax.random.normal(ks[3], (DIM, 2 * DH + DIM), dtype=jnp.float32) * DIM ** (-0.5)
        bqkv = jnp.zeros((2 * DH + DIM,), dtype=jnp.float32)
        Wk_rpe = jax.random.normal(ks[4], (IN_RPE, DH), dtype=jnp.float32) * IN_RPE ** (-0.5)
        bk_rpe = jnp.zeros((DH,), dtype=jnp.float32)
        Wq_rpe = jax.random.normal(ks[5], (IN_RPE, DH), dtype=jnp.float32) * IN_RPE ** (-0.5)
        bq_rpe = jnp.zeros((DH,), dtype=jnp.float32)
        return {'x': x, 'edge_index': edge_index, 'edge_attr': edge_attr, 'Wqkv': Wqkv, 'bqkv': bqkv, 'Wk_rpe': Wk_rpe, 'bk_rpe': bk_rpe, 'Wq_rpe': Wq_rpe, 'bq_rpe': bq_rpe}
    _L0_gnn_all = _L0_gnn_setup()
    _L0_gnn_in = {k: v for k, v in _L0_gnn_all.items() if k in ('Wqkv', 'bqkv', 'Wk_rpe', 'bk_rpe', 'Wq_rpe', 'bq_rpe')}
    del _L0_gnn_all

    def _L0_ffn_setup():
        import jax, jax.numpy as jnp
        import numpy as np
        E = 8
        K = 2
        D = 256
        H = 512
        DOUT = 256
        EPS = 1e-05
        key = jax.random.key(seed)
        ks = jax.random.split(key, 9)
        s = 0.02
        return {'x': jax.random.normal(ks[0], (4, 256, D), jnp.float32), 'gamma': 1.0 + 0.05 * jax.random.normal(ks[1], (D,), jnp.float32), 'beta': 0.05 * jax.random.normal(ks[2], (D,), jnp.float32), 'Wr': 0.01 * jax.random.normal(ks[3], (D, E), jnp.float32), 'br': jnp.zeros((E,), jnp.float32), 'W1': s * jax.random.normal(ks[4], (E, D, H), jnp.float32), 'b1': s * jax.random.normal(ks[5], (E, H), jnp.float32), 'W2': s * jax.random.normal(ks[6], (E, H, DOUT), jnp.float32), 'b2': s * jax.random.normal(ks[7], (E, DOUT), jnp.float32)}
    _L0_ffn_all = _L0_ffn_setup()
    _L0_ffn_in = {k: v for k, v in _L0_ffn_all.items() if k in ('gamma', 'beta', 'Wr', 'br', 'W1', 'b1', 'W2', 'b2')}
    del _L0_ffn_all
    return {'x': x, 'src': src, 'dst': dst, 'edge_attr_18': edge_attr_18, 'L0_gnn_Wqkv': _L0_gnn_in['Wqkv'], 'L0_gnn_bqkv': _L0_gnn_in['bqkv'], 'L0_gnn_Wk_rpe': _L0_gnn_in['Wk_rpe'], 'L0_gnn_bk_rpe': _L0_gnn_in['bk_rpe'], 'L0_gnn_Wq_rpe': _L0_gnn_in['Wq_rpe'], 'L0_gnn_bq_rpe': _L0_gnn_in['bq_rpe'], 'L0_ffn_gamma': _L0_ffn_in['gamma'], 'L0_ffn_beta': _L0_ffn_in['beta'], 'L0_ffn_Wr': _L0_ffn_in['Wr'], 'L0_ffn_br': _L0_ffn_in['br'], 'L0_ffn_W1': _L0_ffn_in['W1'], 'L0_ffn_b1': _L0_ffn_in['b1'], 'L0_ffn_W2': _L0_ffn_in['W2'], 'L0_ffn_b2': _L0_ffn_in['b2']}

def reference(x, src, dst, edge_attr_18, L0_gnn_Wqkv, L0_gnn_bqkv, L0_gnn_Wk_rpe, L0_gnn_bk_rpe, L0_gnn_Wq_rpe, L0_gnn_bq_rpe, L0_ffn_gamma, L0_ffn_beta, L0_ffn_Wr, L0_ffn_br, L0_ffn_W1, L0_ffn_b1, L0_ffn_W2, L0_ffn_b2):
    import jax
    import jax.numpy as jnp

    def _L0_gnn_ref(x, edge_index, edge_attr, Wqkv, bqkv, Wk_rpe, bk_rpe, Wq_rpe, bq_rpe):
        import jax, jax.numpy as jnp
        import numpy as np
        N, E = (50000, 25000)
        DIM, H, D = (256, 16, 8)
        DH = D * H
        IN_RPE = 18
        SCALE = D ** (-0.5)
        EPS = 1e-16

        def _segment_softmax(compat, s, num_nodes):
            m = jax.ops.segment_max(compat, s, num_segments=num_nodes)
            ex = jnp.exp(compat - m[s])
            den = jax.ops.segment_sum(ex, s, num_segments=num_nodes)
            return ex / (den[s] + EPS)
        n = x.shape[0]
        e = edge_index.shape[1]
        qkv = x @ Wqkv + bqkv
        q = qkv[:, :DH].reshape(n, H, D)
        k = qkv[:, DH:2 * DH].reshape(n, H, D)
        v = qkv[:, 2 * DH:].reshape(n, H, DIM // H)
        s, t = (edge_index[0], edge_index[1])
        qe = q[s] * SCALE
        ke = k[t]
        ke = ke + (edge_attr @ Wk_rpe + bk_rpe).reshape(e, H, D)
        qe = qe + (edge_attr @ Wq_rpe + bq_rpe).reshape(e, H, D)
        compat = jnp.einsum('ehd,ehd->eh', qe, ke)
        attn = _segment_softmax(compat, s, n)
        msg = (v[t] * attn[..., None]).reshape(e, DIM)
        out = jax.ops.segment_sum(msg, s, num_segments=n)
        return out

    def _L0_ffn_ref(x, gamma, beta, Wr, br, W1, b1, W2, b2):
        import jax, jax.numpy as jnp
        import numpy as np
        E = 8
        K = 2
        D = 256
        H = 512
        DOUT = 256
        EPS = 1e-05
        mu = jnp.mean(x, axis=-1, keepdims=True)
        var = jnp.mean(jnp.square(x - mu), axis=-1, keepdims=True)
        xn = (x - mu) * jax.lax.rsqrt(var + EPS) * gamma + beta
        logits = jnp.einsum('bsd,de->bse', xn, Wr) + br
        top_vals, top_idx = jax.lax.top_k(logits, K)
        w = jax.nn.softmax(top_vals, axis=-1)
        w_full = jnp.einsum('bsk,bske->bse', w, jax.nn.one_hot(top_idx, E, dtype=w.dtype))
        y = jnp.zeros(x.shape[:-1] + (DOUT,), x.dtype)
        for e in range(E):
            h = jax.nn.gelu(jnp.einsum('bsd,dh->bsh', xn, W1[e]) + b1[e], approximate=False)
            y_e = jnp.einsum('bsh,hd->bsd', h, W2[e]) + b2[e]
            y = y + y_e * w_full[..., e, None]
        return y
    edge_index = jnp.stack([src, dst])
    x = x + _L0_gnn_ref(_layernorm(x, axis=-1), edge_index, edge_attr_18, L0_gnn_Wqkv, L0_gnn_bqkv, L0_gnn_Wk_rpe, L0_gnn_bk_rpe, L0_gnn_Wq_rpe, L0_gnn_bq_rpe)
    x = x + _L0_ffn_ref(_layernorm(x, axis=-1)[None], L0_ffn_gamma, L0_ffn_beta, L0_ffn_Wr, L0_ffn_br, L0_ffn_W1, L0_ffn_b1, L0_ffn_W2, L0_ffn_b2)[0]
    return x

_drawn_inputs = setup_inputs


def setup_inputs(seed=0):
    import zlib

    import numpy as np

    out = dict(_drawn_inputs(seed))
    spreads = {'L0_gnn_bqkv': (0.0, 0.1),
     'L0_gnn_bk_rpe': (0.0, 0.1),
     'L0_gnn_bq_rpe': (0.0, 0.1),
     'L0_ffn_br': (0.0, 0.1)}
    factors = {'L0_ffn_gamma': 7.739, 'L0_ffn_beta': 6.282, 'L0_ffn_b1': 8.0, 'L0_ffn_b2': 5.444}
    for name, (base, spread) in spreads.items():
        noise = np.random.default_rng([zlib.crc32(name.encode()), seed]).standard_normal(out[name].shape)
        drawn = base * np.exp(spread * noise) if base else spread * noise
        out[name] = jnp.asarray(drawn.astype(out[name].dtype))
    for name, factor in factors.items():
        out[name] = (out[name] * factor).astype(out[name].dtype)
    return out
```

```python
from contextlib import ExitStack

import concourse.bass as bass
from concourse import mybir

P = 128
ALU = mybir.AluOpType
ACT = mybir.ActivationFunctionType
F32 = mybir.dt.float32
BF16 = mybir.dt.bfloat16
I32 = mybir.dt.int32
U32 = mybir.dt.uint32
AX_X = mybir.AxisListType.X

LOW = -1.0e30
LN_EPS = 1e-5
DEN_EPS = 1e-16


def ge(engine, sem, count):
    if isinstance(count, int) and count <= 0:
        return
    engine.wait_ge(sem, count)


def wait_turn(engine, turn, sems, others=()):
    count = engine.snap(turn)
    for sem in sems:
        engine.wait_ge(sem, count)
    for sem, other in others:
        ge(engine, sem, other)
    engine.reg_add(turn, turn, 1)


def gnn_ffn(nc, x, src, dst, edge_attr, Wqkv, bqkv, Wk_rpe, bk_rpe, Wq_rpe, bq_rpe,
            gamma, beta, Wr, br, W1, b1, W2, b2, out):
    N, DIM = x.shape
    E, NA = edge_attr.shape
    DH = Wk_rpe.shape[1]
    D = 8
    H = DH // D
    DV = DIM // H
    SCALE = float(D) ** -0.5
    KV = DH + DIM
    KD = DIM // P
    NX, _, HID = W1.shape
    MH = HID // P

    NB = -(-N // P)
    TAIL = N - (NB - 1) * P
    SHIFT = 7
    EP = 125
    EC = E // EP
    TB = 8
    NBATCH = EC // TB
    assert EP * EC == E and NBATCH * TB == EC and NBATCH % 2 == 0
    G = 4
    GS = G * P
    GSHIFT = GS.bit_length() - 1
    NG = (E + NB * (GS - 1)) // GS
    NG += NG % 2
    NSLOT = NG * GS
    F_T, F_S, F_B, F_EA = 0, 1, 2, 3
    AUG = NA + 1
    RW = F_EA + AUG
    DVA = DV + 1
    AW = H * DVA
    PADG = 61
    assert (NSLOT // P) % PADG == 0
    CB = 4
    NCH = -(-NB // CB)

    kv_dram = nc.dram_tensor("kv_table", (N, KV), F32, kind="Internal").ap()
    rec_dram = nc.dram_tensor("sorted_edges", (NSLOT, RW), F32, kind="Internal").ap()
    rec_groups = rec_dram.rearrange("(g p j) r -> g p (j r)", p=P, j=G)
    rec_fill = rec_dram.rearrange("(f p j) r -> f p (j r)", p=P, j=PADG)

    with ExitStack() as ctx:
        where = [ctx]

        def sb(name, shape, dt=F32):
            return where[0].enter_context(nc.sbuf_tensor(name, shape, dt))

        def sem(name):
            return ctx.enter_context(nc.semaphore(name))

        bank = [ctx.enter_context(nc.psum_tensor(f"bank{n}", [P, 512], F32)) for n in range(8)]

        ident = sb("ident", [P, P])
        identb = sb("identb", [P, P], BF16)
        iota = sb("iota", [P, P])
        blk_i = sb("blk_i", [1, NG], I32)
        xs = sb("xs", [P, NB, DIM])
        q_tab = sb("q_tab", [P, NB * DH])
        acc = sb("acc", [P, NB * AW])
        Wrpe = sb("Wrpe", [AUG, 2 * DH])
        stats = sb("stats", [P, 8])
        mv = sb("mv", [P, NB, 2])
        rstd = sb("rstd", [P, NB])
        std = sb("std", [P, NB])

        sort = ExitStack()
        where[0] = sort
        lower = sb("lower", [P, P])
        upper = sb("upper", [P, P])
        ones = sb("ones", [P, P])
        s_i = sb("s_i", [EP, EC], I32)
        t_i = sb("t_i", [EP, EC], I32)
        s_f = sb("s_f", [EP, EC])
        b_f = sb("b_f", [EP, EC])
        ea_raw = sb("ea_raw", [EP, EC * NA])
        hiA = sb("hiA", [EP, EC, NB], BF16)
        loB = [sb(f"loB{n}", [EP, TB, P], BF16) for n in range(2)]
        loBT = [sb(f"loBT{n}", [P, TB, P]) for n in range(2)]
        cnt = [sb(f"cnt{n}", [P, TB, NB]) for n in range(2)]
        picked = sb("picked", [EP, TB, NB])
        same = sb("same", [EP, TB, EP], BF16)
        within = sb("within", [EP, TB])
        prior = sb("prior", [EP, TB])
        pos = [sb(f"pos{n}", [EP, TB], I32) for n in range(2)]
        recb = [sb(f"recb{n}", [EP, TB, RW]) for n in range(2)]
        padrec = sb("padrec", [P, PADG, RW])
        tot = sb("tot", [P, NB])
        bsum = sb("bsum", [P, NB])
        ngrp_i = sb("ngrp_i", [P, NB], I32)
        ngrp = sb("ngrp", [P, NB])
        incl = sb("incl", [P, NB])
        excl = sb("excl", [P, NB])
        zrow = sb("zrow", [P, NB])
        gid = sb("gid", [1, NG, NB])
        gle = sb("gle", [1, NG, NB])
        gblk = sb("gblk", [1, NG])
        Wqkv_s = sb("Wqkv_s", [P, KD, DH + KV])
        bias = sb("bias", [P, DH + KV])
        xl = [sb(f"xl{n}", [P, DIM]) for n in range(2)]
        xlT = [sb(f"xlT{n}", [P, DIM]) for n in range(2)]
        kvrow = [sb(f"kvrow{n}", [P, KV]) for n in range(2)]
        sort.close()

        where[0] = ctx
        W1s = sb("W1s", [P, KD, NX * HID])
        W2s = sb("W2s", [P, MH, NX * DIM])

        attn = ExitStack()
        where[0] = attn
        rec = [sb(f"rec{n}", [P, G, RW]) for n in range(2)]
        kv = [sb(f"kv{n}", [P, G, KV]) for n in range(2)]
        oh = [sb(f"oh{n}", [P, G, P]) for n in range(2)]
        srep = [sb(f"srep{n}", [P, G, H]) for n in range(2)]
        ohT = [sb(f"ohT{n}", [P, GS]) for n in range(2)]
        eaT = [sb(f"eaT{n}", [AUG, GS]) for n in range(2)]
        sT = [sb(f"sT{n}", [H, GS + 1]) for n in range(2)]
        ke = [sb(f"ke{n}", [P, G, DH]) for n in range(2)]
        prod = sb("prod", [P, G, DH])
        cc = [sb(f"cc{n}", [P, G, H]) for n in range(2)]
        nef = [sb(f"nef{n}", [H, GS]) for n in range(2)]
        pen = [sb(f"pen{n}", [H, GS + 1]) for n in range(2)]
        fw = [sb(f"fw{n}", [H, GS]) for n in range(2)]
        segm = sb("segm", [H, GS])
        dlt = sb("dlt", [H, 1])
        dbuf = sb("dbuf", [H, P])
        dT = [sb(f"dT{n}", [P, H]) for n in range(2)]
        diff = [sb(f"diff{n}", [P, G, H]) for n in range(2)]
        wv = [sb(f"wv{n}", [P, G, H, DVA]) for n in range(2)]
        fac = [sb(f"fac{n}", [P, H]) for n in range(2)]
        attn.close()

        ffn = ExitStack()
        where[0] = ffn
        gam = sb("gam", [P, DIM])
        bet = sb("bet", [P, DIM])
        Wr_s = sb("Wr_s", [P, KD, NX])
        br_s = sb("br_s", [P, NX])
        b1_s = sb("b1_s", [NX * MH, P])
        b1T = sb("b1T", [P, NX * MH])
        b2_s = sb("b2_s", [NX, DIM])
        iden = sb("iden", [P, H])
        hn = sb("hn", [P, CB, DIM])
        xnT = [sb(f"xnT{n}", [P, KD, CB * P]) for n in range(2)]
        lg = sb("lg", [P, CB, NX])
        top = sb("top", [P, CB, 8])
        topi = sb("topi", [P, CB, 8], U32)
        topf = sb("topf", [P, CB, 2])
        e1 = sb("e1", [P, CB])
        w0 = sb("w0", [P, CB])
        w1 = sb("w1", [P, CB])
        hit = sb("hit", [P, CB, 2, NX])
        wf = [sb(f"wf{n}", [P, CB, NX]) for n in range(2)]
        wfT = sb("wfT", [NX, CB * P])
        hT = [sb(f"hT{n}", [P, MH, CB * P]) for n in range(2)]
        ffn.close()

        names = """in_src in_x in_ea in_w in_small consts identb_ready a_ready onehot hist totals tot_sb base_mm chain base_ready blk_ready
            pad_ready pad_done lnchain normed xT_done xT_copied qkv_done table_ready kv_stored0 kv_stored1 kv_stored_tail
            loB_ready loB_used sbc_done loBT_ready cnt_chain cnt_ready lk_done within_ready within_ready pos_chain pos_ready recb_ready
            scat0 scat1
            rec_ready0 rec_ready1 kv_ready0 kv_ready1 oh_ready srep_ready tr_oh tr_ea tr_s oht_copied eat_copied st_copied edge_ready
            qk_done ke_ready prod_done c_ready ct_done ne_ready pen_ready fw_ready sm_ready dlt_ready dbuf_ready smt_done diff_ready dT_ready
            f_done fac_ready w_exp w_ready seg_done acc_scaled acc_done init_ready
            ex_w ex_small b1T_done b1T_ready prep prep_act hn_ready hnT_done xnT_ready logit_done wf_ready wft_done wft_ready b2_done xb2_added
            h_done gelu_done y_done y_added out_done""".split()
        S = {}
        for n in names:
            if n not in S:
                S[n] = sem(n)

        block = ctx.enter_context(nc.Block())

        def batches(engine, body):
            body(0, 0)
            body(1, 1)
            with engine.Fori(2, NBATCH - 2, 2) as i:
                body(i, 0)
                body(i + 1, 1)
            body(NBATCH - 2, 0)
            body(NBATCH - 1, 1)

        def groups(engine, body):
            body(0, 0, 0)
            body(1, 1, 0)
            with engine.Fori(1, NG // 2 - 1) as i:
                body(2 * i, 0, i)
                body(2 * i + 1, 1, i)
            body(NG - 2, 0, NG // 2 - 1)
            body(NG - 1, 1, NG // 2 - 1)

        def after_sort(engine):
            engine.wait_ge(S["scat0"], 8 * TB * NBATCH)
            engine.wait_ge(S["scat1"], 8 * TB * NBATCH)
            engine.wait_ge(S["kv_stored0"], 16 * ((NB - 1) // 2))
            engine.wait_ge(S["kv_stored1"], 16 * ((NB - 1) // 2))
            engine.wait_ge(S["kv_stored_tail"], 16)
            engine.wait_ge(S["pos_ready"], NBATCH)

        @block.sync
        def _(sp):
            sp.dma_start(s_i[:, :], src.rearrange("(p c) -> p c", c=EC)).then_inc(S["in_src"], 16)
            sp.dma_start(t_i[:, :], dst.rearrange("(p c) -> p c", c=EC)).then_inc(S["in_ea"], 16)
            sp.dma_start(xs[:, 0:NB - 1, :], x[0:(NB - 1) * P, :].rearrange("(b p) d -> p b d", p=P)).then_inc(S["in_x"], 16)
            sp.wait_ge(S["init_ready"], 2)
            sp.dma_start(xs[0:TAIL, NB - 1, :], x[(NB - 1) * P:N, :]).then_inc(S["in_x"], 16)
            sp.dma_start(Wqkv_s[:, :, :], Wqkv.rearrange("(k p) n -> p k n", p=P)).then_inc(S["in_w"], 16)
            sp.dma_start(bias[:, :], bqkv.partition_broadcast(P)).then_inc(S["in_w"], 16)
            sp.dma_start(ea_raw[:, :], edge_attr.rearrange("(p c) a -> p (c a)", c=EC)).then_inc(S["in_ea"], 16)
            sp.dma_start(Wrpe[0:NA, 0:DH], Wq_rpe).then_inc(S["in_small"], 16)
            sp.dma_start(Wrpe[0:NA, DH:2 * DH], Wk_rpe).then_inc(S["in_small"], 16)
            sp.dma_start(Wrpe[NA:AUG, 0:DH], bq_rpe.rearrange("(a n) -> a n", a=1)).then_inc(S["in_small"], 16)
            sp.dma_start(Wrpe[NA:AUG, DH:2 * DH], bk_rpe.rearrange("(a n) -> a n", a=1)).then_inc(S["in_small"], 16)
            sp.wait_ge(S["pad_ready"], 4)
            for f in range(NSLOT // P // PADG):
                sp.dma_start(rec_fill[f], padrec[:, :, :].rearrange("p j r -> p (j r)")).then_inc(S["pad_done"], 16)
            with sp.Fori(0, (NB - 1) // 2) as i:
                for k in range(2):
                    sp.wait_ge(S["table_ready"], 2 * i + k + 1)
                    sp.dma_start(kv_dram[bass.ds((2 * i + k) * P, P), :], kvrow[k][:, :]).then_inc(S[f"kv_stored{k}"], 16)
            sp.wait_ge(S["table_ready"], NB)
            sp.dma_start(kv_dram[(NB - 1) * P:N, :], kvrow[0][0:TAIL, :]).then_inc(S["kv_stored_tail"], 16)

            after_sort(sp)
            sp.dma_start(W1s[:, 0, :].rearrange("p (e h) -> p e h", h=HID), W1[:, 0:P, :].rearrange("e p h -> p e h")).then_inc(S["ex_w"], 16)
            sp.dma_start(W1s[:, 1, :].rearrange("p (e h) -> p e h", h=HID), W1[:, P:2 * P, :].rearrange("e p h -> p e h")).then_inc(S["ex_w"], 16)
            for m in range(MH):
                sp.dma_start(W2s[:, m, :].rearrange("p (e d) -> p e d", d=DIM),
                             W2[:, m * P:(m + 1) * P, :].rearrange("e p d -> p e d")).then_inc(S["ex_w"], 16)

            def load_records(g, k, i):
                ge(sp, S["srep_ready"], g - 1)
                ge(sp, S["tr_s"], g - 1)
                ge(sp, S[f"kv_ready{k}"], i * 16 * G)
                source = rec_groups[g] if isinstance(g, int) else rec_groups[bass.ds(g, 1)].rearrange("g p r -> (g p) r")
                sp.dma_start(rec[k][:, :, :].rearrange("p j r -> p (j r)"), source).then_inc(S[f"rec_ready{k}"], 16)

            groups(sp, load_records)

            sp.wait_ge(S["acc_done"], NG)
            sp.dma_start(gam[:, :], gamma.partition_broadcast(P)).then_inc(S["ex_small"], 16)
            sp.dma_start(bet[:, :], beta.partition_broadcast(P)).then_inc(S["ex_small"], 16)
            sp.dma_start(Wr_s[:, :, :], Wr.rearrange("(k p) e -> p k e", p=P)).then_inc(S["ex_small"], 16)
            sp.dma_start(br_s[:, :], br.partition_broadcast(P)).then_inc(S["ex_small"], 16)
            sp.dma_start(b1_s[:, :], b1.rearrange("e (m p) -> (e m) p", p=P)).then_inc(S["ex_small"], 16)
            sp.dma_start(b2_s[:, :], b2).then_inc(S["ex_small"], 16)
            YC = NX * CB
            with sp.Fori(0, NCH - 1) as c:
                sp.wait_ge(S["y_added"], (c + 1) * YC)
                sp.dma_start(out[bass.ds(c * (CB * P), CB * P), :].rearrange("(b p) d -> p b d", p=P),
                             xs[:, bass.ds(c * CB, CB), :]).then_inc(S["out_done"], 16)
            sp.wait_ge(S["y_added"], (NCH - 1) * YC + NX)
            sp.dma_start(out[(NB - 1) * P:N, :], xs[0:TAIL, NB - 1, :]).then_inc(S["out_done"], 16)
            sp.wait_ge(S["out_done"], 16 * NCH)

        @block.gpsimd
        def _(pool):
            batch_turn, group_turn = pool.alloc_register("batch_turn"), pool.alloc_register("group_turn")
            pool.reg_mov(batch_turn, 3)
            pool.reg_mov(group_turn, 1)
            nc.gpsimd.iota(iota[:, :], [[1, P]], base=0, channel_multiplier=0,
                           allow_small_or_imprecise_dtypes=True).then_inc(S["consts"], 1)
            nc.gpsimd.memset(ident[:, :], 0.0).then_inc(S["consts"], 1)
            nc.gpsimd.memset(lower[:, :], 1.0).then_inc(S["consts"], 1)
            nc.gpsimd.memset(upper[:, :], 1.0).then_inc(S["consts"], 1)
            nc.gpsimd.memset(ones[:, :], 1.0).then_inc(S["consts"], 1)
            nc.gpsimd.iota(gid[:, :, :], [[1, NG], [0, NB]], base=0, channel_multiplier=0,
                           allow_small_or_imprecise_dtypes=True).then_inc(S["consts"], 1)
            pool.wait_ge(S["consts"], 6)
            nc.gpsimd.affine_select(out=ident[:, :], in_=ident[:, :], compare_op=ALU.not_equal, fill=1.0, base=0,
                                    pattern=[[-1, P]], channel_multiplier=1).then_inc(S["consts"], 1)
            nc.gpsimd.affine_select(out=lower[:, :], in_=lower[:, :], compare_op=ALU.is_gt, fill=0.0, base=0,
                                    pattern=[[-1, P]], channel_multiplier=1).then_inc(S["consts"], 1)
            nc.gpsimd.affine_select(out=upper[:, :], in_=upper[:, :], compare_op=ALU.is_gt, fill=0.0, base=0,
                                    pattern=[[1, P]], channel_multiplier=-1).then_inc(S["consts"], 1)
            nc.gpsimd.memset(padrec[:, :, :], 0.0).then_inc(S["pad_ready"], 1)
            pool.wait_ge(S["pad_ready"], 1)
            nc.gpsimd.memset(padrec[:, :, F_S:F_B + 1], -1.0).then_inc(S["pad_ready"], 3)

            pool.wait_ge(S["pad_done"], 16 * (NSLOT // P // PADG))

            def scatter(i, k):
                if isinstance(i, int):
                    pool.wait_ge(S["pos_ready"], i + 1)
                    pool.wait_ge(S["recb_ready"], i + 1)
                else:
                    wait_turn(pool, batch_turn, [S["pos_ready"], S["recb_ready"]])
                for j in range(TB):
                    nc.gpsimd.indirect_dma_start(
                        rec_dram, bass.IndirectOffsetOnAxis(pos[k][:, j:j + 1], 0),
                        recb[k][:, j, :], None).then_inc(S[f"scat{k}"], 16)

            batches(pool, scatter)

            after_sort(pool)

            def gather(g, k, i):
                if isinstance(g, int):
                    pool.wait_ge(S[f"rec_ready{k}"], 16 * i + 16)
                    ge(pool, S["qk_done"], g - 1)
                    ge(pool, S["w_ready"], g - 1)
                else:
                    wait_turn(pool, group_turn, [S["qk_done"], S["w_ready"]], [(S[f"rec_ready{k}"], 16 * i + 16)])
                for j in range(G):
                    nc.gpsimd.indirect_dma_start(
                        kv[k][:, j, :], None, kv_dram,
                        bass.IndirectOffsetOnAxis(rec[k][:, j, F_T:F_T + 1].bitcast(I32), 0)).then_inc(S[f"kv_ready{k}"], 16)

            groups(pool, gather)

        @block.vector
        def _(dve):
            V = nc.vector
            prep_turn = dve.alloc_register("prep_turn")
            dve.reg_mov(prep_turn, 1)
            V.memset(acc[:, :], 0.0).then_inc(S["init_ready"], 1)
            V.memset(xs[:, NB - 1, :], 0.0).then_inc(S["init_ready"], 1)
            V.memset(zrow[:, :], 0.0).then_inc(S["init_ready"], 1)

            dve.wait_ge(S["in_src"], 16)
            V.tensor_copy(s_f[:, :], s_i[:, :]).then_inc(S["chain"], 1)
            V.tensor_scalar(pos[0][:, :], s_i[:, 0:TB], 0, None, ALU.logical_shift_right).then_inc(S["chain"], 1)
            dve.wait_ge(S["chain"], 2)
            V.tensor_scalar(loBT[0][0:EP, 0:4, 0:100].bitcast(I32), s_i[:, :].rearrange("p (a b) -> p a b", a=4), P - 1, None,
                            ALU.bitwise_and).then_inc(S["chain"], 1)
            V.tensor_scalar(loBT[1][0:EP, 0:4, 0:100].bitcast(I32), s_i[:, :].rearrange("p (a b) -> p a b", a=4), SHIFT, None,
                            ALU.logical_shift_right).then_inc(S["chain"], 1)
            dve.wait_ge(S["chain"], 4)
            V.tensor_copy(b_f[:, :].rearrange("p (a b) -> p a b", a=4), loBT[0][0:EP, 0:4, 0:100].bitcast(I32)).then_inc(S["chain"], 1)
            dve.wait_ge(S["consts"], 9)
            V.tensor_copy(identb[:, :], ident[:, :]).then_inc(S["identb_ready"], 1)
            a_cols = loBT[0][0:EP, 4:8, 0:100]
            V.tensor_copy(a_cols, loBT[1][0:EP, 0:4, 0:100].bitcast(I32)).then_inc(S["chain"], 1)
            dve.wait_ge(S["chain"], 6)
            for a in range(4):
                w = EC // 4
                V.tensor_tensor(hiA[:, a * w:(a + 1) * w, :], iota[0:EP, None, 0:NB].to_broadcast([EP, w, NB]),
                                loBT[0][0:EP, 4 + a, 0:100, None].to_broadcast([EP, w, NB]), ALU.is_equal).then_inc(S["a_ready"], 1)

            def onehot(i, k):
                first = i * TB
                cols = b_f[:, first:first + TB] if isinstance(i, int) else b_f[:, bass.ds(first, TB)]
                return V.tensor_tensor(loB[k][:, :, :], iota[0:EP, None, :].to_broadcast([EP, TB, P]),
                                       cols.unsqueeze(2).to_broadcast([EP, TB, P]), ALU.is_equal)

            def pass1(i, k):
                ge(dve, S["hist"], i - 1)
                onehot(i, k).then_inc(S["onehot"], 1)

            batches(dve, pass1)

            dve.wait_ge(S["hist"], NBATCH)
            V.tensor_copy(tot[:, :], bank[7][:, 0:NB]).then_inc(S["tot_sb"], 1)
            dve.wait_ge(S["base_mm"], 1)
            V.tensor_scalar(bsum[:, :], bank[7][:, 64:64 + NB], float(GS - 1), None, ALU.add).then_inc(S["chain"], 1)
            dve.wait_ge(S["chain"], 7)
            V.tensor_copy(ngrp_i[:, :], bsum[:, :]).then_inc(S["chain"], 1)
            dve.wait_ge(S["chain"], 8)
            V.tensor_scalar(ngrp_i[:, :], ngrp_i[:, :], GSHIFT, None, ALU.logical_shift_right).then_inc(S["chain"], 1)
            dve.wait_ge(S["chain"], 9)
            V.tensor_copy(ngrp[:, :], ngrp_i[:, :]).then_inc(S["chain"], 1)
            dve.wait_ge(S["chain"], 10)
            V.tensor_tensor_scan(incl[:, :], ngrp[:, :], zrow[:, :], 0.0, ALU.add, ALU.add).then_inc(S["chain"], 1)
            dve.wait_ge(S["chain"], 11)
            V.tensor_tensor(excl[:, :], incl[:, :], ngrp[:, :], ALU.subtract).then_inc(S["chain"], 1)
            dve.wait_ge(S["chain"], 12)
            V.scalar_tensor_tensor(cnt[0][:, 0, :], excl[:, :], float(GS), bank[7][:, 128:128 + NB], ALU.mult, ALU.add)\
                .then_inc(S["base_ready"], 1)
            V.tensor_tensor(gle[:, :, :], incl[0:1, None, :].to_broadcast([1, NG, NB]), gid[:, :, :], ALU.is_le).then_inc(S["chain"], 1)
            dve.wait_ge(S["chain"], 13)
            V.tensor_reduce(gblk[:, :], gle[:, :, :], AX_X, ALU.add).then_inc(S["chain"], 1)
            dve.wait_ge(S["chain"], 14)
            V.tensor_scalar(blk_i[:, :], gblk[:, :], float(NB - 1), None, ALU.min).then_inc(S["blk_ready"], 1)

            dve.wait_ge(S["in_x"], 32)
            for t in range(NB):
                V.bn_stats(stats[:, 0:6], xs[:, t, :]).then_inc(S["lnchain"], 1)
                dve.wait_ge(S["lnchain"], 2 * t + 1)
                V.bn_aggr(mv[:, t, :], stats[:, 0:6]).then_inc(S["lnchain"], 1)
                dve.wait_ge(S["lnchain"], 2 * t + 2)
            V.tensor_scalar(std[:, :], mv[:, :, 1], LN_EPS, None, ALU.add).then_inc(S["lnchain"], 1)
            dve.wait_ge(S["lnchain"], 2 * NB + 2)
            V.reciprocal(rstd[:, :], std[:, :]).then_inc(S["lnchain"], 1)
            dve.wait_ge(S["lnchain"], 2 * NB + 3)
            dve.wait_ge(S["in_w"], 32)
            V.tensor_scalar(bias[:, 0:DH], bias[:, 0:DH], SCALE, None, ALU.mult).then_inc(S["lnchain"], 1)
            dve.wait_ge(S["lnchain"], 2 * NB + 4)

            def normalize(t, k):
                ge(dve, S["xT_done"], t - 1)
                V.tensor_scalar(xl[k][:, :], xs[:, bass.ds(t, 1), :].rearrange("p a d -> p (a d)"),
                                mv[:, bass.ds(t, 1), 0], rstd[:, bass.ds(t, 1)],
                                ALU.subtract, ALU.mult).then_inc(S["normed"], 1)

            def table(t, k, i):
                dve.wait_ge(S["qkv_done"], t + 1)
                V.scalar_tensor_tensor(q_tab[:, bass.ds(t * DH, DH)], bank[2 + k][:, 0:DH], SCALE, bias[:, 0:DH],
                                       ALU.mult, ALU.add)
                ge(dve, S[f"kv_stored{k}"], 16 * i)
                V.tensor_tensor(kvrow[k][:, :], bank[2 + k][:, DH:DH + KV], bias[:, DH:DH + KV], ALU.add)\
                    .then_inc(S["table_ready"], 1)

            normalize(0, 0)
            normalize(1, 1)
            table(0, 0, 0)
            normalize(2, 0)
            table(1, 1, 0)
            with dve.Fori(1, (NB - 1) // 2) as i:
                normalize(2 * i + 1, 1)
                table(2 * i, 0, i)
                normalize(2 * i + 2, 0)
                table(2 * i + 1, 1, i)
            table(NB - 1, 0, (NB - 1) // 2)

            def lo_onehot(i, k):
                ge(dve, S["loB_used"], i - 1)
                onehot(i, k).then_inc(S["loB_ready"], 1)

            def counts(i, k):
                dve.wait_ge(S["loB_used"], i + 1)
                ge(dve, S["lk_done"], i)
                for j in range(TB):
                    nxt = cnt[k][:, j + 1, :] if j + 1 < TB else cnt[1 - k][:, 0, :]
                    V.tensor_tensor(nxt, cnt[k][:, j, :], bank[k][:, j * NB:(j + 1) * NB], ALU.add).then_inc(S["cnt_ready"], 1)
                    dve.wait_ge(S["cnt_ready"], i * TB + (j + 1))

            def slots(i, k):
                dve.wait_ge(S["sbc_done"], i + 1)
                for j in range(TB):
                    col = s_f[:, i * TB + j:i * TB + j + 1] if isinstance(i, int) else s_f[:, bass.ds(i * TB + j, 1)]
                    V.scalar_tensor_tensor(same[:, j, :], bank[4 + j // 4][0:EP, (j % 4) * P:(j % 4) * P + EP], col,
                                           lower[0:EP, 0:EP], ALU.is_equal, ALU.mult,
                                           accum_out=within[:, j:j + 1]).then_inc(S["within_ready"], 1)
                dve.wait_ge(S["lk_done"], i + 1)
                V.tensor_tensor(picked[:, :, :], bank[6][0:EP, 0:TB * NB].rearrange("p (j a) -> p j a", a=NB),
                                hiA[:, bass.ds(i * TB, TB), :], ALU.mult).then_inc(S["pos_chain"], 1)
                dve.wait_ge(S["pos_chain"], 2 * i + 1)
                V.tensor_reduce(prior[:, :], picked[:, :, :], AX_X, ALU.add).then_inc(S["pos_chain"], 1)
                dve.wait_ge(S["pos_chain"], 2 * i + 2)
                dve.wait_ge(S["within_ready"], TB * (i + 1))
                ge(dve, S[f"scat{k}"], (i - k) * (8 * TB))
                V.tensor_tensor(pos[k][:, :], prior[:, :], within[:, :], ALU.add).then_inc(S["pos_ready"], 1)

            lo_onehot(0, 0)
            lo_onehot(1, 1)
            counts(0, 0)
            slots(0, 0)
            lo_onehot(2, 0)
            counts(1, 1)
            slots(1, 1)
            with dve.Fori(1, NBATCH // 2 - 1) as i:
                lo_onehot(2 * i + 1, 1)
                counts(2 * i, 0)
                slots(2 * i, 0)
                lo_onehot(2 * i + 2, 0)
                counts(2 * i + 1, 1)
                slots(2 * i + 1, 1)
            lo_onehot(NBATCH - 1, 1)
            counts(NBATCH - 2, 0)
            slots(NBATCH - 2, 0)
            counts(NBATCH - 1, 1)
            slots(NBATCH - 1, 1)

            after_sort(dve)
            V.memset(pen[0][:, GS:GS + 1], 0.0)
            V.memset(pen[1][:, GS:GS + 1], 0.0)
            V.memset(dbuf[:, :], 0.0).then_inc(S["init_ready"], 1)
            dve.wait_ge(S["init_ready"], 4)

            def onehots(g, k, i):
                dve.wait_ge(S[f"rec_ready{k}"], 16 * i + 16)
                ge(dve, S["seg_done"], g - 1)
                V.tensor_tensor(oh[k][:, :, :], iota[:, None, :].to_broadcast([P, G, P]),
                                rec[k][:, :, F_B:F_B + 1].to_broadcast([P, G, P]), ALU.is_equal).then_inc(S["oh_ready"], 1)
                V.tensor_copy(srep[k][:, :, :], rec[k][:, :, F_S:F_S + 1].to_broadcast([P, G, H])).then_inc(S["srep_ready"], 1)

            def scores(g, k):
                dve.wait_ge(S["ke_ready"], g + 1)
                for a in range(2):
                    V.tensor_tensor(prod[:, 2 * a:2 * a + 2, :],
                                    bank[3 + a][:, :].rearrange("p (j c) -> p j c", c=2 * DH)[:, :, 0:DH],
                                    ke[k][:, 2 * a:2 * a + 2, :], ALU.mult).then_inc(S["prod_done"], 1)
                dve.wait_ge(S["prod_done"], 2 * g + 2)
                V.tensor_reduce(cc[k][:, :, :].rearrange("p j h -> p (j h)"),
                                prod[:, :, :].rearrange("p j (h d) -> p (j h) d", d=D), AX_X, ALU.add).then_inc(S["c_ready"], 1)

            def bounds(g, k):
                dve.wait_ge(S["edge_ready"], g + 1)
                ge(dve, S["pen_ready"], g - 1)
                V.tensor_tensor(nef[k][:, :], sT[k][:, 1:GS + 1], sT[k][:, 0:GS], ALU.not_equal).then_inc(S["ne_ready"], 1)

            def maxima(g, k):
                dve.wait_ge(S["pen_ready"], g + 1)
                dve.wait_ge(S["ct_done"], g + 1)
                first = isinstance(g, int) and g == 0
                V.tensor_tensor_scan(fw[k][:, :], pen[k][:, 0:GS], bank[5][0:H, :],
                                     LOW if first else fw[1 - k][:, GS - 1:GS], ALU.add, ALU.max).then_inc(S["fw_ready"], 1)
                dve.wait_ge(S["fw_ready"], g + 1)
                ge(dve, S["smt_done"], g)
                V.tensor_tensor_scan(segm[:, GS - 1::-1], pen[k][:, GS:0:-1], fw[k][:, GS - 1::-1],
                                     LOW, ALU.add, ALU.max).then_inc(S["sm_ready"], 1)
                dve.wait_ge(S["sm_ready"], g + 1)
                if not first:
                    V.tensor_tensor(dlt[:, :], fw[1 - k][:, GS - 1:GS], segm[:, 0:1], ALU.subtract).then_inc(S["dlt_ready"], 1)
                    dve.wait_ge(S["dlt_ready"], g)
                    V.scalar_tensor_tensor(dbuf[:, 0:1], nef[k][:, 0:1], 0.0, dlt[:, :], ALU.is_equal, ALU.mult)\
                        .then_inc(S["dbuf_ready"], 1)

            def shifts(g, k):
                dve.wait_ge(S["smt_done"], g + 1)
                ge(dve, S["w_exp"], g - 1)
                V.tensor_tensor(diff[k][:, :, :].rearrange("p j h -> p (j h)"), cc[k][:, :, :].rearrange("p j h -> p (j h)"),
                                bank[6][:, 0:G * H], ALU.subtract).then_inc(S["diff_ready"], 1)
                ge(dve, S["f_done"], g - 1)
                V.tensor_copy(dT[k][:, :], bank[6][:, G * H:G * H + H]).then_inc(S["dT_ready"], 1)

            def weighted(g, k):
                dve.wait_ge(S["w_exp"], g + 1)
                ge(dve, S["seg_done"], g - 1)
                V.tensor_tensor(wv[k][:, :, :, 0:DV],
                                kv[k][:, :, DH:KV].rearrange("p j (h d) -> p j h d", d=DV),
                                wv[k][:, :, :, DV:DVA].to_broadcast([P, G, H, DV]), ALU.mult).then_inc(S["w_ready"], 1)

            def gather_up(g, k):
                here = dve.value_load(blk_i[0:1, bass.ds(g, 1)], min_val=0, max_val=NB - 1)
                mine = acc[:, bass.ds(here * AW, AW)]
                dve.wait_ge(S["fac_ready"], g + 1)
                ge(dve, S["acc_done"], g)
                V.tensor_tensor(mine.rearrange("p (h d) -> p h d", d=DVA), mine.rearrange("p (h d) -> p h d", d=DVA),
                                fac[k][:, :, None].to_broadcast([P, H, DVA]), ALU.mult).then_inc(S["acc_scaled"], 1)
                dve.wait_ge(S["acc_scaled"], g + 1)
                dve.wait_ge(S["seg_done"], g + 1)
                V.tensor_tensor(mine, mine, bank[7][:, 0:AW], ALU.add).then_inc(S["acc_done"], 1)

            onehots(0, 0, 0)
            scores(0, 0)
            bounds(0, 0)

            def step(g, k, i_next, last=False):
                if not last:
                    onehots(g + 1, 1 - k, i_next)
                maxima(g, k)
                shifts(g, k)
                if not last:
                    scores(g + 1, 1 - k)
                    bounds(g + 1, 1 - k)
                weighted(g, k)
                gather_up(g, k)

            step(0, 0, 0)
            step(1, 1, 1)
            with dve.Fori(1, NG // 2 - 1) as i:
                step(2 * i, 0, i)
                step(2 * i + 1, 1, i + 1)
            step(NG - 2, 0, NG // 2 - 1)
            step(NG - 1, 1, 0, last=True)

            dve.wait_ge(S["ex_small"], 96)
            dve.wait_ge(S["acc_done"], NG)
            dve.wait_ge(S["b1T_done"], 1)
            V.tensor_copy(b1T[:, :], bank[7][:, 0:NX * MH]).then_inc(S["b1T_ready"], 1)
            steps = 14 * CB + 11

            def prepare(c, nb, kx):
                n = [0]

                def did(ins):
                    n[0] += 1
                    ins.then_inc(S["prep"], 1)
                    wait_turn(dve, prep_turn, [S["prep"]])

                for q in range(nb):
                    b = c * CB + q
                    mine = acc[:, bass.ds(b * AW, AW)].rearrange("p (h d) -> p h d", d=DVA)
                    xb = xs[:, bass.ds(b, 1), :].rearrange("p a d -> p (a d)")
                    did(V.tensor_scalar(iden[:, :], mine[:, :, DV], DEN_EPS, None, ALU.add))
                    did(V.reciprocal(iden[:, :], iden[:, :]))
                    did(V.tensor_tensor(mine[:, :, 0:DV], mine[:, :, 0:DV], iden[:, :, None].to_broadcast([P, H, DV]), ALU.mult))
                    did(V.tensor_tensor(xb.rearrange("p (h d) -> p h d", d=DV), xb.rearrange("p (h d) -> p h d", d=DV),
                                        mine[:, :, 0:DV], ALU.add))
                    did(V.bn_stats(stats[:, 0:6], xb))
                    did(V.bn_aggr(mv[:, q, :], stats[:, 0:6]))
                did(V.tensor_scalar(std[:, 0:nb], mv[:, 0:nb, 1], LN_EPS, None, ALU.add))
                dve.wait_ge(S["prep_act"], 3 * c + 1)
                did(V.reciprocal(rstd[:, 0:nb], std[:, 0:nb]))
                ge(dve, S["hnT_done"], c)
                for q in range(nb):
                    xb = xs[:, bass.ds(c * CB + q, 1), :].rearrange("p a d -> p (a d)")
                    did(V.tensor_scalar(hn[:, q, :], xb, mv[:, q, 0:1], rstd[:, q:q + 1], ALU.subtract, ALU.mult))
                    did(V.bn_stats(stats[:, 0:6], hn[:, q, :]))
                    did(V.bn_aggr(mv[:, q, :], stats[:, 0:6]))
                did(V.tensor_scalar(std[:, 0:nb], mv[:, 0:nb, 1], LN_EPS, None, ALU.add))
                dve.wait_ge(S["prep_act"], 3 * c + 2)
                did(V.reciprocal(rstd[:, 0:nb], std[:, 0:nb]))
                for q in range(nb):
                    did(V.tensor_scalar(hn[:, q, :], hn[:, q, :], mv[:, q, 0:1], rstd[:, q:q + 1], ALU.subtract, ALU.mult))
                did(V.tensor_tensor(hn[:, 0:nb, :], hn[:, 0:nb, :], gam[:, None, :].to_broadcast([P, nb, DIM]), ALU.mult))
                V.tensor_tensor(hn[:, 0:nb, :], hn[:, 0:nb, :], bet[:, None, :].to_broadcast([P, nb, DIM]), ALU.add)\
                    .then_inc(S["hn_ready"], 1)
                dve.wait_ge(S["logit_done"], c + 1)
                did(V.tensor_tensor(lg[:, 0:nb, :], bank[5][:, 0:nb * NX].rearrange("p (q e) -> p q e", e=NX),
                                    br_s[:, None, :].to_broadcast([P, nb, NX]), ALU.add))
                for q in range(nb):
                    did(V.max(top[:, q, :], lg[:, q, :]))
                    did(V.max_index(topi[:, q, :], top[:, q, :], lg[:, q, :]))
                did(V.tensor_copy(topf[:, 0:nb, :], topi[:, 0:nb, 0:2]))
                did(V.tensor_tensor(e1[:, 0:nb], top[:, 0:nb, 1], top[:, 0:nb, 0], ALU.subtract))
                dve.wait_ge(S["prep_act"], 3 * c + 3)
                did(V.tensor_scalar(w0[:, 0:nb], e1[:, 0:nb], 1.0, None, ALU.add))
                did(V.reciprocal(w0[:, 0:nb], w0[:, 0:nb]))
                did(V.tensor_tensor(w1[:, 0:nb], w0[:, 0:nb], e1[:, 0:nb], ALU.mult))
                for q in range(nb):
                    did(V.tensor_scalar(hit[:, q, 0, :], iota[:, 0:NX], topf[:, q, 0:1], w0[:, q:q + 1], ALU.is_equal, ALU.mult))
                    did(V.tensor_scalar(hit[:, q, 1, :], iota[:, 0:NX], topf[:, q, 1:2], w1[:, q:q + 1], ALU.is_equal, ALU.mult))
                V.tensor_tensor(wf[kx][:, 0:nb, :], hit[:, 0:nb, 0, :], hit[:, 0:nb, 1, :], ALU.add).then_inc(S["wf_ready"], 1)
                assert nb < CB or n[0] == per_chunk(CB), (n[0], per_chunk(CB))

            def per_chunk(nb):
                return 14 * nb + 11

            def combine(c, nb, kx):
                for q in range(nb):
                    xb = xs[:, bass.ds(c * CB + q, 1), :].rearrange("p a d -> p (a d)")
                    dve.wait_ge(S["b2_done"], c * CB + q + 1)
                    V.tensor_tensor(xb, xb, bank[6 + q % 2][:, 0:DIM], ALU.add).then_inc(S["xb2_added"], 1)
                dve.wait_ge(S["xb2_added"], c * CB + nb)
                for e in range(NX):
                    for q in range(nb):
                        at = c * (NX * CB) + e * nb + q
                        xb = xs[:, bass.ds(c * CB + q, 1), :].rearrange("p a d -> p (a d)")
                        dve.wait_ge(S["y_done"], at + 1)
                        if e:
                            dve.wait_ge(S["y_added"], at - nb + 1)
                        V.scalar_tensor_tensor(xb, bank[6 + q % 2][:, 0:DIM], wf[kx][:, q, e:e + 1], xb,
                                               ALU.mult, ALU.add).then_inc(S["y_added"], 1)

            prepare(0, CB, 0)
            combine(0, CB, 0)
            with dve.Fori(1, NCH - 1) as c:
                prepare(c, CB, 0)
                combine(c, CB, 0)
            prepare(NCH - 1, NB - (NCH - 1) * CB, 0)
            combine(NCH - 1, NB - (NCH - 1) * CB, 0)

        @block.scalar
        def _(act):
            A = nc.scalar
            act.wait_ge(S["lnchain"], 2 * NB + 1)
            A.activation(std[:, :], std[:, :], ACT.Sqrt).then_inc(S["lnchain"], 1)

            def copy_xT(t, k):
                act.wait_ge(S["xT_done"], t + 1)
                ge(act, S["qkv_done"], t - 1)
                A.activation(xlT[k][:, :], bank[k][:, 0:DIM], ACT.Copy).then_inc(S["xT_copied"], 1)

            copy_xT(0, 0)
            copy_xT(1, 1)
            with act.Fori(1, (NB - 1) // 2) as i:
                copy_xT(2 * i, 0)
                copy_xT(2 * i + 1, 1)
            copy_xT(NB - 1, 0)

            act.wait_ge(S["in_ea"], 32)

            def batch(i, k):
                ge(act, S[f"scat{k}"], (i - k) * (8 * TB))
                ge(act, S["sbc_done"], i - 1)
                A.activation(recb[k][:, :, F_T:F_T + 1].rearrange("p j r -> p (j r)").bitcast(I32), t_i[:, bass.ds(i * TB, TB)], ACT.Copy)
                A.activation(recb[k][:, :, F_S:F_S + 1].rearrange("p j r -> p (j r)"), s_f[:, bass.ds(i * TB, TB)], ACT.Copy)
                A.activation(recb[k][:, :, F_B:F_B + 1].rearrange("p j r -> p (j r)"), b_f[:, bass.ds(i * TB, TB)], ACT.Copy)
                A.activation(recb[k][:, :, RW - 1:RW].rearrange("p j r -> p (j r)"), b_f[:, bass.ds(i * TB, TB)], ACT.Copy,
                             bias=1.0, scale=0.0)
                A.activation(recb[k][:, :, F_EA:F_EA + NA],
                             ea_raw[:, bass.ds(i * (TB * NA), TB * NA)].rearrange("p (j a) -> p j a", a=NA),
                             ACT.Copy).then_inc(S["recb_ready"], 1)
                act.wait_ge(S["loB_used"], i + 1)
                ge(act, S["lk_done"], i - 1)
                A.activation(loBT[k][:, :, 0:EP], bank[2 + k][:, :].bitcast(BF16).rearrange("p (j e) -> p j e", e=P)[:, :, 0:EP],
                             ACT.Copy).then_inc(S["loBT_ready"], 1)

            batches(act, batch)

            def turned(g, k):
                act.wait_ge(S["tr_oh"], g + 1)
                ge(act, S["qk_done"], g - 1)
                A.activation(ohT[k][:, :], bank[0][:, :], ACT.Copy).then_inc(S["oht_copied"], 1)
                act.wait_ge(S["tr_ea"], g + 1)
                A.activation(eaT[k][:, :], bank[1][0:AUG, :], ACT.Copy).then_inc(S["eat_copied"], 1)
                act.wait_ge(S["tr_s"], g + 1)
                ge(act, S["ne_ready"], g - 1)
                A.activation(sT[k][:, 1:GS + 1], bank[2][0:H, :], ACT.Copy).then_inc(S["st_copied"], 1)
                if isinstance(g, int) and g == 0:
                    A.activation(sT[k][:, 0:1], bank[2][0:H, 0:1], ACT.Copy, bias=-5.0, scale=0.0).then_inc(S["edge_ready"], 1)
                else:
                    act.wait_ge(S["st_copied"], g)
                    A.activation(sT[k][:, 0:1], sT[1 - k][:, GS:GS + 1], ACT.Copy).then_inc(S["edge_ready"], 1)

            def keys(g, k):
                act.wait_ge(S["qk_done"], g + 1)
                for a in range(2):
                    ins = A.activation(ke[k][:, 2 * a:2 * a + 2, :],
                                       bank[3 + a][:, :].rearrange("p (j c) -> p j c", c=2 * DH)[:, :, DH:2 * DH], ACT.Copy)
                ins.then_inc(S["ke_ready"], 1)

            def penalty(g, k):
                act.wait_ge(S["ne_ready"], g + 1)
                A.activation(pen[k][:, 0:GS], nef[k][:, :], ACT.Copy, scale=LOW).then_inc(S["pen_ready"], 1)

            def exps(g, k):
                act.wait_ge(S["diff_ready"], g + 1)
                ge(act, S["seg_done"], g - 1)
                A.activation(wv[k][:, :, :, DV], diff[k][:, :, :], ACT.Exp).then_inc(S["w_exp"], 1)
                act.wait_ge(S["f_done"], g + 1)
                ge(act, S["acc_done"], g - 1)
                A.activation(fac[k][:, :], bank[5][:, 0:H], ACT.Exp).then_inc(S["fac_ready"], 1)

            act.wait_ge(S["init_ready"], 4)
            turned(0, 0)
            keys(0, 0)
            penalty(0, 0)

            def step(g, k, last=False):
                if not last:
                    turned(g + 1, 1 - k)
                    keys(g + 1, 1 - k)
                exps(g, k)
                if not last:
                    penalty(g + 1, 1 - k)

            step(0, 0)
            step(1, 1)
            with act.Fori(1, NG // 2 - 1) as i:
                step(2 * i, 0)
                step(2 * i + 1, 1)
            step(NG - 2, 0)
            step(NG - 1, 1, last=True)

            act.wait_ge(S["b1T_ready"], 1)
            steps = 14 * CB + 11

            def chunk(c, nb):
                W = nb * P
                base = c * steps
                act.wait_ge(S["prep"], base + 6 * nb + 1)
                A.activation(std[:, 0:nb], std[:, 0:nb], ACT.Sqrt).then_inc(S["prep_act"], 1)
                act.wait_ge(S["prep"], base + 9 * nb + 3)
                A.activation(std[:, 0:nb], std[:, 0:nb], ACT.Sqrt).then_inc(S["prep_act"], 1)
                for k in range(KD):
                    act.wait_ge(S["hnT_done"], c + 1)
                    A.activation(xnT[0][:, k, 0:W], bank[k][:, 0:W], ACT.Copy).then_inc(S["xnT_ready"], 1)
                act.wait_ge(S["prep"], base + 12 * nb + 8)
                A.activation(e1[:, 0:nb], e1[:, 0:nb], ACT.Exp).then_inc(S["prep_act"], 1)
                act.wait_ge(S["wft_done"], c + 1)
                A.activation(wfT[:, 0:W], bank[4][0:NX, 0:W], ACT.Copy).then_inc(S["wft_ready"], 1)
                for e in range(NX):
                    for m in range(MH):
                        at = c * (NX * MH) + e * MH + m
                        act.wait_ge(S["h_done"], at + 1)
                        if e >= 2:
                            act.wait_ge(S["y_done"], c * (NX * CB) + (e - 1) * nb)
                        A.activation(hT[e % 2][:, m, 0:W], bank[m % 4][:, 0:W], ACT.Gelu,
                                     bias=b1T[:, e * MH + m:e * MH + m + 1]).then_inc(S["gelu_done"], 1)

            chunk(0, CB)
            with act.Fori(1, NCH - 1) as c:
                chunk(c, CB)
            chunk(NCH - 1, NB - (NCH - 1) * CB)

        @block.tensor
        def _(pe):
            T = nc.tensor
            maxima_turn = pe.alloc_register("maxima_turn")
            pe.reg_mov(maxima_turn, 3)
            pe.wait_ge(S["a_ready"], 4)

            def histogram(i, k):
                pe.wait_ge(S["onehot"], i + 1)
                for j in range(TB):
                    mm = T.matmul(bank[7][:, 0:NB], loB[k][:, j, :],
                                  hiA[:, bass.ds(i * TB + j, 1), :].rearrange("p a n -> p (a n)"),
                                  start=(isinstance(i, int) and i == 0 and j == 0),
                                  stop=(isinstance(i, int) and i == NBATCH - 1 and j == TB - 1), skip_group_check=True)
                mm.then_inc(S["hist"], 1)

            batches(pe, histogram)
            pe.wait_ge(S["consts"], 9)
            pe.wait_ge(S["tot_sb"], 1)
            T.matmul(bank[7][:, 64:64 + NB], ones[:, :], tot[:, :], start=True, stop=True, skip_group_check=True)
            T.matmul(bank[7][:, 128:128 + NB], upper[:, :], tot[:, :], start=True, stop=True,
                     skip_group_check=True).then_inc(S["base_mm"], 1)

            pe.wait_ge(S["in_w"], 32)

            def turn_x(t, k):
                pe.wait_ge(S["normed"], t + 1)
                ge(pe, S["xT_copied"], t - 1)
                for a in range(KD):
                    mm = T.transpose(bank[k][:, a * P:(a + 1) * P], xl[k][:, a * P:(a + 1) * P], ident[:, :])
                mm.then_inc(S["xT_done"], 1)

            def project(t, k):
                pe.wait_ge(S["xT_copied"], t + 1)
                ge(pe, S["table_ready"], t - 1)
                for a in range(KD):
                    mm = T.matmul(bank[2 + k][:, :], xlT[k][:, a * P:(a + 1) * P], Wqkv_s[:, a, :],
                                  start=(a == 0), stop=(a == KD - 1))
                mm.then_inc(S["qkv_done"], 1)

            turn_x(0, 0)
            turn_x(1, 1)
            project(0, 0)
            turn_x(2, 0)
            project(1, 1)
            with pe.Fori(1, (NB - 1) // 2) as i:
                turn_x(2 * i + 1, 1)
                project(2 * i, 0)
                turn_x(2 * i + 2, 0)
                project(2 * i + 1, 1)
            project(NB - 1, 0)

            pe.wait_ge(S["identb_ready"], 1)
            pe.wait_ge(S["base_ready"], 1)
            pe.wait_ge(S["table_ready"], NB)

            def tile_counts(i, k):
                pe.wait_ge(S["loB_ready"], i + 1)
                ge(pe, S["cnt_ready"], (i - 1) * TB)
                ge(pe, S["loBT_ready"], i - 1)
                for j in range(TB):
                    T.matmul(bank[k][:, j * NB:(j + 1) * NB], loB[k][:, j, :],
                             hiA[:, bass.ds(i * TB + j, 1), :].rearrange("p a n -> p (a n)"),
                             start=True, stop=True, skip_group_check=True)
                for j in range(TB):
                    mm = T.transpose(bank[2 + k][:, :].bitcast(BF16)[:, j * P:j * P + EP], loB[k][:, j, :], identb[0:EP, 0:EP])
                mm.then_inc(S["loB_used"], 1)

            def spread_sources(i, k):
                ge(pe, S["within_ready"], i * TB)
                pe.wait_ge(S["recb_ready"], i + 1)
                for j in range(TB):
                    mm = T.matmul(bank[4 + j // 4][0:EP, (j % 4) * P:(j % 4) * P + EP],
                                  recb[k][:, j, F_S:F_S + 1].to_broadcast([EP, EP]), ident[0:EP, 0:EP],
                                  start=True, stop=True, skip_group_check=True)
                mm.then_inc(S["sbc_done"], 1)

            def look_up(i, k):
                pe.wait_ge(S["loBT_ready"], i + 1)
                pe.wait_ge(S["cnt_ready"], (i + 1) * TB)
                ge(pe, S["pos_chain"], 2 * i)
                for j in range(TB):
                    mm = T.matmul(bank[6][0:EP, j * NB:(j + 1) * NB], loBT[k][:, j, 0:EP], cnt[k][:, j, :],
                                  start=True, stop=True, skip_group_check=True)
                mm.then_inc(S["lk_done"], 1)

            tile_counts(0, 0)
            spread_sources(0, 0)
            tile_counts(1, 1)
            look_up(0, 0)
            spread_sources(1, 1)
            tile_counts(2, 0)
            look_up(1, 1)
            spread_sources(2, 0)
            with pe.Fori(1, NBATCH // 2 - 1) as i:
                tile_counts(2 * i + 1, 1)
                look_up(2 * i, 0)
                spread_sources(2 * i + 1, 1)
                tile_counts(2 * i + 2, 0)
                look_up(2 * i + 1, 1)
                spread_sources(2 * i + 2, 0)
            tile_counts(NBATCH - 1, 1)
            look_up(NBATCH - 2, 0)
            spread_sources(NBATCH - 1, 1)
            look_up(NBATCH - 1, 1)

            after_sort(pe)
            pe.wait_ge(S["in_small"], 64)
            pe.wait_ge(S["blk_ready"], 1)

            def turn_edges(g, k, i):
                pe.wait_ge(S["oh_ready"], g + 1)
                ge(pe, S["oht_copied"], g)
                for j in range(G):
                    mm = T.transpose(bank[0][:, j * P:(j + 1) * P], oh[k][:, j, :], ident[:, :])
                mm.then_inc(S["tr_oh"], 1)
                pe.wait_ge(S[f"rec_ready{k}"], 16 * i + 16)
                ge(pe, S["eat_copied"], g)
                for j in range(G):
                    mm = T.transpose(bank[1][0:AUG, j * P:(j + 1) * P], rec[k][:, j, F_EA:F_EA + AUG], ident[:, :])
                mm.then_inc(S["tr_ea"], 1)
                pe.wait_ge(S["srep_ready"], g + 1)
                ge(pe, S["edge_ready"], g)
                for j in range(G):
                    mm = T.transpose(bank[2][0:H, j::G], srep[k][:, j, :], ident[:, :])
                mm.then_inc(S["tr_s"], 1)

            def queries_keys(g, k, i):
                here = pe.value_load(blk_i[0:1, bass.ds(g, 1)], min_val=0, max_val=NB - 1)
                pe.wait_ge(S["oht_copied"], g + 1)
                pe.wait_ge(S["eat_copied"], g + 1)
                pe.wait_ge(S[f"kv_ready{k}"], (16 * G) * i + 16 * G)
                ge(pe, S["prod_done"], 2 * g)
                for j in range(G):
                    o = bank[3 + j // 2][:, (j % 2) * 2 * DH:(j % 2 + 1) * 2 * DH]
                    T.matmul(o, eaT[k][:, j * P:(j + 1) * P], Wrpe[:, :], start=True, stop=False, skip_group_check=True)
                    T.matmul(o[:, 0:DH], ohT[k][:, j * P:(j + 1) * P], q_tab[:, bass.ds(here * DH, DH)], start=False, stop=False,
                             skip_group_check=True)
                    mm = T.matmul(o[:, DH:2 * DH], ident[:, :], kv[k][:, j, 0:DH], start=False, stop=True, skip_group_check=True)
                mm.then_inc(S["qk_done"], 1)

            def turn_scores(g, k):
                pe.wait_ge(S["c_ready"], g + 1)
                ge(pe, S["fac_ready"], g)
                for j in range(G):
                    mm = T.transpose(bank[5][0:H, j::G], cc[k][:, j, :], ident[:, :])
                mm.then_inc(S["ct_done"], 1)

            def turn_maxima(g, k):
                if isinstance(g, int):
                    pe.wait_ge(S["sm_ready"], g + 1)
                    ge(pe, S["dbuf_ready"], g)
                    ge(pe, S["dT_ready"], g)
                else:
                    wait_turn(pe, maxima_turn, [S["sm_ready"]], [(S["dbuf_ready"], g), (S["dT_ready"], g)])
                for j in range(G):
                    T.transpose(bank[6][:, j * H:(j + 1) * H], segm[:, j::G], ident[0:H, 0:H])
                T.transpose(bank[6][:, G * H:(G + 1) * H], dbuf[:, :], ident[0:H, 0:H]).then_inc(S["smt_done"], 1)
                pe.wait_ge(S["dT_ready"], g + 1)
                T.matmul(bank[5][:, 0:H], oh[k][:, 0, :], dT[k][:, :], start=True, stop=True,
                         skip_group_check=True).then_inc(S["f_done"], 1)

            def segment_sums(g, k):
                pe.wait_ge(S["w_ready"], g + 1)
                ge(pe, S["acc_done"], g)
                for j in range(G):
                    mm = T.matmul(bank[7][:, 0:AW], oh[k][:, j, :], wv[k][:, j, :, :].rearrange("p h d -> p (h d)"),
                                  start=(j == 0), stop=(j == G - 1))
                mm.then_inc(S["seg_done"], 1)

            turn_edges(0, 0, 0)
            queries_keys(0, 0, 0)

            def step(g, k, i_next, last=False):
                turn_scores(g, k)
                if not last:
                    turn_edges(g + 1, 1 - k, i_next)
                    queries_keys(g + 1, 1 - k, i_next)
                turn_maxima(g, k)
                segment_sums(g, k)

            step(0, 0, 0)
            step(1, 1, 1)
            with pe.Fori(1, NG // 2 - 1) as i:
                step(2 * i, 0, i)
                step(2 * i + 1, 1, i + 1)
            step(NG - 2, 0, NG // 2 - 1)
            step(NG - 1, 1, 0, last=True)

            pe.wait_ge(S["ex_small"], 96)
            pe.wait_ge(S["ex_w"], 16 * (KD + MH))
            pe.wait_ge(S["acc_done"], NG)
            T.transpose(bank[7][:, 0:NX * MH], b1_s[:, :], ident[0:NX * MH, 0:NX * MH]).then_inc(S["b1T_done"], 1)

            def chunk(c, nb):
                W = nb * P
                pe.wait_ge(S["hn_ready"], c + 1)
                ge(pe, S["gelu_done"], c * (NX * MH))
                for k in range(KD):
                    for q in range(nb):
                        mm = T.transpose(bank[k][:, q * P:(q + 1) * P], hn[:, q, k * P:(k + 1) * P], ident[:, :])
                mm.then_inc(S["hnT_done"], 1)
                pe.wait_ge(S["xnT_ready"], (c + 1) * KD)
                for q in range(nb):
                    for k in range(KD):
                        mm = T.matmul(bank[5][:, q * NX:(q + 1) * NX], xnT[0][:, k, q * P:(q + 1) * P], Wr_s[:, k, :],
                                      start=(k == 0), stop=(k == KD - 1), skip_group_check=True)
                mm.then_inc(S["logit_done"], 1)
                pe.wait_ge(S["wf_ready"], c + 1)
                ge(pe, S["wft_ready"], c)
                for q in range(nb):
                    mm = T.transpose(bank[4][0:NX, q * P:(q + 1) * P], wf[0][:, q, :], ident[:, :])
                mm.then_inc(S["wft_done"], 1)

                def hidden(e):
                    for m in range(MH):
                        at = c * (NX * MH) + e * MH + m
                        if not (isinstance(c, int) and c == 0 and e == 0 and m < 4):
                            if e > 0:
                                pe.wait_ge(S["gelu_done"], at - 3)
                        for k in range(KD):
                            mm = T.matmul(bank[m % 4][:, 0:W], W1s[:, k, e * HID + m * P:e * HID + (m + 1) * P], xnT[0][:, k, 0:W],
                                          start=(k == 0), stop=(k == KD - 1))
                        mm.then_inc(S["h_done"], 1)

                def output(e):
                    pe.wait_ge(S["gelu_done"], c * (NX * MH) + (e + 1) * MH)
                    for q in range(nb):
                        at = c * (NX * CB) + e * nb + q
                        if e or q >= 2:
                            pe.wait_ge(S["y_added"], at - 1 if nb > 1 else at)
                        for m in range(MH):
                            mm = T.matmul(bank[6 + q % 2][:, 0:DIM], hT[e % 2][:, m, q * P:(q + 1) * P],
                                          W2s[:, m, e * DIM:(e + 1) * DIM], start=(m == 0), stop=(m == MH - 1))
                        mm.then_inc(S["y_done"], 1)

                hidden(0)
                pe.wait_ge(S["wft_ready"], c + 1)
                ge(pe, S["y_added"], c * (NX * CB))
                for q in range(nb):
                    if q >= 2:
                        pe.wait_ge(S["xb2_added"], c * CB + q - 1)
                    T.matmul(bank[6 + q % 2][:, 0:DIM], wfT[:, q * P:(q + 1) * P], b2_s[:, :], start=True, stop=True)\
                        .then_inc(S["b2_done"], 1)
                pe.wait_ge(S["xb2_added"], c * CB + nb)
                for e in range(NX):
                    if e + 1 < NX:
                        hidden(e + 1)
                    output(e)

            chunk(0, CB)
            with pe.Fori(1, NCH - 1) as c:
                chunk(c, CB)
            chunk(NCH - 1, NB - (NCH - 1) * CB)


INPUTS = ['x', 'src', 'dst', 'edge_attr_18', 'L0_gnn_Wqkv', 'L0_gnn_bqkv', 'L0_gnn_Wk_rpe', 'L0_gnn_bk_rpe',
          'L0_gnn_Wq_rpe', 'L0_gnn_bq_rpe', 'L0_ffn_gamma', 'L0_ffn_beta', 'L0_ffn_Wr', 'L0_ffn_br', 'L0_ffn_W1',
          'L0_ffn_b1', 'L0_ffn_W2', 'L0_ffn_b2']


def kernel(**inputs):
    import numpy as _np
    import concourse.bacc as _bacc
    from concourse import mybir as _mybir
    from concourse.bass_utils import run_bass_kernel_spmd as _run

    nc = _bacc.Bacc("TRN2", target_bir_lowering=False, num_devices=1)
    arrays, args = {}, []
    for name in INPUTS:
        a = _np.ascontiguousarray(inputs[name])
        arrays[f"in_{name}"] = a
        args.append(nc.dram_tensor(f"in_{name}", a.shape, _mybir.dt.from_np(a.dtype), kind="ExternalInput").ap())
    shape = tuple(inputs['x'].shape)
    args.append(nc.dram_tensor("out_x", shape, _mybir.dt.from_np(_np.dtype("float32")), kind="ExternalOutput").ap())
    gnn_ffn(nc, *args)
    r = _run(nc, [arrays], core_ids=[0])
    return r.results[0]["out_x"]
```

```python
from contextlib import ExitStack

import concourse.bass as bass
from concourse import mybir

P = 128
ALU = mybir.AluOpType
ACT = mybir.ActivationFunctionType
F32 = mybir.dt.float32
BF16 = mybir.dt.bfloat16
I32 = mybir.dt.int32
U32 = mybir.dt.uint32
AX_X = mybir.AxisListType.X

LOW = -1.0e30
LN_EPS = 1e-5
DEN_EPS = 1e-16


def ge(engine, sem, count):
    if isinstance(count, int) and count <= 0:
        return
    engine.wait_ge(sem, count)


def wait_turn(engine, turn, sems, others=()):
    count = engine.snap(turn)
    for sem in sems:
        engine.wait_ge(sem, count)
    for sem, other in others:
        ge(engine, sem, other)
    engine.reg_add(turn, turn, 1)


def gnn_ffn(nc, x, src, dst, edge_attr, Wqkv, bqkv, Wk_rpe, bk_rpe, Wq_rpe, bq_rpe,
            gamma, beta, Wr, br, W1, b1, W2, b2, out):
    N, DIM = x.shape
    E, NA = edge_attr.shape
    DH = Wk_rpe.shape[1]
    D = 8
    H = DH // D
    DV = DIM // H
    SCALE = float(D) ** -0.5
    PARTS = 3
    KW = PARTS * DH // 2
    KV = KW + DIM
    KD = DIM // P
    NX, _, HID = W1.shape
    MH = HID // P

    NB = -(-N // P)
    TAIL = N - (NB - 1) * P
    SHIFT = 7
    EP = 125
    EC = E // EP
    TB = 8
    NBATCH = EC // TB
    assert EP * EC == E and NBATCH * TB == EC and NBATCH % 2 == 0
    G = 4
    GS = G * P
    GSHIFT = GS.bit_length() - 1
    NG = (E + NB * (GS - 1)) // GS
    RING = 4
    NG = -(-NG // RING) * RING
    NSLOT = NG * GS
    F_T, F_S, F_B, F_EA = 0, 1, 2, 3
    AUG = NA + 1
    STK = 6 * AUG
    RW = F_EA + STK // 2
    LEAD = G
    DVA = DV + 1
    AW = H * DVA
    PADG = 31
    assert (NSLOT // P) % PADG == 0 and STK % 2 == 0 and STK <= P
    CB = 4
    NCH = -(-NB // CB)

    kv_dram = nc.dram_tensor("kv_table", (N, KV), F32, kind="Internal").ap()
    rec_dram = nc.dram_tensor("sorted_edges", (NSLOT + LEAD, RW), F32, kind="Internal").ap()
    rec_groups = rec_dram[LEAD:LEAD + NSLOT, :].rearrange("(g p j) r -> g p (j r)", p=P, j=G)
    rec_before = rec_dram[0:NSLOT, :].rearrange("(g p j) r -> g p (j r)", p=P, j=G)
    B_S = (G - 1) * RW + F_S
    rec_fill = rec_dram[0:NSLOT, :].rearrange("(f p j) r -> f p (j r)", p=P, j=PADG)

    with ExitStack() as ctx:
        where = [ctx]

        def sb(name, shape, dt=F32):
            return where[0].enter_context(nc.sbuf_tensor(name, shape, dt))

        def sem(name):
            return ctx.enter_context(nc.semaphore(name))

        bank = [ctx.enter_context(nc.psum_tensor(f"bank{n}", [P, 512], F32)) for n in range(8)]

        ident = sb("ident", [P, P])
        identb = sb("identb", [P, P], BF16)
        iota = sb("iota", [P, P])
        iotab = sb("iotab", [P, P], BF16)
        blk_i = sb("blk_i", [1, NG], I32)
        xs = sb("xs", [P, NB, DIM])
        q_tab = sb("q_tab", [P, NB, PARTS, DH], BF16)
        acc = sb("acc", [P, NB * AW])
        Wrpe = sb("Wrpe", [STK, 2 * DH], BF16)
        stats = sb("stats", [P, 8])
        mv = sb("mv", [P, NB, 2])
        rstd = sb("rstd", [P, NB])
        std = sb("std", [P, NB])

        sort = ExitStack()
        where[0] = sort
        lower = sb("lower", [P, P])
        upper = sb("upper", [P, P])
        ones = sb("ones", [P, P])
        s_i = sb("s_i", [EP, EC], I32)
        t_i = sb("t_i", [EP, EC], I32)
        s_f = sb("s_f", [EP, EC])
        b_f = sb("b_f", [EP, EC])
        ea_raw = sb("ea_raw", [EP, EC * NA])
        hiA = sb("hiA", [EP, EC, NB], BF16)
        loB = [sb(f"loB{n}", [EP, TB, P], BF16) for n in range(2)]
        loBT = [sb(f"loBT{n}", [P, TB, P]) for n in range(2)]
        cnt = [sb(f"cnt{n}", [P, TB, NB]) for n in range(2)]
        picked = sb("picked", [EP, TB, NB])
        same = sb("same", [EP, TB, EP], BF16)
        within = sb("within", [EP, TB])
        prior = sb("prior", [EP, TB])
        pos = [sb(f"pos{n}", [EP, TB], I32) for n in range(2)]
        recb = [sb(f"recb{n}", [EP, TB, RW]) for n in range(2)]
        padrec = sb("padrec", [P, PADG, RW])
        tot = sb("tot", [P, NB])
        bsum = sb("bsum", [P, NB])
        ngrp_i = sb("ngrp_i", [P, NB], I32)
        ngrp = sb("ngrp", [P, NB])
        incl = sb("incl", [P, NB])
        excl = sb("excl", [P, NB])
        zrow = sb("zrow", [P, NB])
        gid = sb("gid", [1, NG])
        gle = sb("gle", [1, NG, NB], BF16)
        gblk = sb("gblk", [1, NG])
        Wqkv_s = sb("Wqkv_s", [P, KD, 2 * DH + DIM])
        bias = sb("bias", [P, 2 * DH + DIM])
        wraw = sb("wraw", [STK, 2 * DH])
        wpart = [sb(f"wpart{n}", [STK, 2 * DH], BF16) for n in range(PARTS)]
        wres = sb("wres", [STK, 2 * DH])
        wmask = sb("wmask", [STK, 4])
        wsum = [sb(f"wsum{n}", [STK, 2 * DH]) for n in range(2)]
        eres = [sb(f"eres{n}", [EP, TB, NA]) for n in range(2)]
        qk32 = sb("qk32", [P, 2 * DH])
        qkres = sb("qkres", [P, 2 * DH])
        qkp = [sb(f"qkp{n}", [P, PARTS, 2 * DH], BF16) for n in range(2)]
        xl = [sb(f"xl{n}", [P, DIM]) for n in range(2)]
        xlT = [sb(f"xlT{n}", [P, DIM]) for n in range(2)]
        kvrow = [sb(f"kvrow{n}", [P, DIM]) for n in range(2)]
        sort.close()

        where[0] = ctx
        W1s = sb("W1s", [P, KD, NX * HID])

        attn = ExitStack()
        where[0] = attn
        rec = [sb(f"rec{n}", [P, G, RW]) for n in range(RING)]
        before = [sb(f"before{n}", [P, 1]) for n in range(RING)]
        kv = [sb(f"kv{n}", [P, G, KV]) for n in range(RING)]
        oh = [sb(f"oh{n}", [P, G, P], BF16) for n in range(2)]
        oh32 = [sb(f"ohw{n}", [P, G, P]) for n in range(RING)]
        new = [sb(f"new{n}", [P, G]) for n in range(2)]
        newr = [sb(f"newr{n}", [P, G, H]) for n in range(2)]
        ohT = [sb(f"ohT{n}", [P, GS], BF16) for n in range(2)]
        eaT = [sb(f"eaT{n}", [STK, GS], BF16) for n in range(2)]
        pen = [sb(f"pen{n}", [H, GS + 1]) for n in range(RING)]
        ke = sb("ke", [P, G, DH])
        prod = sb("prod", [P, G, DH])
        cc = [sb(f"cc{n}", [P, G, H]) for n in range(2)]
        fw = [sb(f"fw{n}", [H, GS]) for n in range(2)]
        segm = sb("segm", [H, GS])
        dlt = sb("dlt", [H, 1])
        dbuf = sb("dbuf", [H, P])
        dT = [sb(f"dT{n}", [P, H]) for n in range(RING)]
        diff = [sb(f"diff{n}", [P, G, H]) for n in range(RING)]
        wv = [sb(f"wv{n}", [P, G, H, DVA]) for n in range(2)]
        fac = [sb(f"fac{n}", [P, H]) for n in range(RING)]
        attn.close()

        ffn = ExitStack()
        where[0] = ffn
        W2s = sb("W2s", [P, MH, NX * DIM])
        gam = sb("gam", [P, DIM])
        bet = sb("bet", [P, DIM])
        Wr_s = sb("Wr_s", [P, KD, NX])
        br_s = sb("br_s", [P, NX])
        b1_s = sb("b1_s", [NX * MH, P])
        b1T = sb("b1T", [P, NX * MH])
        b2_s = sb("b2_s", [NX, DIM])
        iden = sb("iden", [P, H])
        hn = sb("hn", [P, CB, DIM])
        xnT = [sb(f"xnT{n}", [P, KD, CB * P]) for n in range(2)]
        lg = sb("lg", [P, CB, NX])
        top = sb("top", [P, CB, 8])
        topi = sb("topi", [P, CB, 8], U32)
        topf = sb("topf", [P, CB, 2])
        e1 = sb("e1", [P, CB])
        w0 = sb("w0", [P, CB])
        w1 = sb("w1", [P, CB])
        hit = sb("hit", [P, CB, 2, NX])
        wf = [sb(f"wf{n}", [P, CB, NX]) for n in range(2)]
        wfT = sb("wfT", [NX, CB * P])
        hT = [sb(f"hT{n}", [P, MH, CB * P]) for n in range(2)]
        ffn.close()

        names = """in_src in_x in_ea in_w in_small consts identb_ready a_ready onehot hist totals tot_sb base_mm chain base_ready blk_ready
            pad_ready pad_done lnchain normed xT_done xT_copied qkv_done table_ready kv_stored0 kv_stored1 kv_stored_tail
            loB_ready loB_used sbc_done loBT_ready cnt_chain cnt_ready lk_done within_ready within_ready pos_chain pos_ready recb_ready
            scat0 scat1
            rec_ready0 rec_ready1 rec_ready2 rec_ready3 kv_ready0 kv_ready1 kv_ready2 kv_ready3 oh_ready new_ready newr_ready tr_oh tr_ea tr_s oh32_ready oht_copied eat_copied pen_ready
            wstk recb_const e1_ready e2_ready eres_ready e3_ready lead_done qk_chain qkp1 qkp2 qkp3 qtab_ready
            qk_done ke_ready prod_done c_ready ct_done fw_ready sm_ready dlt_ready dbuf_ready smt_done diff_ready dT_ready
            f_done fac_ready w_exp w_ready seg_done acc_scaled acc_done init_ready
            ex_w ex_small b1T_done b1T_ready prep prep_act hn_ready hnT_done xnT_ready logit_done wf_ready wft_done wft_ready b2_done xb2_added
            h_done gelu_done y_done y_added out_done""".split()
        S = {}
        for n in names:
            if n not in S:
                S[n] = sem(n)

        block = ctx.enter_context(nc.Block())

        def batches(engine, body):
            body(0, 0)
            body(1, 1)
            with engine.Fori(2, NBATCH - 2, 2) as i:
                body(i, 0)
                body(i + 1, 1)
            body(NBATCH - 2, 0)
            body(NBATCH - 1, 1)

        def groups(engine, body):
            for k in range(RING):
                body(k, k, 0)
            with engine.Fori(1, NG // RING - 1) as i:
                for k in range(RING):
                    body(RING * i + k, k, i)
            for k in range(RING):
                body(NG - RING + k, k, NG // RING - 1)

        def after_sort(engine):
            engine.wait_ge(S["scat0"], 8 * TB * NBATCH)
            engine.wait_ge(S["scat1"], 8 * TB * NBATCH)
            engine.wait_ge(S["kv_stored0"], 32 * ((NB - 1) // 2))
            engine.wait_ge(S["kv_stored1"], 32 * ((NB - 1) // 2))
            engine.wait_ge(S["kv_stored_tail"], 32)
            engine.wait_ge(S["pos_ready"], NBATCH)

        @block.sync
        def _(sp):
            sp.dma_start(s_i[:, :], src.rearrange("(p c) -> p c", c=EC)).then_inc(S["in_src"], 16)
            sp.dma_start(t_i[:, :], dst.rearrange("(p c) -> p c", c=EC)).then_inc(S["in_ea"], 16)
            sp.dma_start(xs[:, 0:NB - 1, :], x[0:(NB - 1) * P, :].rearrange("(b p) d -> p b d", p=P)).then_inc(S["in_x"], 16)
            sp.wait_ge(S["init_ready"], 2)
            sp.dma_start(xs[0:TAIL, NB - 1, :], x[(NB - 1) * P:N, :]).then_inc(S["in_x"], 16)
            sp.dma_start(Wqkv_s[:, :, :], Wqkv.rearrange("(k p) n -> p k n", p=P)).then_inc(S["in_w"], 16)
            sp.dma_start(bias[:, :], bqkv.partition_broadcast(P)).then_inc(S["in_w"], 16)
            sp.dma_start(ea_raw[:, :], edge_attr.rearrange("(p c) a -> p (c a)", c=EC)).then_inc(S["in_ea"], 16)
            for n in range(STK // AUG):
                r = n * AUG
                sp.dma_start(wraw[r:r + NA, 0:DH], Wq_rpe).then_inc(S["in_small"], 16)
                sp.dma_start(wraw[r:r + NA, DH:2 * DH], Wk_rpe).then_inc(S["in_small"], 16)
                sp.dma_start(wraw[r + NA:r + AUG, 0:DH], bq_rpe.rearrange("(a n) -> a n", a=1)).then_inc(S["in_small"], 16)
                sp.dma_start(wraw[r + NA:r + AUG, DH:2 * DH], bk_rpe.rearrange("(a n) -> a n", a=1)).then_inc(S["in_small"], 16)
            sp.wait_ge(S["pad_ready"], 4)
            for f in range(NSLOT // P // PADG):
                sp.dma_start(rec_fill[f], padrec[:, :, :].rearrange("p j r -> p (j r)")).then_inc(S["pad_done"], 16)
            sp.dma_start(rec_dram[NSLOT:NSLOT + LEAD, :], padrec[0:LEAD, 0, :]).then_inc(S["pad_done"], 16)
            with sp.Fori(0, (NB - 1) // 2) as i:
                for k in range(2):
                    sp.wait_ge(S["qkp3"], 2 * i + k + 1)
                    sp.dma_start(kv_dram[bass.ds((2 * i + k) * P, P), KW:KV], kvrow[k][:, :]).then_inc(S[f"kv_stored{k}"], 16)
                    sp.dma_start(kv_dram[bass.ds((2 * i + k) * P, P), 0:KW].bitcast(BF16).rearrange("n (a c) -> n a c", c=DH),
                                 qkp[k][:, :, DH:2 * DH]).then_inc(S[f"kv_stored{k}"], 16)
            sp.wait_ge(S["qkp3"], NB)
            sp.dma_start(kv_dram[(NB - 1) * P:N, KW:KV], kvrow[0][0:TAIL, :]).then_inc(S["kv_stored_tail"], 16)
            sp.dma_start(kv_dram[(NB - 1) * P:N, 0:KW].bitcast(BF16).rearrange("n (a c) -> n a c", c=DH),
                         qkp[0][0:TAIL, :, DH:2 * DH]).then_inc(S["kv_stored_tail"], 16)

            after_sort(sp)
            sp.dma_start(W1s[:, 0, :].rearrange("p (e h) -> p e h", h=HID), W1[:, 0:P, :].rearrange("e p h -> p e h")).then_inc(S["ex_w"], 16)
            sp.dma_start(W1s[:, 1, :].rearrange("p (e h) -> p e h", h=HID), W1[:, P:2 * P, :].rearrange("e p h -> p e h")).then_inc(S["ex_w"], 16)

            def load_records(g, k, i):
                ge(sp, S["new_ready"], g - RING + 1)
                ge(sp, S["oh_ready"], g - RING + 1)
                ge(sp, S["tr_ea"], g - RING + 1)
                ge(sp, S[f"kv_ready{k}"], i * 16 * G)
                for tile, source, a, b in ((rec[k][:, :, :].rearrange("p j r -> p (j r)"), rec_groups, 0, G * RW),
                                           (before[k][:, :], rec_before, B_S, B_S + 1)):
                    one = source[g][:, a:b] if isinstance(g, int) else source[bass.ds(g, 1)].rearrange("g p r -> (g p) r")[:, a:b]
                    sp.dma_start(tile, one, allow_slow_non_contiguous=True).then_inc(S[f"rec_ready{k}"], 16)

            groups(sp, load_records)

            sp.wait_ge(S["acc_done"], NG)
            sp.dma_start(gam[:, :], gamma.partition_broadcast(P)).then_inc(S["ex_small"], 16)
            sp.dma_start(bet[:, :], beta.partition_broadcast(P)).then_inc(S["ex_small"], 16)
            sp.dma_start(Wr_s[:, :, :], Wr.rearrange("(k p) e -> p k e", p=P)).then_inc(S["ex_small"], 16)
            sp.dma_start(br_s[:, :], br.partition_broadcast(P)).then_inc(S["ex_small"], 16)
            sp.dma_start(b1_s[:, :], b1.rearrange("e (m p) -> (e m) p", p=P)).then_inc(S["ex_small"], 16)
            sp.dma_start(b2_s[:, :], b2).then_inc(S["ex_small"], 16)
            for m in range(MH):
                sp.dma_start(W2s[:, m, :].rearrange("p (e d) -> p e d", d=DIM),
                             W2[:, m * P:(m + 1) * P, :].rearrange("e p d -> p e d")).then_inc(S["ex_w"], 16)
            YC = NX * CB
            with sp.Fori(0, NCH - 1) as c:
                sp.wait_ge(S["y_added"], (c + 1) * YC)
                sp.dma_start(out[bass.ds(c * (CB * P), CB * P), :].rearrange("(b p) d -> p b d", p=P),
                             xs[:, bass.ds(c * CB, CB), :]).then_inc(S["out_done"], 16)
            sp.wait_ge(S["y_added"], (NCH - 1) * YC + NX)
            sp.dma_start(out[(NB - 1) * P:N, :], xs[0:TAIL, NB - 1, :]).then_inc(S["out_done"], 16)
            sp.wait_ge(S["out_done"], 16 * NCH)

        @block.gpsimd
        def _(pool):
            batch_turn, group_turn = pool.alloc_register("batch_turn"), pool.alloc_register("group_turn")
            pool.reg_mov(batch_turn, 3)
            pool.reg_mov(group_turn, 1)
            nc.gpsimd.iota(iota[:, :], [[1, P]], base=0, channel_multiplier=0,
                           allow_small_or_imprecise_dtypes=True).then_inc(S["consts"], 1)
            nc.gpsimd.memset(ident[:, :], 0.0).then_inc(S["consts"], 1)
            nc.gpsimd.memset(lower[:, :], 1.0).then_inc(S["consts"], 1)
            nc.gpsimd.memset(upper[:, :], 1.0).then_inc(S["consts"], 1)
            nc.gpsimd.memset(ones[:, :], 1.0).then_inc(S["consts"], 1)
            nc.gpsimd.iota(gid[:, :], [[1, NG]], base=0, channel_multiplier=0,
                           allow_small_or_imprecise_dtypes=True).then_inc(S["consts"], 1)
            pool.wait_ge(S["consts"], 6)
            nc.gpsimd.affine_select(out=ident[:, :], in_=ident[:, :], compare_op=ALU.not_equal, fill=1.0, base=0,
                                    pattern=[[-1, P]], channel_multiplier=1).then_inc(S["consts"], 1)
            nc.gpsimd.affine_select(out=lower[:, :], in_=lower[:, :], compare_op=ALU.is_gt, fill=0.0, base=0,
                                    pattern=[[-1, P]], channel_multiplier=1).then_inc(S["consts"], 1)
            nc.gpsimd.affine_select(out=upper[:, :], in_=upper[:, :], compare_op=ALU.is_gt, fill=0.0, base=0,
                                    pattern=[[1, P]], channel_multiplier=-1).then_inc(S["consts"], 1)
            nc.gpsimd.memset(padrec[:, :, :], 0.0).then_inc(S["pad_ready"], 1)
            pool.wait_ge(S["pad_ready"], 1)
            nc.gpsimd.memset(padrec[:, :, F_S:F_B + 1], -1.0).then_inc(S["pad_ready"], 3)

            nc.gpsimd.memset(recb[0][:, :, :], 0.0).then_inc(S["recb_const"], 1)
            nc.gpsimd.memset(recb[1][:, :, :], 0.0).then_inc(S["recb_const"], 1)
            nc.gpsimd.memset(wmask[:, :], 1.0).then_inc(S["recb_const"], 1)
            pool.wait_ge(S["recb_const"], 3)
            for n in range(2):
                parts = recb[n][:, :, F_EA:RW].bitcast(BF16).rearrange("p j (b a) -> p j b a", a=AUG)
                nc.gpsimd.memset(parts[:, :, 0:4:3, NA:AUG], 1.0).then_inc(S["recb_const"], 1)
                nc.gpsimd.memset(parts[:, :, 5:6, NA:AUG], 1.0).then_inc(S["recb_const"], 1)
            for n, first in enumerate((3 * AUG, 5 * AUG)):
                nc.gpsimd.affine_select(out=wmask[:, n:n + 1], in_=wmask[:, n:n + 1], compare_op=ALU.is_ge, fill=0.0,
                                        base=-first, pattern=[[0, 1]], channel_multiplier=1).then_inc(S["recb_const"], 1)

            pool.wait_ge(S["pad_done"], 16 * (NSLOT // P // PADG + 1))

            def scatter(i, k):
                if isinstance(i, int):
                    pool.wait_ge(S["pos_ready"], i + 1)
                    pool.wait_ge(S["recb_ready"], i + 1)
                    pool.wait_ge(S["e3_ready"], i + 1)
                else:
                    wait_turn(pool, batch_turn, [S["pos_ready"], S["recb_ready"], S["e3_ready"]])
                for j in range(TB):
                    nc.gpsimd.indirect_dma_start(
                        rec_dram, bass.IndirectOffsetOnAxis(pos[k][:, j:j + 1], 0),
                        recb[k][:, j, :], None).then_inc(S[f"scat{k}"], 16)

            batches(pool, scatter)

            after_sort(pool)

            def gather(g, k, i):
                if isinstance(g, int):
                    pool.wait_ge(S[f"rec_ready{k}"], 32 * i + 32)
                    ge(pool, S["qk_done"], g - RING + 1)
                    ge(pool, S["w_ready"], g - RING + 1)
                else:
                    wait_turn(pool, group_turn, [S["qk_done"], S["w_ready"]], [(S[f"rec_ready{k}"], 32 * i + 32)])
                for j in range(G):
                    nc.gpsimd.indirect_dma_start(
                        kv[k][:, j, :], None, kv_dram,
                        bass.IndirectOffsetOnAxis(rec[k][:, j, F_T:F_T + 1].bitcast(I32), 0)).then_inc(S[f"kv_ready{k}"], 16)

            groups(pool, gather)

        @block.vector
        def _(dve):
            V = nc.vector
            prep_turn = dve.alloc_register("prep_turn")
            dve.reg_mov(prep_turn, 1)
            V.memset(acc[:, :], 0.0).then_inc(S["init_ready"], 1)
            V.memset(xs[:, NB - 1, :], 0.0).then_inc(S["init_ready"], 1)
            V.memset(zrow[:, :], 0.0).then_inc(S["init_ready"], 1)

            dve.wait_ge(S["in_src"], 16)
            V.tensor_copy(s_f[:, :], s_i[:, :]).then_inc(S["chain"], 1)
            V.tensor_scalar(pos[0][:, :], s_i[:, 0:TB], 0, None, ALU.logical_shift_right).then_inc(S["chain"], 1)
            dve.wait_ge(S["chain"], 2)
            V.tensor_scalar(loBT[0][0:EP, 0:4, 0:100].bitcast(I32), s_i[:, :].rearrange("p (a b) -> p a b", a=4), P - 1, None,
                            ALU.bitwise_and).then_inc(S["chain"], 1)
            V.tensor_scalar(loBT[1][0:EP, 0:4, 0:100].bitcast(I32), s_i[:, :].rearrange("p (a b) -> p a b", a=4), SHIFT, None,
                            ALU.logical_shift_right).then_inc(S["chain"], 1)
            dve.wait_ge(S["chain"], 4)
            V.tensor_copy(b_f[:, :].rearrange("p (a b) -> p a b", a=4), loBT[0][0:EP, 0:4, 0:100].bitcast(I32)).then_inc(S["chain"], 1)
            dve.wait_ge(S["consts"], 9)
            V.tensor_copy(identb[:, :], ident[:, :]).then_inc(S["identb_ready"], 1)
            V.tensor_copy(iotab[:, :], iota[:, :]).then_inc(S["identb_ready"], 1)
            a_cols = loBT[0][0:EP, 4:8, 0:100]
            V.tensor_copy(a_cols, loBT[1][0:EP, 0:4, 0:100].bitcast(I32)).then_inc(S["chain"], 1)
            dve.wait_ge(S["chain"], 6)
            for a in range(4):
                w = EC // 4
                V.tensor_tensor(hiA[:, a * w:(a + 1) * w, :], iota[0:EP, None, 0:NB].to_broadcast([EP, w, NB]),
                                loBT[0][0:EP, 4 + a, 0:100, None].to_broadcast([EP, w, NB]), ALU.is_equal).then_inc(S["a_ready"], 1)

            def onehot(i, k):
                first = i * TB
                cols = b_f[:, first:first + TB] if isinstance(i, int) else b_f[:, bass.ds(first, TB)]
                return V.tensor_tensor(loB[k][:, :, :], iota[0:EP, None, :].to_broadcast([EP, TB, P]),
                                       cols.unsqueeze(2).to_broadcast([EP, TB, P]), ALU.is_equal)

            def pass1(i, k):
                ge(dve, S["hist"], i - 1)
                onehot(i, k).then_inc(S["onehot"], 1)

            batches(dve, pass1)

            dve.wait_ge(S["hist"], NBATCH)
            V.tensor_copy(tot[:, :], bank[7][:, 0:NB]).then_inc(S["tot_sb"], 1)
            dve.wait_ge(S["base_mm"], 1)
            V.tensor_scalar(bsum[:, :], bank[7][:, 64:64 + NB], float(GS - 1), None, ALU.add).then_inc(S["chain"], 1)
            dve.wait_ge(S["chain"], 7)
            V.tensor_copy(ngrp_i[:, :], bsum[:, :]).then_inc(S["chain"], 1)
            dve.wait_ge(S["chain"], 8)
            V.tensor_scalar(ngrp_i[:, :], ngrp_i[:, :], GSHIFT, None, ALU.logical_shift_right).then_inc(S["chain"], 1)
            dve.wait_ge(S["chain"], 9)
            V.tensor_copy(ngrp[:, :], ngrp_i[:, :]).then_inc(S["chain"], 1)
            dve.wait_ge(S["chain"], 10)
            V.tensor_tensor_scan(incl[:, :], ngrp[:, :], zrow[:, :], 0.0, ALU.add, ALU.add).then_inc(S["chain"], 1)
            dve.wait_ge(S["chain"], 11)
            V.tensor_tensor(excl[:, :], incl[:, :], ngrp[:, :], ALU.subtract).then_inc(S["chain"], 1)
            dve.wait_ge(S["chain"], 12)
            V.scalar_tensor_tensor(tot[:, :], excl[:, :], float(GS), bank[7][:, 128:128 + NB], ALU.mult, ALU.add)\
                .then_inc(S["base_ready"], 1)
            dve.wait_ge(S["base_ready"], 1)
            V.tensor_scalar(cnt[0][:, 0, :], tot[:, :], float(LEAD), None, ALU.add).then_inc(S["base_ready"], 1)
            V.tensor_tensor(gle[:, :, :], incl[0:1, None, :].to_broadcast([1, NG, NB]), gid[:, :, None].to_broadcast([1, NG, NB]), ALU.is_le).then_inc(S["chain"], 1)
            dve.wait_ge(S["chain"], 13)
            V.tensor_reduce(gblk[:, :], gle[:, :, :], AX_X, ALU.add).then_inc(S["chain"], 1)
            dve.wait_ge(S["chain"], 14)
            V.tensor_scalar(blk_i[:, :], gblk[:, :], float(NB - 1), None, ALU.min).then_inc(S["blk_ready"], 1)

            dve.wait_ge(S["in_x"], 32)
            for t in range(NB):
                V.bn_stats(stats[:, 0:6], xs[:, t, :]).then_inc(S["lnchain"], 1)
                dve.wait_ge(S["lnchain"], 2 * t + 1)
                V.bn_aggr(mv[:, t, :], stats[:, 0:6]).then_inc(S["lnchain"], 1)
                dve.wait_ge(S["lnchain"], 2 * t + 2)
            V.tensor_scalar(std[:, :], mv[:, :, 1], LN_EPS, None, ALU.add).then_inc(S["lnchain"], 1)
            dve.wait_ge(S["lnchain"], 2 * NB + 2)
            V.reciprocal(rstd[:, :], std[:, :]).then_inc(S["lnchain"], 1)
            dve.wait_ge(S["lnchain"], 2 * NB + 3)
            dve.wait_ge(S["in_w"], 32)
            V.tensor_scalar(bias[:, 0:DH], bias[:, 0:DH], SCALE, None, ALU.mult).then_inc(S["lnchain"], 1)
            V.tensor_scalar(Wqkv_s[:, :, 0:DH], Wqkv_s[:, :, 0:DH], SCALE, None, ALU.mult).then_inc(S["lnchain"], 1)
            dve.wait_ge(S["in_small"], 64 * (STK // AUG))
            dve.wait_ge(S["recb_const"], 9)
            for n in range(PARTS):
                left = wraw if n == 0 else wres
                V.tensor_copy(wpart[n][:, :], left[:, :]).then_inc(S["wstk"], 1)
                dve.wait_ge(S["wstk"], 2 * n + 1)
                V.tensor_tensor(wres[:, :], left[:, :], wpart[n][:, :], ALU.subtract).then_inc(S["wstk"], 1)
                dve.wait_ge(S["wstk"], 2 * n + 2)
            V.tensor_scalar(wmask[:, 2:3], wmask[:, 0:1], -1.0, 1.0, ALU.mult, ALU.add).then_inc(S["wstk"], 1)
            V.tensor_tensor(wmask[:, 3:4], wmask[:, 0:1], wmask[:, 1:2], ALU.subtract).then_inc(S["wstk"], 1)
            dve.wait_ge(S["wstk"], 2 * PARTS + 2)
            V.tensor_scalar(wsum[0][:, :], wpart[0][:, :], wmask[:, 2:3], None, ALU.mult).then_inc(S["wstk"], 1)
            dve.wait_ge(S["wstk"], 2 * PARTS + 3)
            V.scalar_tensor_tensor(wsum[1][:, :], wpart[1][:, :], wmask[:, 3:4], wsum[0][:, :], ALU.mult, ALU.add).then_inc(S["wstk"], 1)
            dve.wait_ge(S["wstk"], 2 * PARTS + 4)
            V.scalar_tensor_tensor(Wrpe[:, :], wpart[2][:, :], wmask[:, 1:2], wsum[1][:, :], ALU.mult, ALU.add).then_inc(S["wstk"], 1)
            dve.wait_ge(S["lnchain"], 2 * NB + 5)

            def normalize(t, k):
                ge(dve, S["xT_done"], t - 1)
                V.tensor_scalar(xl[k][:, :], xs[:, bass.ds(t, 1), :].rearrange("p a d -> p (a d)"),
                                mv[:, bass.ds(t, 1), 0], rstd[:, bass.ds(t, 1)],
                                ALU.subtract, ALU.mult).then_inc(S["normed"], 1)

            def table(t, k, i):
                dve.wait_ge(S["qkv_done"], t + 1)
                ge(dve, S[f"kv_stored{k}"], 32 * i)
                ge(dve, S["qkp3"], t)
                V.tensor_tensor(kvrow[k][:, :], bank[2 + k][:, 2 * DH:2 * DH + DIM], bias[:, 2 * DH:2 * DH + DIM], ALU.add)
                V.tensor_tensor(qk32[:, :], bank[2 + k][:, 0:2 * DH], bias[:, 0:2 * DH], ALU.add).then_inc(S["table_ready"], 1)
                dve.wait_ge(S["qkp1"], t + 1)
                V.tensor_tensor(qkres[:, :], qk32[:, :], qkp[k][:, 0, :], ALU.subtract).then_inc(S["qk_chain"], 1)
                dve.wait_ge(S["qkp2"], t + 1)
                V.tensor_tensor(qkp[k][:, 2, :], qkres[:, :], qkp[k][:, 1, :], ALU.subtract).then_inc(S["qkp3"], 1)

            normalize(0, 0)
            normalize(1, 1)
            table(0, 0, 0)
            normalize(2, 0)
            table(1, 1, 0)
            with dve.Fori(1, (NB - 1) // 2) as i:
                normalize(2 * i + 1, 1)
                table(2 * i, 0, i)
                normalize(2 * i + 2, 0)
                table(2 * i + 1, 1, i)
            table(NB - 1, 0, (NB - 1) // 2)

            def lo_onehot(i, k):
                ge(dve, S["loB_used"], i - 1)
                onehot(i, k).then_inc(S["loB_ready"], 1)

            def counts(i, k):
                dve.wait_ge(S["loB_used"], i + 1)
                ge(dve, S["lk_done"], i)
                for j in range(TB):
                    nxt = cnt[k][:, j + 1, :] if j + 1 < TB else cnt[1 - k][:, 0, :]
                    V.tensor_tensor(nxt, cnt[k][:, j, :], bank[k][:, j * NB:(j + 1) * NB], ALU.add).then_inc(S["cnt_ready"], 1)
                    dve.wait_ge(S["cnt_ready"], i * TB + (j + 1))

            def after_first_part(i, k):
                raw = ea_raw[:, bass.ds(i * (TB * NA), TB * NA)].rearrange("p (j a) -> p j a", a=NA)
                parts = recb[k][:, :, F_EA:RW].bitcast(BF16).rearrange("p j (b a) -> p j b a", a=AUG)
                dve.wait_ge(S["e1_ready"], i + 1)
                V.tensor_tensor(eres[k][:, :, :], raw, parts[:, :, 0, 0:NA], ALU.subtract).then_inc(S["eres_ready"], 1)

            def third_part(i, k):
                parts = recb[k][:, :, F_EA:RW].bitcast(BF16).rearrange("p j (b a) -> p j b a", a=AUG)
                dve.wait_ge(S["e2_ready"], i + 1)
                V.tensor_tensor(parts[:, :, 2, 0:NA], eres[k][:, :, :], parts[:, :, 1, 0:NA], ALU.subtract)\
                    .then_inc(S["e3_ready"], 1)

            def slots(i, k):
                dve.wait_ge(S["sbc_done"], i + 1)
                for j in range(TB):
                    col = s_f[:, i * TB + j:i * TB + j + 1] if isinstance(i, int) else s_f[:, bass.ds(i * TB + j, 1)]
                    V.scalar_tensor_tensor(same[:, j, :], bank[4 + j // 4][0:EP, (j % 4) * P:(j % 4) * P + EP], col,
                                           lower[0:EP, 0:EP], ALU.is_equal, ALU.mult,
                                           accum_out=within[:, j:j + 1]).then_inc(S["within_ready"], 1)
                dve.wait_ge(S["lk_done"], i + 1)
                V.tensor_tensor(picked[:, :, :], bank[6][0:EP, 0:TB * NB].rearrange("p (j a) -> p j a", a=NB),
                                hiA[:, bass.ds(i * TB, TB), :], ALU.mult).then_inc(S["pos_chain"], 1)
                dve.wait_ge(S["pos_chain"], 2 * i + 1)
                V.tensor_reduce(prior[:, :], picked[:, :, :], AX_X, ALU.add).then_inc(S["pos_chain"], 1)
                dve.wait_ge(S["pos_chain"], 2 * i + 2)
                dve.wait_ge(S["within_ready"], TB * (i + 1))
                ge(dve, S[f"scat{k}"], (i - k) * (8 * TB))
                V.tensor_tensor(pos[k][:, :], prior[:, :], within[:, :], ALU.add).then_inc(S["pos_ready"], 1)

            lo_onehot(0, 0)
            lo_onehot(1, 1)
            after_first_part(0, 0)
            counts(0, 0)
            third_part(0, 0)
            slots(0, 0)
            lo_onehot(2, 0)
            after_first_part(1, 1)
            counts(1, 1)
            third_part(1, 1)
            slots(1, 1)
            with dve.Fori(1, NBATCH // 2 - 1) as i:
                lo_onehot(2 * i + 1, 1)
                after_first_part(2 * i, 0)
                counts(2 * i, 0)
                third_part(2 * i, 0)
                slots(2 * i, 0)
                lo_onehot(2 * i + 2, 0)
                after_first_part(2 * i + 1, 1)
                counts(2 * i + 1, 1)
                third_part(2 * i + 1, 1)
                slots(2 * i + 1, 1)
            lo_onehot(NBATCH - 1, 1)
            after_first_part(NBATCH - 2, 0)
            counts(NBATCH - 2, 0)
            third_part(NBATCH - 2, 0)
            slots(NBATCH - 2, 0)
            after_first_part(NBATCH - 1, 1)
            counts(NBATCH - 1, 1)
            third_part(NBATCH - 1, 1)
            slots(NBATCH - 1, 1)

            after_sort(dve)
            for n in range(RING):
                V.memset(pen[n][:, GS:GS + 1], 0.0)
            V.memset(dbuf[:, :], 0.0).then_inc(S["init_ready"], 1)
            dve.wait_ge(S["init_ready"], 4)

            def onehots(g, k, i):
                dve.wait_ge(S[f"rec_ready{k}"], 32 * i + 32)
                ge(dve, S["tr_oh"], g - 1)
                ge(dve, S["oh32_ready"], g - 1)
                for j in range(G):
                    ins = V.tensor_scalar(oh[k % 2][:, j, :], iotab[:, :], rec[k][:, j, F_B:F_B + 1], None, ALU.is_equal)
                ins.then_inc(S["oh_ready"], 1)
                V.tensor_tensor(new[k % 2][:, 1:G], rec[k][:, 1:G, F_S], rec[k][:, 0:G - 1, F_S], ALU.not_equal)
                V.tensor_tensor(new[k % 2][:, 0:1], rec[k][:, 0, F_S:F_S + 1], before[k][:, :], ALU.not_equal).then_inc(S["new_ready"], 1)
                dve.wait_ge(S["new_ready"], g + 1)
                ge(dve, S["tr_s"], g - 1)
                V.tensor_scalar(newr[k % 2][:, :, :], new[k % 2][:, :, None].to_broadcast([P, G, H]), LOW, None, ALU.mult)\
                    .then_inc(S["newr_ready"], 1)

            def scores(g, k):
                dve.wait_ge(S["ke_ready"], g + 1)
                for a in range(2):
                    V.tensor_tensor(prod[:, 2 * a:2 * a + 2, :],
                                    bank[3 + a][:, :].rearrange("p (j c) -> p j c", c=2 * DH)[:, :, 0:DH],
                                    ke[:, 2 * a:2 * a + 2, :], ALU.mult).then_inc(S["prod_done"], 1)
                dve.wait_ge(S["prod_done"], 2 * g + 2)
                V.tensor_reduce(cc[k % 2][:, :, :].rearrange("p j h -> p (j h)"),
                                prod[:, :, :].rearrange("p j (h d) -> p (j h) d", d=D), AX_X, ALU.add).then_inc(S["c_ready"], 1)

            def maxima(g, k):
                dve.wait_ge(S["pen_ready"], g + 1)
                dve.wait_ge(S["ct_done"], g + 1)
                first = isinstance(g, int) and g == 0
                before_it = fw[(k - 1) % 2][:, GS - 1:GS]
                V.tensor_tensor_scan(fw[k % 2][:, :], pen[k][:, 0:GS], bank[5][0:H, :],
                                     LOW if first else before_it, ALU.add, ALU.max).then_inc(S["fw_ready"], 1)
                dve.wait_ge(S["fw_ready"], g + 1)
                ge(dve, S["smt_done"], g)
                V.tensor_tensor_scan(segm[:, GS - 1::-1], pen[k][:, GS:0:-1], fw[k % 2][:, GS - 1::-1],
                                     LOW, ALU.add, ALU.max).then_inc(S["sm_ready"], 1)
                dve.wait_ge(S["sm_ready"], g + 1)
                if not first:
                    V.tensor_tensor(dlt[:, :], before_it, segm[:, 0:1], ALU.subtract).then_inc(S["dlt_ready"], 1)
                    dve.wait_ge(S["dlt_ready"], g)
                    V.scalar_tensor_tensor(dbuf[:, 0:1], pen[k][:, 0:1], 0.0, dlt[:, :], ALU.is_equal, ALU.mult)\
                        .then_inc(S["dbuf_ready"], 1)

            def shifts(g, k):
                dve.wait_ge(S["smt_done"], g + 1)
                V.tensor_tensor(diff[k][:, :, :].rearrange("p j h -> p (j h)"), cc[k % 2][:, :, :].rearrange("p j h -> p (j h)"),
                                bank[6][:, 0:G * H], ALU.subtract).then_inc(S["diff_ready"], 1)
                V.tensor_copy(dT[k][:, :], bank[6][:, G * H:G * H + H]).then_inc(S["dT_ready"], 1)

            def weighted(g, k):
                dve.wait_ge(S["w_exp"], g + 1)
                V.tensor_tensor(wv[k % 2][:, :, :, 0:DV],
                                kv[k][:, :, KW:KV].rearrange("p j (h d) -> p j h d", d=DV),
                                wv[k % 2][:, :, :, DV:DVA].to_broadcast([P, G, H, DV]), ALU.mult).then_inc(S["w_ready"], 1)

            def accumulate(g, k):
                here = dve.value_load(blk_i[0:1, bass.ds(g, 1)], min_val=0, max_val=NB - 1)
                mine = acc[:, bass.ds(here * AW, AW)]
                dve.wait_ge(S["fac_ready"], g + 1)
                ge(dve, S["acc_done"], g)
                V.tensor_tensor(mine.rearrange("p (h d) -> p h d", d=DVA), mine.rearrange("p (h d) -> p h d", d=DVA),
                                fac[k][:, :, None].to_broadcast([P, H, DVA]), ALU.mult).then_inc(S["acc_scaled"], 1)
                dve.wait_ge(S["acc_scaled"], g + 1)
                dve.wait_ge(S["seg_done"], g + 1)
                V.tensor_tensor(mine, mine, bank[7][:, 0:AW], ALU.add).then_inc(S["acc_done"], 1)

            for n in range(RING - 1):
                onehots(n, n, 0)
            scores(0, 0)

            def step(g, k, i):
                inner = not isinstance(g, int)
                maxima(g, k)
                if inner or g + 3 < NG:
                    onehots(g + 3, (k + 3) % RING, i + (k + 3) // RING)
                shifts(g, k)
                if inner or g + 1 < NG:
                    scores(g + 1, (k + 1) % RING)
                if inner or g:
                    accumulate(g - 1, (k - 1) % RING)
                weighted(g, k)

            groups(dve, step)
            accumulate(NG - 1, RING - 1)

            dve.wait_ge(S["ex_small"], 96)
            dve.wait_ge(S["acc_done"], NG)
            dve.wait_ge(S["b1T_done"], 1)
            V.tensor_copy(b1T[:, :], bank[7][:, 0:NX * MH]).then_inc(S["b1T_ready"], 1)
            steps = 14 * CB + 11

            def prepare(c, nb, kx):
                n = [0]

                def did(ins):
                    n[0] += 1
                    ins.then_inc(S["prep"], 1)
                    wait_turn(dve, prep_turn, [S["prep"]])

                for q in range(nb):
                    b = c * CB + q
                    mine = acc[:, bass.ds(b * AW, AW)].rearrange("p (h d) -> p h d", d=DVA)
                    xb = xs[:, bass.ds(b, 1), :].rearrange("p a d -> p (a d)")
                    did(V.tensor_scalar(iden[:, :], mine[:, :, DV], DEN_EPS, None, ALU.add))
                    did(V.reciprocal(iden[:, :], iden[:, :]))
                    did(V.tensor_tensor(mine[:, :, 0:DV], mine[:, :, 0:DV], iden[:, :, None].to_broadcast([P, H, DV]), ALU.mult))
                    did(V.tensor_tensor(xb.rearrange("p (h d) -> p h d", d=DV), xb.rearrange("p (h d) -> p h d", d=DV),
                                        mine[:, :, 0:DV], ALU.add))
                    did(V.bn_stats(stats[:, 0:6], xb))
                    did(V.bn_aggr(mv[:, q, :], stats[:, 0:6]))
                did(V.tensor_scalar(std[:, 0:nb], mv[:, 0:nb, 1], LN_EPS, None, ALU.add))
                dve.wait_ge(S["prep_act"], 3 * c + 1)
                did(V.reciprocal(rstd[:, 0:nb], std[:, 0:nb]))
                ge(dve, S["hnT_done"], c)
                for q in range(nb):
                    xb = xs[:, bass.ds(c * CB + q, 1), :].rearrange("p a d -> p (a d)")
                    did(V.tensor_scalar(hn[:, q, :], xb, mv[:, q, 0:1], rstd[:, q:q + 1], ALU.subtract, ALU.mult))
                    did(V.bn_stats(stats[:, 0:6], hn[:, q, :]))
                    did(V.bn_aggr(mv[:, q, :], stats[:, 0:6]))
                did(V.tensor_scalar(std[:, 0:nb], mv[:, 0:nb, 1], LN_EPS, None, ALU.add))
                dve.wait_ge(S["prep_act"], 3 * c + 2)
                did(V.reciprocal(rstd[:, 0:nb], std[:, 0:nb]))
                for q in range(nb):
                    did(V.tensor_scalar(hn[:, q, :], hn[:, q, :], mv[:, q, 0:1], rstd[:, q:q + 1], ALU.subtract, ALU.mult))
                did(V.tensor_tensor(hn[:, 0:nb, :], hn[:, 0:nb, :], gam[:, None, :].to_broadcast([P, nb, DIM]), ALU.mult))
                V.tensor_tensor(hn[:, 0:nb, :], hn[:, 0:nb, :], bet[:, None, :].to_broadcast([P, nb, DIM]), ALU.add)\
                    .then_inc(S["hn_ready"], 1)
                dve.wait_ge(S["logit_done"], c + 1)
                did(V.tensor_tensor(lg[:, 0:nb, :], bank[5][:, 0:nb * NX].rearrange("p (q e) -> p q e", e=NX),
                                    br_s[:, None, :].to_broadcast([P, nb, NX]), ALU.add))
                for q in range(nb):
                    did(V.max(top[:, q, :], lg[:, q, :]))
                    did(V.max_index(topi[:, q, :], top[:, q, :], lg[:, q, :]))
                did(V.tensor_copy(topf[:, 0:nb, :], topi[:, 0:nb, 0:2]))
                did(V.tensor_tensor(e1[:, 0:nb], top[:, 0:nb, 1], top[:, 0:nb, 0], ALU.subtract))
                dve.wait_ge(S["prep_act"], 3 * c + 3)
                did(V.tensor_scalar(w0[:, 0:nb], e1[:, 0:nb], 1.0, None, ALU.add))
                did(V.reciprocal(w0[:, 0:nb], w0[:, 0:nb]))
                did(V.tensor_tensor(w1[:, 0:nb], w0[:, 0:nb], e1[:, 0:nb], ALU.mult))
                for q in range(nb):
                    did(V.tensor_scalar(hit[:, q, 0, :], iota[:, 0:NX], topf[:, q, 0:1], w0[:, q:q + 1], ALU.is_equal, ALU.mult))
                    did(V.tensor_scalar(hit[:, q, 1, :], iota[:, 0:NX], topf[:, q, 1:2], w1[:, q:q + 1], ALU.is_equal, ALU.mult))
                V.tensor_tensor(wf[kx][:, 0:nb, :], hit[:, 0:nb, 0, :], hit[:, 0:nb, 1, :], ALU.add).then_inc(S["wf_ready"], 1)
                assert nb < CB or n[0] == per_chunk(CB), (n[0], per_chunk(CB))

            def per_chunk(nb):
                return 14 * nb + 11

            def combine(c, nb, kx):
                for q in range(nb):
                    xb = xs[:, bass.ds(c * CB + q, 1), :].rearrange("p a d -> p (a d)")
                    dve.wait_ge(S["b2_done"], c * CB + q + 1)
                    V.tensor_tensor(xb, xb, bank[6 + q % 2][:, 0:DIM], ALU.add).then_inc(S["xb2_added"], 1)
                dve.wait_ge(S["xb2_added"], c * CB + nb)
                for e in range(NX):
                    for q in range(nb):
                        at = c * (NX * CB) + e * nb + q
                        xb = xs[:, bass.ds(c * CB + q, 1), :].rearrange("p a d -> p (a d)")
                        dve.wait_ge(S["y_done"], at + 1)
                        if e:
                            dve.wait_ge(S["y_added"], at - nb + 1)
                        V.scalar_tensor_tensor(xb, bank[6 + q % 2][:, 0:DIM], wf[kx][:, q, e:e + 1], xb,
                                               ALU.mult, ALU.add).then_inc(S["y_added"], 1)

            prepare(0, CB, 0)
            combine(0, CB, 0)
            with dve.Fori(1, NCH - 1) as c:
                prepare(c, CB, 0)
                combine(c, CB, 0)
            prepare(NCH - 1, NB - (NCH - 1) * CB, 0)
            combine(NCH - 1, NB - (NCH - 1) * CB, 0)

        @block.scalar
        def _(act):
            A = nc.scalar
            act.wait_ge(S["lnchain"], 2 * NB + 1)
            A.activation(std[:, :], std[:, :], ACT.Sqrt).then_inc(S["lnchain"], 1)

            def copy_xT(t, k):
                act.wait_ge(S["xT_done"], t + 1)
                ge(act, S["qkv_done"], t - 1)
                A.activation(xlT[k][:, :], bank[k][:, 0:DIM], ACT.Copy).then_inc(S["xT_copied"], 1)

            def table_parts(t, k, i):
                act.wait_ge(S["table_ready"], t + 1)
                ge(act, S[f"kv_stored{k}"], 32 * i)
                A.activation(qkp[k][:, 0, :], qk32[:, :], ACT.Copy).then_inc(S["qkp1"], 1)
                act.wait_ge(S["qk_chain"], t + 1)
                A.activation(qkp[k][:, 1, :], qkres[:, :], ACT.Copy).then_inc(S["qkp2"], 1)
                act.wait_ge(S["qkp3"], t + 1)
                A.activation(q_tab[:, bass.ds(t, 1), :, :].rearrange("p t a c -> p (t a) c"), qkp[k][:, :, 0:DH], ACT.Copy)\
                    .then_inc(S["qtab_ready"], 1)

            copy_xT(0, 0)
            copy_xT(1, 1)
            table_parts(0, 0, 0)
            copy_xT(2, 0)
            table_parts(1, 1, 0)
            with act.Fori(1, (NB - 1) // 2) as i:
                copy_xT(2 * i + 1, 1)
                table_parts(2 * i, 0, i)
                copy_xT(2 * i + 2, 0)
                table_parts(2 * i + 1, 1, i)
            table_parts(NB - 1, 0, (NB - 1) // 2)

            act.wait_ge(S["in_ea"], 32)

            def batch(i, k):
                ge(act, S[f"scat{k}"], (i - k) * (8 * TB))
                ge(act, S["sbc_done"], i - 1)
                A.activation(recb[k][:, :, F_T:F_T + 1].rearrange("p j r -> p (j r)").bitcast(I32), t_i[:, bass.ds(i * TB, TB)], ACT.Copy)
                A.activation(recb[k][:, :, F_S:F_S + 1].rearrange("p j r -> p (j r)"), s_f[:, bass.ds(i * TB, TB)], ACT.Copy)
                A.activation(recb[k][:, :, F_B:F_B + 1].rearrange("p j r -> p (j r)"), b_f[:, bass.ds(i * TB, TB)], ACT.Copy)
                raw = ea_raw[:, bass.ds(i * (TB * NA), TB * NA)].rearrange("p (j a) -> p j a", a=NA)
                parts = recb[k][:, :, F_EA:RW].bitcast(BF16).rearrange("p j (b a) -> p j b a", a=AUG)
                for b in (0, 3, 5):
                    ins = A.activation(parts[:, :, b, 0:NA], raw, ACT.Copy)
                ins.then_inc(S["e1_ready"], 1)
                act.wait_ge(S["eres_ready"], i + 1)
                A.activation(parts[:, :, 1, 0:NA], eres[k][:, :, :], ACT.Copy).then_inc(S["e2_ready"], 1)
                A.activation(parts[:, :, 4, 0:NA], eres[k][:, :, :], ACT.Copy).then_inc(S["recb_ready"], 1)
                act.wait_ge(S["loB_used"], i + 1)
                ge(act, S["lk_done"], i - 1)
                A.activation(loBT[k][:, :, 0:EP], bank[2 + k][:, :].bitcast(BF16).rearrange("p (j e) -> p j e", e=P)[:, :, 0:EP],
                             ACT.Copy).then_inc(S["loBT_ready"], 1)

            batches(act, batch)

            def turned(g, k):
                act.wait_ge(S["tr_oh"], g + 1)
                ge(act, S["qk_done"], g - 1)
                A.activation(ohT[k % 2][:, :], bank[0][:, :].bitcast(BF16)[:, 0:GS], ACT.Copy).then_inc(S["oht_copied"], 1)
                act.wait_ge(S["tr_ea"], g + 1)
                A.activation(eaT[k % 2][:, :], bank[1][0:STK, :].bitcast(BF16)[:, 0:GS], ACT.Copy).then_inc(S["eat_copied"], 1)
                act.wait_ge(S["tr_s"], g + 1)
                ge(act, S["sm_ready"], g - RING + 1)
                A.activation(pen[k][:, 0:GS], bank[2][0:H, :], ACT.Copy).then_inc(S["pen_ready"], 1)
                ge(act, S["seg_done"], g - RING + 1)
                A.activation(oh32[k][:, :, :], oh[k % 2][:, :, :], ACT.Copy).then_inc(S["oh32_ready"], 1)

            def keys(g, k):
                act.wait_ge(S["qk_done"], g + 1)
                ge(act, S["prod_done"], 2 * g)
                for a in range(2):
                    ins = A.activation(ke[:, 2 * a:2 * a + 2, :],
                                       bank[3 + a][:, :].rearrange("p (j c) -> p j c", c=2 * DH)[:, :, DH:2 * DH], ACT.Copy)
                ins.then_inc(S["ke_ready"], 1)

            def exps(g, k):
                act.wait_ge(S["diff_ready"], g + 1)
                ge(act, S["seg_done"], g - 1)
                A.activation(wv[k % 2][:, :, :, DV], diff[k][:, :, :], ACT.Exp).then_inc(S["w_exp"], 1)

            def factor(g, k):
                act.wait_ge(S["f_done"], g + 1)
                A.activation(fac[k][:, :], bank[6][:, 0:H], ACT.Exp).then_inc(S["fac_ready"], 1)

            act.wait_ge(S["init_ready"], 4)
            turned(0, 0)
            turned(1, 1)
            keys(0, 0)
            turned(2, 2)
            keys(1, 1)

            def step(g, k, i):
                inner = not isinstance(g, int)
                exps(g, k)
                factor(g, k)
                if inner or g + 3 < NG:
                    turned(g + 3, (k + 3) % RING)
                if inner or g + 2 < NG:
                    keys(g + 2, (k + 2) % RING)

            groups(act, step)

            act.wait_ge(S["b1T_ready"], 1)
            steps = 14 * CB + 11

            def chunk(c, nb):
                W = nb * P
                base = c * steps
                act.wait_ge(S["prep"], base + 6 * nb + 1)
                A.activation(std[:, 0:nb], std[:, 0:nb], ACT.Sqrt).then_inc(S["prep_act"], 1)
                act.wait_ge(S["prep"], base + 9 * nb + 3)
                A.activation(std[:, 0:nb], std[:, 0:nb], ACT.Sqrt).then_inc(S["prep_act"], 1)
                for k in range(KD):
                    act.wait_ge(S["hnT_done"], c + 1)
                    A.activation(xnT[0][:, k, 0:W], bank[k][:, 0:W], ACT.Copy).then_inc(S["xnT_ready"], 1)
                act.wait_ge(S["prep"], base + 12 * nb + 8)
                A.activation(e1[:, 0:nb], e1[:, 0:nb], ACT.Exp).then_inc(S["prep_act"], 1)
                act.wait_ge(S["wft_done"], c + 1)
                A.activation(wfT[:, 0:W], bank[4][0:NX, 0:W], ACT.Copy).then_inc(S["wft_ready"], 1)
                for e in range(NX):
                    for m in range(MH):
                        at = c * (NX * MH) + e * MH + m
                        act.wait_ge(S["h_done"], at + 1)
                        if e >= 2:
                            act.wait_ge(S["y_done"], c * (NX * CB) + (e - 1) * nb)
                        A.activation(hT[e % 2][:, m, 0:W], bank[m % 4][:, 0:W], ACT.Gelu,
                                     bias=b1T[:, e * MH + m:e * MH + m + 1]).then_inc(S["gelu_done"], 1)

            chunk(0, CB)
            with act.Fori(1, NCH - 1) as c:
                chunk(c, CB)
            chunk(NCH - 1, NB - (NCH - 1) * CB)

        @block.tensor
        def _(pe):
            T = nc.tensor
            maxima_turn = pe.alloc_register("maxima_turn")
            pe.reg_mov(maxima_turn, RING + 1)
            pe.wait_ge(S["a_ready"], 4)

            def histogram(i, k):
                pe.wait_ge(S["onehot"], i + 1)
                for j in range(TB):
                    mm = T.matmul(bank[7][:, 0:NB], loB[k][:, j, :],
                                  hiA[:, bass.ds(i * TB + j, 1), :].rearrange("p a n -> p (a n)"),
                                  start=(isinstance(i, int) and i == 0 and j == 0),
                                  stop=(isinstance(i, int) and i == NBATCH - 1 and j == TB - 1), skip_group_check=True)
                mm.then_inc(S["hist"], 1)

            batches(pe, histogram)
            pe.wait_ge(S["consts"], 9)
            pe.wait_ge(S["tot_sb"], 1)
            T.matmul(bank[7][:, 64:64 + NB], ones[:, :], tot[:, :], start=True, stop=True, skip_group_check=True)
            T.matmul(bank[7][:, 128:128 + NB], upper[:, :], tot[:, :], start=True, stop=True,
                     skip_group_check=True).then_inc(S["base_mm"], 1)

            pe.wait_ge(S["in_w"], 32)

            def turn_x(t, k):
                pe.wait_ge(S["normed"], t + 1)
                ge(pe, S["xT_copied"], t - 1)
                for a in range(KD):
                    mm = T.transpose(bank[k][:, a * P:(a + 1) * P], xl[k][:, a * P:(a + 1) * P], ident[:, :])
                mm.then_inc(S["xT_done"], 1)

            def project(t, k):
                pe.wait_ge(S["xT_copied"], t + 1)
                ge(pe, S["table_ready"], t - 1)
                for a in range(KD):
                    mm = T.matmul(bank[2 + k][:, :], xlT[k][:, a * P:(a + 1) * P], Wqkv_s[:, a, :],
                                  start=(a == 0), stop=(a == KD - 1))
                mm.then_inc(S["qkv_done"], 1)

            turn_x(0, 0)
            turn_x(1, 1)
            project(0, 0)
            turn_x(2, 0)
            project(1, 1)
            with pe.Fori(1, (NB - 1) // 2) as i:
                turn_x(2 * i + 1, 1)
                project(2 * i, 0)
                turn_x(2 * i + 2, 0)
                project(2 * i + 1, 1)
            project(NB - 1, 0)

            pe.wait_ge(S["identb_ready"], 2)
            pe.wait_ge(S["base_ready"], 2)
            pe.wait_ge(S["table_ready"], NB)

            def tile_counts(i, k):
                pe.wait_ge(S["loB_ready"], i + 1)
                ge(pe, S["cnt_ready"], (i - 1) * TB)
                ge(pe, S["loBT_ready"], i - 1)
                for j in range(TB):
                    T.matmul(bank[k][:, j * NB:(j + 1) * NB], loB[k][:, j, :],
                             hiA[:, bass.ds(i * TB + j, 1), :].rearrange("p a n -> p (a n)"),
                             start=True, stop=True, skip_group_check=True)
                for j in range(TB):
                    mm = T.transpose(bank[2 + k][:, :].bitcast(BF16)[:, j * P:j * P + EP], loB[k][:, j, :], identb[0:EP, 0:EP])
                mm.then_inc(S["loB_used"], 1)

            def spread_sources(i, k):
                ge(pe, S["within_ready"], i * TB)
                pe.wait_ge(S["e1_ready"], i + 1)
                for j in range(TB):
                    mm = T.matmul(bank[4 + j // 4][0:EP, (j % 4) * P:(j % 4) * P + EP],
                                  recb[k][:, j, F_S:F_S + 1].to_broadcast([EP, EP]), ident[0:EP, 0:EP],
                                  start=True, stop=True, skip_group_check=True)
                mm.then_inc(S["sbc_done"], 1)

            def look_up(i, k):
                pe.wait_ge(S["loBT_ready"], i + 1)
                pe.wait_ge(S["cnt_ready"], (i + 1) * TB)
                ge(pe, S["pos_chain"], 2 * i)
                for j in range(TB):
                    mm = T.matmul(bank[6][0:EP, j * NB:(j + 1) * NB], loBT[k][:, j, 0:EP], cnt[k][:, j, :],
                                  start=True, stop=True, skip_group_check=True)
                mm.then_inc(S["lk_done"], 1)

            tile_counts(0, 0)
            spread_sources(0, 0)
            tile_counts(1, 1)
            look_up(0, 0)
            spread_sources(1, 1)
            tile_counts(2, 0)
            look_up(1, 1)
            spread_sources(2, 0)
            with pe.Fori(1, NBATCH // 2 - 1) as i:
                tile_counts(2 * i + 1, 1)
                look_up(2 * i, 0)
                spread_sources(2 * i + 1, 1)
                tile_counts(2 * i + 2, 0)
                look_up(2 * i + 1, 1)
                spread_sources(2 * i + 2, 0)
            tile_counts(NBATCH - 1, 1)
            look_up(NBATCH - 2, 0)
            spread_sources(NBATCH - 1, 1)
            look_up(NBATCH - 1, 1)

            after_sort(pe)
            pe.wait_ge(S["wstk"], 2 * PARTS + 5)
            pe.wait_ge(S["blk_ready"], 1)
            pe.wait_ge(S["qtab_ready"], NB)

            def turn_edges(g, k, i):
                pe.wait_ge(S["oh_ready"], g + 1)
                ge(pe, S["oht_copied"], g)
                for j in range(G):
                    mm = T.transpose(bank[0][:, :].bitcast(BF16)[:, j * P:(j + 1) * P], oh[k % 2][:, j, :], identb[:, :])
                mm.then_inc(S["tr_oh"], 1)
                pe.wait_ge(S[f"rec_ready{k}"], 32 * i + 32)
                ge(pe, S["eat_copied"], g)
                for j in range(G):
                    mm = T.transpose(bank[1][0:STK, :].bitcast(BF16)[:, j * P:(j + 1) * P], rec[k][:, j, F_EA:RW].bitcast(BF16),
                                     identb[:, :])
                mm.then_inc(S["tr_ea"], 1)
                pe.wait_ge(S["newr_ready"], g + 1)
                ge(pe, S["pen_ready"], g)
                for j in range(G):
                    mm = T.transpose(bank[2][0:H, j::G], newr[k % 2][:, j, :], ident[:, :])
                mm.then_inc(S["tr_s"], 1)

            def queries_keys(g, k, i):
                here = pe.value_load(blk_i[0:1, bass.ds(g, 1)], min_val=0, max_val=NB - 1)
                pe.wait_ge(S["oht_copied"], g + 1)
                pe.wait_ge(S["eat_copied"], g + 1)
                pe.wait_ge(S[f"kv_ready{k}"], (16 * G) * i + 16 * G)
                ge(pe, S["prod_done"], 2 * g)
                for j in range(G):
                    o = bank[3 + j // 2][:, (j % 2) * 2 * DH:(j % 2 + 1) * 2 * DH]
                    T.matmul(o, eaT[k % 2][:, j * P:(j + 1) * P], Wrpe[:, :], start=True, stop=False, skip_group_check=True)
                    for a in range(PARTS):
                        T.matmul(o[:, 0:DH], ohT[k % 2][:, j * P:(j + 1) * P],
                                 q_tab[:, bass.ds(here, 1), a, :].rearrange("p b c -> p (b c)"), start=False, stop=False,
                                 skip_group_check=True)
                    for a in range(PARTS):
                        mm = T.matmul(o[:, DH:2 * DH], identb[:, :], kv[k][:, j, 0:KW].bitcast(BF16)[:, a * DH:(a + 1) * DH],
                                      start=False, stop=(a == PARTS - 1), skip_group_check=True)
                mm.then_inc(S["qk_done"], 1)

            def turn_scores(g, k):
                pe.wait_ge(S["c_ready"], g + 1)
                ge(pe, S["fw_ready"], g)
                for j in range(G):
                    mm = T.transpose(bank[5][0:H, j::G], cc[k % 2][:, j, :], ident[:, :])
                mm.then_inc(S["ct_done"], 1)

            def turn_maxima(g, k):
                if isinstance(g, int):
                    pe.wait_ge(S["sm_ready"], g + 1)
                    ge(pe, S["dbuf_ready"], g)
                    ge(pe, S["fac_ready"], g)
                else:
                    wait_turn(pe, maxima_turn, [S["sm_ready"]], [(S["dbuf_ready"], g), (S["fac_ready"], g)])
                for j in range(G):
                    T.transpose(bank[6][:, j * H:(j + 1) * H], segm[:, j::G], ident[0:H, 0:H])
                T.transpose(bank[6][:, G * H:(G + 1) * H], dbuf[:, :], ident[0:H, 0:H]).then_inc(S["smt_done"], 1)

            def growth(g, k):
                pe.wait_ge(S["dT_ready"], g + 1)
                pe.wait_ge(S["oh32_ready"], g + 1)
                T.matmul(bank[6][:, 0:H], oh32[k][:, 0, :], dT[k][:, :], start=True, stop=True,
                         skip_group_check=True).then_inc(S["f_done"], 1)

            def segment_sums(g, k):
                pe.wait_ge(S["w_ready"], g + 1)
                ge(pe, S["acc_done"], g)
                for j in range(G):
                    mm = T.matmul(bank[7][:, 0:AW], oh32[k][:, j, :], wv[k % 2][:, j, :, :].rearrange("p h d -> p (h d)"),
                                  start=(j == 0), stop=(j == G - 1))
                mm.then_inc(S["seg_done"], 1)

            turn_edges(0, 0, 0)
            turn_edges(1, 1, 0)
            queries_keys(0, 0, 0)
            turn_edges(2, 2, 0)
            turn_scores(0, 0)
            queries_keys(1, 1, 0)

            def step(g, k, i):
                inner = not isinstance(g, int)
                turn_maxima(g, k)
                if inner or g:
                    segment_sums(g - 1, (k - 1) % RING)
                growth(g, k)
                if inner or g + 3 < NG:
                    turn_edges(g + 3, (k + 3) % RING, i + (k + 3) // RING)
                if inner or g + 1 < NG:
                    turn_scores(g + 1, (k + 1) % RING)
                if inner or g + 2 < NG:
                    queries_keys(g + 2, (k + 2) % RING, i + (k + 2) // RING)

            groups(pe, step)
            segment_sums(NG - 1, RING - 1)

            pe.wait_ge(S["ex_small"], 96)
            pe.wait_ge(S["ex_w"], 16 * (KD + MH))
            pe.wait_ge(S["acc_done"], NG)
            T.transpose(bank[7][:, 0:NX * MH], b1_s[:, :], ident[0:NX * MH, 0:NX * MH]).then_inc(S["b1T_done"], 1)

            def chunk(c, nb):
                W = nb * P
                pe.wait_ge(S["hn_ready"], c + 1)
                ge(pe, S["gelu_done"], c * (NX * MH))
                for k in range(KD):
                    for q in range(nb):
                        mm = T.transpose(bank[k][:, q * P:(q + 1) * P], hn[:, q, k * P:(k + 1) * P], ident[:, :])
                mm.then_inc(S["hnT_done"], 1)
                pe.wait_ge(S["xnT_ready"], (c + 1) * KD)
                for q in range(nb):
                    for k in range(KD):
                        mm = T.matmul(bank[5][:, q * NX:(q + 1) * NX], xnT[0][:, k, q * P:(q + 1) * P], Wr_s[:, k, :],
                                      start=(k == 0), stop=(k == KD - 1), skip_group_check=True)
                mm.then_inc(S["logit_done"], 1)
                pe.wait_ge(S["wf_ready"], c + 1)
                ge(pe, S["wft_ready"], c)
                for q in range(nb):
                    mm = T.transpose(bank[4][0:NX, q * P:(q + 1) * P], wf[0][:, q, :], ident[:, :])
                mm.then_inc(S["wft_done"], 1)

                def hidden(e):
                    for m in range(MH):
                        at = c * (NX * MH) + e * MH + m
                        if not (isinstance(c, int) and c == 0 and e == 0 and m < 4):
                            if e > 0:
                                pe.wait_ge(S["gelu_done"], at - 3)
                        for k in range(KD):
                            mm = T.matmul(bank[m % 4][:, 0:W], W1s[:, k, e * HID + m * P:e * HID + (m + 1) * P], xnT[0][:, k, 0:W],
                                          start=(k == 0), stop=(k == KD - 1))
                        mm.then_inc(S["h_done"], 1)

                def output(e):
                    pe.wait_ge(S["gelu_done"], c * (NX * MH) + (e + 1) * MH)
                    for q in range(nb):
                        at = c * (NX * CB) + e * nb + q
                        if e or q >= 2:
                            pe.wait_ge(S["y_added"], at - 1 if nb > 1 else at)
                        for m in range(MH):
                            mm = T.matmul(bank[6 + q % 2][:, 0:DIM], hT[e % 2][:, m, q * P:(q + 1) * P],
                                          W2s[:, m, e * DIM:(e + 1) * DIM], start=(m == 0), stop=(m == MH - 1))
                        mm.then_inc(S["y_done"], 1)

                hidden(0)
                pe.wait_ge(S["wft_ready"], c + 1)
                ge(pe, S["y_added"], c * (NX * CB))
                for q in range(nb):
                    if q >= 2:
                        pe.wait_ge(S["xb2_added"], c * CB + q - 1)
                    T.matmul(bank[6 + q % 2][:, 0:DIM], wfT[:, q * P:(q + 1) * P], b2_s[:, :], start=True, stop=True)\
                        .then_inc(S["b2_done"], 1)
                pe.wait_ge(S["xb2_added"], c * CB + nb)
                for e in range(NX):
                    if e + 1 < NX:
                        hidden(e + 1)
                    output(e)

            chunk(0, CB)
            with pe.Fori(1, NCH - 1) as c:
                chunk(c, CB)
            chunk(NCH - 1, NB - (NCH - 1) * CB)


INPUTS = ['x', 'src', 'dst', 'edge_attr_18', 'L0_gnn_Wqkv', 'L0_gnn_bqkv', 'L0_gnn_Wk_rpe', 'L0_gnn_bk_rpe',
          'L0_gnn_Wq_rpe', 'L0_gnn_bq_rpe', 'L0_ffn_gamma', 'L0_ffn_beta', 'L0_ffn_Wr', 'L0_ffn_br', 'L0_ffn_W1',
          'L0_ffn_b1', 'L0_ffn_W2', 'L0_ffn_b2']


def kernel(**inputs):
    import numpy as _np
    import concourse.bacc as _bacc
    from concourse import mybir as _mybir
    from concourse.bass_utils import run_bass_kernel_spmd as _run

    nc = _bacc.Bacc("TRN2", target_bir_lowering=False, num_devices=1)
    arrays, args = {}, []
    for name in INPUTS:
        a = _np.ascontiguousarray(inputs[name])
        arrays[f"in_{name}"] = a
        args.append(nc.dram_tensor(f"in_{name}", a.shape, _mybir.dt.from_np(a.dtype), kind="ExternalInput").ap())
    shape = tuple(inputs['x'].shape)
    args.append(nc.dram_tensor("out_x", shape, _mybir.dt.from_np(_np.dtype("float32")), kind="ExternalOutput").ap())
    gnn_ffn(nc, *args)
    r = _run(nc, [arrays], core_ids=[0])
    return r.results[0]["out_x"]
```

```python
from contextlib import ExitStack

import concourse.bass as bass
from concourse import mybir

P = 128
ALU = mybir.AluOpType
ACT = mybir.ActivationFunctionType
F32 = mybir.dt.float32
BF16 = mybir.dt.bfloat16
I32 = mybir.dt.int32
U32 = mybir.dt.uint32
AX_X = mybir.AxisListType.X

LOW = -1.0e30
LN_EPS = 1e-5
DEN_EPS = 1e-16


def ge(engine, sem, count):
    if isinstance(count, int) and count <= 0:
        return
    engine.wait_ge(sem, count)


def wait_turn(engine, turn, sems, others=(), steps=1):
    count = engine.snap(turn)
    for sem in sems:
        engine.wait_ge(sem, count + (steps - 1) if steps > 1 else count)
    for sem, other in others:
        ge(engine, sem, other)
    engine.reg_add(turn, turn, steps)


def gnn_ffn(nc, x, src, dst, edge_attr, Wqkv, bqkv, Wk_rpe, bk_rpe, Wq_rpe, bq_rpe,
            gamma, beta, Wr, br, W1, b1, W2, b2, out):
    N, DIM = x.shape
    E, NA = edge_attr.shape
    DH = Wk_rpe.shape[1]
    D = 8
    H = DH // D
    DV = DIM // H
    SCALE = float(D) ** -0.5
    PARTS = 3
    KW = PARTS * DH // 2
    KV = KW + DIM
    KD = DIM // P
    NX, _, HID = W1.shape
    MH = HID // P

    NB = -(-N // P)
    TAIL = N - (NB - 1) * P
    SHIFT = 7
    EP = 125
    EC = E // EP
    TB = 8
    NBATCH = EC // TB
    assert EP * EC == E and NBATCH * TB == EC and NBATCH == 2 * NB
    G = 4
    GS = G * P
    GSHIFT = GS.bit_length() - 1
    NG = (E + NB * (GS - 1)) // GS
    RING = 4
    NG = -(-NG // RING) * RING
    NSLOT = NG * GS
    F_T, F_S, F_B, F_EA = 0, 1, 2, 3
    AUG = NA + 1
    STK = 6 * AUG
    RW = F_EA + STK // 2
    LEAD = G
    DVA = DV + 1
    AW = H * DVA
    PADG = 16
    assert (NSLOT // P) % PADG == 0 and STK % 2 == 0 and STK <= P
    TOP = 2
    CB = 5
    NCH = NB // CB
    NC = NB * TOP
    NT = (NC * P + NX * (P - 1)) // P
    TR = 3
    BR = 3 * NX
    HB = HID + DIM
    assert NCH * CB == NB and NT % TR == 0 and NT <= P and NX == 8

    kv_dram = nc.dram_tensor("kv_table", (N, KV), F32, kind="Internal").ap()
    rec_dram = nc.dram_tensor("sorted_edges", (NSLOT + LEAD, RW), F32, kind="Internal").ap()
    routed_dram = nc.dram_tensor("routed_rows", (NT * P, DIM), F32, kind="Internal").ap()
    results_dram = nc.dram_tensor("expert_results", (NT * P, DIM), F32, kind="Internal").ap()
    rec_groups = rec_dram[LEAD:LEAD + NSLOT, :].rearrange("(g p j) r -> g p (j r)", p=P, j=G)
    rec_before = rec_dram[0:NSLOT, :].rearrange("(g p j) r -> g p (j r)", p=P, j=G)
    B_S = (G - 1) * RW + F_S
    rec_fill = rec_dram[0:NSLOT, :].rearrange("(f p j) r -> f p (j r)", p=P, j=PADG)

    with ExitStack() as ctx:
        where = [ctx]

        def sb(name, shape, dt=F32):
            return where[0].enter_context(nc.sbuf_tensor(name, shape, dt))

        def sem(name):
            return ctx.enter_context(nc.semaphore(name))

        bank = [ctx.enter_context(nc.psum_tensor(f"bank{n}", [P, 512], F32)) for n in range(8)]

        ident = sb("ident", [P, P])
        identb = sb("identb", [P, P], BF16)
        iota = sb("iota", [P, P])
        upper = sb("upper", [P, P])
        ones = sb("ones", [P, P])
        zrows = sb("zrows", [P, DIM])
        blk_i = sb("blk_i", [1, NG], I32)
        xs = sb("xs", [P, NB, DIM])
        q_tab = sb("q_tab", [P, NB, PARTS, DH], BF16)
        acc = sb("acc", [P, NB * AW])
        Wrpe = sb("Wrpe", [STK, 2 * DH], BF16)
        W1s = sb("W1s", [P, KD, NX * HID])
        rstd = sb("rstd", [P, NB])
        std = sb("std", [P, NB])

        sort = ExitStack()
        where[0] = sort
        lower = sb("lower", [P, P])
        s_i = sb("s_i", [EP, EC], I32)
        t_i = sb("t_i", [EP, EC], I32)
        s_f = sb("s_f", [EP, EC])
        b_f = sb("b_f", [EP, EC])
        ea_raw = sb("ea_raw", [EP, EC * NA])
        hiA = sb("hiA", [EP, EC, NB], BF16)
        loB = [sb(f"loB{n}", [EP, TB, P], BF16) for n in range(2)]
        loBT = [sb(f"loBT{n}", [P, TB, P]) for n in range(2)]
        cnt = [sb(f"cnt{n}", [P, TB, NB]) for n in range(2)]
        picked = sb("picked", [EP, TB, NB])
        same = sb("same", [EP, TB, EP], BF16)
        within = sb("within", [EP, TB])
        prior = sb("prior", [EP, TB])
        pos = [sb(f"pos{n}", [EP, TB], I32) for n in range(2)]
        recb = [sb(f"recb{n}", [EP, TB, RW]) for n in range(2)]
        padrec = sb("padrec", [P, PADG, RW])
        tot = sb("tot", [P, NB])
        bsum = sb("bsum", [P, NB])
        ngrp_i = sb("ngrp_i", [P, NB], I32)
        ngrp = sb("ngrp", [P, NB])
        incl = sb("incl", [P, NB])
        excl = sb("excl", [P, NB])
        zrow = sb("zrow", [P, NB])
        gid = sb("gid", [1, NG])
        gblk = sb("gblk", [1, NG])
        Wqkv_s = sb("Wqkv_s", [P, KD, 2 * DH + DIM])
        bias = sb("bias", [P, 2 * DH + DIM])
        wraw = sb("wraw", [STK, 2 * DH])
        wpart = [sb(f"wpart{n}", [STK, 2 * DH], BF16) for n in range(PARTS)]
        wres = sb("wres", [STK, 2 * DH])
        wmask = sb("wmask", [STK, 4])
        eres = [sb(f"eres{n}", [EP, TB, NA]) for n in range(2)]
        qk32 = sb("qk32", [P, 2 * DH])
        qkres = sb("qkres", [P, 2 * DH])
        qkp = sb("qkp", [P, PARTS, 2 * DH], BF16)
        xl = sb("xl", [P, DIM])
        xlT = sb("xlT", [P, DIM])
        kvrow = sb("kvrow", [P, DIM])
        srcb = sb("srcb", [EP, EC, 2], BF16)
        xsum = sb("xsum", [P, NB])
        negmean = sb("negmean", [P, NB])
        xsq = sb("xsq", [P, NB])
        sort.close()

        attn = ExitStack()
        where[0] = attn
        rec = [sb(f"rec{n}", [P, G, RW]) for n in range(RING)]
        before = [sb(f"before{n}", [P, 1]) for n in range(RING)]
        kv = [sb(f"kv{n}", [P, G, KV]) for n in range(RING)]
        away = sb("away", [P, G, P])
        oh = [sb(f"oh{n}", [P, G, P], BF16) for n in range(2)]
        oh32 = [sb(f"ohw{n}", [P, G, P]) for n in range(RING)]
        new = [sb(f"new{n}", [P, G], BF16) for n in range(2)]
        ohT = [sb(f"ohT{n}", [P, GS], BF16) for n in range(2)]
        eaT = [sb(f"eaT{n}", [STK, GS], BF16) for n in range(2)]
        pen = [sb(f"pen{n}", [H, GS + 1]) for n in range(RING)]
        ke = sb("ke", [P, G, DH])
        prod = sb("prod", [P, G, DH])
        cc = [sb(f"cc{n}", [P, G, H]) for n in range(2)]
        fw = [sb(f"fw{n}", [H, GS]) for n in range(2)]
        segm = sb("segm", [H, GS])
        goes_on = sb("goes_on", [H, 1])
        dbuf = sb("dbuf", [H, P])
        dT = [sb(f"dT{n}", [P, H]) for n in range(RING)]
        diff = [sb(f"diff{n}", [P, G, H]) for n in range(RING)]
        wv = [sb(f"wv{n}", [P, G, H, DVA]) for n in range(2)]
        fac = [sb(f"fac{n}", [P, H]) for n in range(RING)]
        attn.close()

        ffn = ExitStack()
        where[0] = ffn
        W2s = sb("W2s", [P, MH, NX * DIM])
        gamT = sb("gamT", [P, KD])
        betT = sb("betT", [P, KD])
        Wr_s = sb("Wr_s", [P, KD, NX])
        br_s = sb("br_s", [P, NX])
        hbst = sb("hbst", [BR, HB], BF16)
        hn = sb("hn", [P, NB, DIM])
        w0 = sb("w0", [P, NB])
        w1 = sb("w1", [P, NB])
        slot = sb("slot", [P, NC], I32)
        sel = sb("sel", [BR, NT])
        texp_i = sb("texp_i", [1, NT], I32)
        selw = [sb(f"selw{n}", [BR, P], BF16) for n in range(TR)]
        routing = ExitStack()
        where[0] = routing
        hb = sb("hb", [BR, HB])
        hbres = [sb(f"hbres{n}", [BR, HB]) for n in range(2)]
        hbpart = [sb(f"hbpart{n}", [BR, HB], BF16) for n in range(PARTS)]
        row = sb("row", [BR, 1])
        rowm = sb("rowm", [BR, 4])
        rowexp = sb("rowexp", [BR, 1])
        den = sb("den", [P, NB * H])
        att = sb("att", [P, CB * DIM])
        bst = sb("bst", [P, CB, 6])
        cmv = sb("cmv", [P, CB, 2])
        cstd = sb("cstd", [P, CB])
        crstd = sb("crstd", [P, CB])
        xnT = sb("xnT", [P, KD, CB * P])
        lg = sb("lg", [P, CB, NX])
        top = sb("top", [P, CB, 8])
        topi = sb("topi", [P, CB, 8], U32)
        tops = sb("tops", [P, NB, TOP])
        topf = sb("topf", [P, NC])
        e1 = sb("e1", [P, NB])
        hit = sb("hit", [P, NX, NC])
        inner1 = sb("inner1", [P, NX, NC])
        upto = sb("upto", [P, NX, NC])
        place = sb("place", [P, NX, NC])
        place2 = sb("place2", [P, NX, NC])
        slotf = sb("slotf", [P, NC])
        tiles_i = sb("tiles_i", [P, NX], I32)
        tiles_f = sb("tiles_f", [P, NX])
        tzero = sb("tzero", [P, NX])
        tincl = sb("tincl", [P, NX])
        tbase = sb("tbase", [P, NX])
        tle = sb("tle", [BR, NT, NX])
        texp = sb("texp", [BR, NT])
        routing.close()
        where[0] = ffn
        xt = [sb(f"xt{n}", [P, DIM]) for n in range(TR)]
        xtT = [sb(f"xtT{n}", [P, KD, P]) for n in range(TR)]
        hid = [sb(f"hid{n}", [P, HID]) for n in range(TR)]
        hidT = [sb(f"hidT{n}", [P, HID]) for n in range(TR)]
        yt = [sb(f"yt{n}", [P, DIM]) for n in range(TR)]
        yg = [sb(f"yg{n}", [P, TOP, DIM]) for n in range(CB)]
        ffn.close()

        names = """in_src in_x in_ea in_w in_small consts identb_ready a_ready onehot hist tot_sb base_mm chain
            base_ready blk_ready pad_ready pad_done lnchain normed xT_done xT_copied qkv_done table_ready
            kv_stored moments loB_ready loB_used sbc_done loBT_ready cnt_ready lk_done within_ready
            pos_chain pos_ready recb_ready scat0 scat1 rec_ready0 rec_ready1 rec_ready2 rec_ready3 kv_ready0
            kv_ready1 kv_ready2 kv_ready3 away_ready oh_ready new_ready tr_oh tr_ea tr_s oh32_ready
            oht_copied eat_copied pen_ready wstk recb_const e1_ready e2_ready eres_ready e3_ready qk_chain
            qkp1 qkp2 qkp3 qtab_ready qk_done ke_ready prod_done c_ready ct_done fw_ready sm_ready
            dbuf_ready smt_done diff_ready dT_ready f_done fac_ready w_exp w_ready seg_done acc_scaled
            acc_done init_ready ex_w ex_small hb_raw rowc residual den prep prep_act norm_ready hnT_done
            xnT_ready logit_done router route route_pe route_act slot_ready filled zrows_ready sent
            xt_ready0 xt_ready1 xt_ready2 tx_done xt_copied sel_ready h_done gelu_done th_done hT_copied
            y_done y_copied stored0 stored1 stored2 yg_ready0 yg_ready1 yg_ready2 yg_ready3 yg_ready4
            combined out_done""".split()
        S = {n: sem(n) for n in names}

        ROUTE = 34
        PREP, HALF = 6 * CB + 3, 2 * CB + 1
        block = ctx.enter_context(nc.Block())

        def batches(engine, body):
            body(0, 0)
            body(1, 1)
            with engine.Fori(2, NBATCH - 2, 2) as i:
                body(i, 0)
                body(i + 1, 1)
            body(NBATCH - 2, 0)
            body(NBATCH - 1, 1)

        def groups(engine, body):
            for k in range(RING):
                body(k, k, 0)
            with engine.Fori(1, NG // RING - 1) as i:
                for k in range(RING):
                    body(RING * i + k, k, i)
            for k in range(RING):
                body(NG - RING + k, k, NG // RING - 1)

        def tiles(engine, body):
            for k in range(TR):
                body(k, k, 0)
            with engine.Fori(1, NT // TR - 1) as i:
                for k in range(TR):
                    body(TR * i + k, k, i)
            for k in range(TR):
                body(NT - TR + k, k, NT // TR - 1)

        def after_sort(engine):
            engine.wait_ge(S["scat0"], 8 * TB * NBATCH)
            engine.wait_ge(S["scat1"], 8 * TB * NBATCH)
            engine.wait_ge(S["kv_stored"], 32 * NB)
            engine.wait_ge(S["wstk"], 2 * PARTS + 5)
            engine.wait_ge(S["qtab_ready"], NB)
            engine.wait_ge(S["blk_ready"], 1)
            engine.wait_ge(S["pos_ready"], NBATCH)

        @block.sync
        def _(sp):
            sp.dma_start(s_i[:, :], src.rearrange("(p c) -> p c", c=EC)).then_inc(S["in_src"], 16)
            sp.dma_start(t_i[:, :], dst.rearrange("(p c) -> p c", c=EC)).then_inc(S["in_ea"], 16)
            sp.dma_start(xs[:, 0:NB - 1, :], x[0:(NB - 1) * P, :].rearrange("(b p) d -> p b d", p=P)).then_inc(S["in_x"], 16)
            sp.wait_ge(S["init_ready"], 2)
            sp.dma_start(xs[0:TAIL, NB - 1, :], x[(NB - 1) * P:N, :]).then_inc(S["in_x"], 16)
            sp.dma_start(Wqkv_s[:, :, :], Wqkv.rearrange("(k p) n -> p k n", p=P)).then_inc(S["in_w"], 16)
            sp.dma_start(bias[:, :], bqkv.partition_broadcast(P)).then_inc(S["in_w"], 16)
            sp.dma_start(ea_raw[:, :], edge_attr.rearrange("(p c) a -> p (c a)", c=EC)).then_inc(S["in_ea"], 16)
            for n in range(STK // AUG):
                r = n * AUG
                sp.dma_start(wraw[r:r + NA, 0:DH], Wq_rpe).then_inc(S["in_small"], 16)
                sp.dma_start(wraw[r:r + NA, DH:2 * DH], Wk_rpe).then_inc(S["in_small"], 16)
                sp.dma_start(wraw[r + NA:r + AUG, 0:DH], bq_rpe.rearrange("(a n) -> a n", a=1)).then_inc(S["in_small"], 16)
                sp.dma_start(wraw[r + NA:r + AUG, DH:2 * DH], bk_rpe.rearrange("(a n) -> a n", a=1)).then_inc(S["in_small"], 16)
            sp.wait_ge(S["pad_ready"], 4)
            for f in range(NSLOT // P // PADG):
                sp.dma_start(rec_fill[f], padrec[:, :, :].rearrange("p j r -> p (j r)")).then_inc(S["pad_done"], 16)
            sp.dma_start(rec_dram[NSLOT:NSLOT + LEAD, :], padrec[0:LEAD, 0, :]).then_inc(S["pad_done"], 16)
            for k in range(KD):
                sp.dma_start(W1s[:, k, :].rearrange("p (e h) -> p e h", h=HID),
                             W1[:, k * P:(k + 1) * P, :].rearrange("e p h -> p e h")).then_inc(S["ex_w"], 16)
            with sp.Fori(0, NB - 1) as t:
                sp.wait_ge(S["qkp3"], t + 1)
                sp.dma_start(kv_dram[bass.ds(t * P, P), KW:KV], kvrow[:, :]).then_inc(S["kv_stored"], 16)
                sp.dma_start(kv_dram[bass.ds(t * P, P), 0:KW].bitcast(BF16).rearrange("n (a c) -> n a c", c=DH),
                             qkp[:, :, DH:2 * DH]).then_inc(S["kv_stored"], 16)
            sp.wait_ge(S["qkp3"], NB)
            sp.dma_start(kv_dram[(NB - 1) * P:N, KW:KV], kvrow[0:TAIL, :]).then_inc(S["kv_stored"], 16)
            sp.dma_start(kv_dram[(NB - 1) * P:N, 0:KW].bitcast(BF16).rearrange("n (a c) -> n a c", c=DH),
                         qkp[0:TAIL, :, DH:2 * DH]).then_inc(S["kv_stored"], 16)

            after_sort(sp)
            def load_records(g, k, i):
                ge(sp, S["new_ready"], g - RING + 1)
                ge(sp, S["oh_ready"], g - RING + 1)
                ge(sp, S["tr_ea"], g - RING + 1)
                ge(sp, S[f"kv_ready{k}"], i * 16 * G)
                for tile, source, a, b in ((rec[k][:, :, :].rearrange("p j r -> p (j r)"), rec_groups, 0, G * RW),
                                           (before[k][:, :], rec_before, B_S, B_S + 1)):
                    one = source[g][:, a:b] if isinstance(g, int) else source[bass.ds(g, 1)].rearrange("g p r -> (g p) r")[:, a:b]
                    sp.dma_start(tile, one, allow_slow_non_contiguous=True).then_inc(S[f"rec_ready{k}"], 16)

            groups(sp, load_records)

            sp.wait_ge(S["acc_done"], NG)
            for n in range(PARTS):
                sp.dma_start(hb[n * NX:(n + 1) * NX, 0:HID], b1).then_inc(S["hb_raw"], 16)
                sp.dma_start(hb[n * NX:(n + 1) * NX, HID:HB], b2).then_inc(S["hb_raw"], 16)
            sp.dma_start(gamT[:, :], gamma.rearrange("(k p) -> p k", p=P), allow_slow_non_contiguous=True).then_inc(S["ex_small"], 16)
            sp.dma_start(betT[:, :], beta.rearrange("(k p) -> p k", p=P), allow_slow_non_contiguous=True).then_inc(S["ex_small"], 16)
            sp.dma_start(Wr_s[:, :, :], Wr.rearrange("(k p) e -> p k e", p=P)).then_inc(S["ex_small"], 16)
            sp.dma_start(br_s[:, :], br.partition_broadcast(P)).then_inc(S["ex_small"], 16)
            for m in range(MH):
                sp.dma_start(W2s[:, m, :].rearrange("p (e d) -> p e d", d=DIM),
                             W2[:, m * P:(m + 1) * P, :].rearrange("e p d -> p e d")).then_inc(S["ex_w"], 16)

            sp.wait_ge(S["zrows_ready"], 1)
            sp.dma_start(routed_dram.rearrange("(t p) d -> p t d", p=P), zrows[:, None, :].to_broadcast([P, NT, DIM]))\
                .then_inc(S["filled"], 16)

            sp.wait_ge(S["sent"], 16 * NC)
            sp.wait_ge(S["route"], ROUTE)

            def load_tile(t, k, i):
                ge(sp, S["tx_done"], t - TR + 1)
                sp.dma_start(xt[k][:, :], routed_dram[bass.ds(t * P, P), :]).then_inc(S[f"xt_ready{k}"], 16)

            def store_tile(t, k):
                sp.wait_ge(S["y_copied"], t + 1)
                sp.dma_start(results_dram[bass.ds(t * P, P), :], yt[k][:, :]).then_inc(S[f"stored{k}"], 16)

            def load_store(t, k, i):
                load_tile(t, k, i)
                if not isinstance(t, int) or t >= TR:
                    store_tile(t - TR, k)

            tiles(sp, load_store)
            for k in range(TR):
                store_tile(NT - TR + k, k)

            for c in range(NCH):
                sp.wait_ge(S["combined"], TOP * CB * (c + 1))
                first = c * CB
                blocks = CB if c + 1 < NCH else CB - 1
                sp.dma_start(out[first * P:(first + blocks) * P, :].rearrange("(b p) d -> p b d", p=P),
                             xs[:, first:first + blocks, :]).then_inc(S["out_done"], 16)
            sp.dma_start(out[(NB - 1) * P:N, :], xs[0:TAIL, NB - 1, :]).then_inc(S["out_done"], 16)
            sp.wait_ge(S["out_done"], 16 * (NCH + 1))

        @block.gpsimd
        def _(pool):
            batch_turn, group_turn = pool.alloc_register("batch_turn"), pool.alloc_register("group_turn")
            pool.reg_mov(batch_turn, 3)
            pool.reg_mov(group_turn, 1)
            nc.gpsimd.iota(iota[:, :], [[1, P]], base=0, channel_multiplier=0,
                           allow_small_or_imprecise_dtypes=True).then_inc(S["consts"], 1)
            nc.gpsimd.memset(ident[:, :], 0.0).then_inc(S["consts"], 1)
            nc.gpsimd.memset(lower[:, :], 1.0).then_inc(S["consts"], 1)
            nc.gpsimd.memset(upper[:, :], 1.0).then_inc(S["consts"], 1)
            nc.gpsimd.memset(ones[:, :], 1.0).then_inc(S["consts"], 1)
            nc.gpsimd.iota(gid[:, :], [[1, NG]], base=0, channel_multiplier=0,
                           allow_small_or_imprecise_dtypes=True).then_inc(S["consts"], 1)
            pool.wait_ge(S["consts"], 6)
            nc.gpsimd.affine_select(out=ident[:, :], in_=ident[:, :], compare_op=ALU.not_equal, fill=1.0, base=0,
                                    pattern=[[-1, P]], channel_multiplier=1).then_inc(S["consts"], 1)
            nc.gpsimd.affine_select(out=lower[:, :], in_=lower[:, :], compare_op=ALU.is_gt, fill=0.0, base=0,
                                    pattern=[[-1, P]], channel_multiplier=1).then_inc(S["consts"], 1)
            nc.gpsimd.affine_select(out=upper[:, :], in_=upper[:, :], compare_op=ALU.is_gt, fill=0.0, base=0,
                                    pattern=[[1, P]], channel_multiplier=-1).then_inc(S["consts"], 1)
            nc.gpsimd.memset(zrows[:, :], 0.0).then_inc(S["zrows_ready"], 1)
            nc.gpsimd.memset(padrec[:, :, :], 0.0).then_inc(S["pad_ready"], 1)
            pool.wait_ge(S["pad_ready"], 1)
            nc.gpsimd.memset(padrec[:, :, F_S:F_S + 1], -1.0).then_inc(S["pad_ready"], 1)
            nc.gpsimd.memset(padrec[:, :, F_B:F_B + 1], 1.0).then_inc(S["pad_ready"], 2)

            nc.gpsimd.memset(recb[0][:, :, :], 0.0).then_inc(S["recb_const"], 1)
            nc.gpsimd.memset(recb[1][:, :, :], 0.0).then_inc(S["recb_const"], 1)
            nc.gpsimd.memset(wmask[:, :], 1.0).then_inc(S["recb_const"], 1)
            pool.wait_ge(S["recb_const"], 3)
            for n in range(2):
                parts = recb[n][:, :, F_EA:RW].bitcast(BF16).rearrange("p j (b a) -> p j b a", a=AUG)
                nc.gpsimd.memset(parts[:, :, 0:4:3, NA:AUG], 1.0).then_inc(S["recb_const"], 1)
                nc.gpsimd.memset(parts[:, :, 5:6, NA:AUG], 1.0).then_inc(S["recb_const"], 1)
            for n, first in enumerate((3 * AUG, 5 * AUG)):
                nc.gpsimd.affine_select(out=wmask[:, n:n + 1], in_=wmask[:, n:n + 1], compare_op=ALU.is_ge, fill=0.0,
                                        base=-first, pattern=[[0, 1]], channel_multiplier=1).then_inc(S["recb_const"], 1)

            pool.wait_ge(S["pad_done"], 16 * (NSLOT // P // PADG + 1))

            def scatter(i, k):
                if isinstance(i, int):
                    pool.wait_ge(S["pos_ready"], i + 1)
                    pool.wait_ge(S["recb_ready"], i + 1)
                    pool.wait_ge(S["e3_ready"], i + 1)
                else:
                    wait_turn(pool, batch_turn, [S["pos_ready"], S["recb_ready"], S["e3_ready"]])
                for j in range(TB):
                    nc.gpsimd.indirect_dma_start(
                        rec_dram, bass.IndirectOffsetOnAxis(pos[k][:, j:j + 1], 0),
                        recb[k][:, j, :], None).then_inc(S[f"scat{k}"], 16)

            batches(pool, scatter)

            after_sort(pool)

            def gather(g, k, i):
                if isinstance(g, int):
                    pool.wait_ge(S[f"rec_ready{k}"], 32 * i + 32)
                    ge(pool, S["qk_done"], g - RING + 1)
                    ge(pool, S["w_ready"], g - RING + 1)
                else:
                    wait_turn(pool, group_turn, [S["qk_done"], S["w_ready"]], [(S[f"rec_ready{k}"], 32 * i + 32)])
                for j in range(G):
                    nc.gpsimd.indirect_dma_start(
                        kv[k][:, j, :], None, kv_dram,
                        bass.IndirectOffsetOnAxis(rec[k][:, j, F_T:F_T + 1].bitcast(I32), 0)).then_inc(S[f"kv_ready{k}"], 16)

            groups(pool, gather)

            pool.wait_ge(S["acc_done"], NG)
            nc.gpsimd.iota(row[:, :], [[0, 1]], base=0, channel_multiplier=1,
                           allow_small_or_imprecise_dtypes=True).then_inc(S["rowc"], 1)
            nc.gpsimd.memset(rowm[:, :], 1.0).then_inc(S["rowc"], 1)
            nc.gpsimd.memset(tzero[:, :], 0.0).then_inc(S["rowc"], 1)
            nc.gpsimd.memset(inner1[:, :, :], 1.0).then_inc(S["rowc"], 1)
            pool.wait_ge(S["rowc"], 4)
            nc.gpsimd.memset(inner1[:, :, 0:1], 0.0).then_inc(S["rowc"], 1)
            for n in range(2):
                nc.gpsimd.affine_select(out=rowm[:, n:n + 1], in_=rowm[:, n:n + 1], compare_op=ALU.is_ge, fill=0.0,
                                        base=-(n + 1) * NX, pattern=[[0, 1]], channel_multiplier=1).then_inc(S["rowc"], 1)

            pool.wait_ge(S["den"], 2)
            with pool.Fori(0, NCH) as c:
                heads = acc[:, bass.ds(c * (CB * AW), CB * AW)].rearrange("p (q d) -> p q d", d=DVA)
                xc = xs[:, bass.ds(c * CB, CB), :].rearrange("p q d -> p (q d)")
                nc.gpsimd.tensor_tensor(att[:, :].rearrange("p (q d) -> p q d", d=DV), heads[:, :, 0:DV],
                                        den[:, bass.ds(c * (CB * H), CB * H)].unsqueeze(2).to_broadcast([P, CB * H, DV]), ALU.mult)\
                    .then_inc(S["residual"], 1)
                pool.wait_ge(S["residual"], 2 * c + 1)
                nc.gpsimd.tensor_tensor(xc, xc, att[:, :], ALU.add).then_inc(S["residual"], 1)
                pool.wait_ge(S["residual"], 2 * c + 2)

            pool.wait_ge(S["filled"], 16)
            pool.wait_ge(S["slot_ready"], 1)
            for c in range(NC):
                nc.gpsimd.indirect_dma_start(routed_dram, bass.IndirectOffsetOnAxis(slot[:, c:c + 1], 0),
                                             hn[:, c // TOP, :], None).then_inc(S["sent"], 16)

            for k in range(TR):
                pool.wait_ge(S[f"stored{k}"], 16 * (NT // TR))
            for b in range(NB):
                ge(pool, S["combined"], TOP * (b - CB + 1))
                for n in range(TOP):
                    c = b * TOP + n
                    nc.gpsimd.indirect_dma_start(yg[b % CB][:, n, :], None, results_dram,
                                                 bass.IndirectOffsetOnAxis(slot[:, c:c + 1], 0)).then_inc(S[f"yg_ready{b % CB}"], 16)

        @block.vector
        def _(dve):
            V = nc.vector
            prep_turn, router_turn = dve.alloc_register("prep_turn"), dve.alloc_register("router_turn")
            dve.reg_mov(prep_turn, PREP + 1)
            dve.reg_mov(router_turn, 1)
            V.memset(acc[:, :], 0.0).then_inc(S["init_ready"], 1)
            V.memset(xs[:, NB - 1, :], 0.0).then_inc(S["init_ready"], 1)
            V.memset(zrow[:, :], 0.0).then_inc(S["init_ready"], 1)

            dve.wait_ge(S["in_src"], 16)
            V.tensor_copy(s_f[:, :], s_i[:, :]).then_inc(S["chain"], 1)
            V.tensor_scalar(loBT[0][0:EP, 0:4, 0:100].bitcast(I32), s_i[:, :].rearrange("p (a b) -> p a b", a=4), P - 1, None,
                            ALU.bitwise_and).then_inc(S["chain"], 1)
            V.tensor_scalar(loBT[1][0:EP, 0:4, 0:100].bitcast(I32), s_i[:, :].rearrange("p (a b) -> p a b", a=4), SHIFT, None,
                            ALU.logical_shift_right).then_inc(S["chain"], 1)
            dve.wait_ge(S["chain"], 3)
            V.tensor_copy(b_f[:, :].rearrange("p (a b) -> p a b", a=4), loBT[0][0:EP, 0:4, 0:100].bitcast(I32)).then_inc(S["chain"], 1)
            dve.wait_ge(S["consts"], 9)
            V.tensor_copy(identb[:, :], ident[:, :]).then_inc(S["identb_ready"], 1)
            a_cols = loBT[0][0:EP, 4:8, 0:100]
            V.tensor_copy(a_cols, loBT[1][0:EP, 0:4, 0:100].bitcast(I32)).then_inc(S["chain"], 1)
            dve.wait_ge(S["chain"], 5)
            V.tensor_copy(srcb[:, :, 0], b_f[:, :])
            V.tensor_tensor(srcb[:, :, 1], s_f[:, :], b_f[:, :], ALU.subtract)
            for a in range(4):
                w = EC // 4
                V.tensor_tensor(hiA[:, a * w:(a + 1) * w, :], iota[0:EP, None, 0:NB].to_broadcast([EP, w, NB]),
                                loBT[0][0:EP, 4 + a, 0:100, None].to_broadcast([EP, w, NB]), ALU.is_equal).then_inc(S["a_ready"], 1)

            def onehot(i, k):
                first = i * TB
                cols = b_f[:, first:first + TB] if isinstance(i, int) else b_f[:, bass.ds(first, TB)]
                return V.tensor_tensor(loB[k][:, :, :], iota[0:EP, None, :].to_broadcast([EP, TB, P]),
                                       cols.unsqueeze(2).to_broadcast([EP, TB, P]), ALU.is_equal)

            def pass1(i, k):
                ge(dve, S["hist"], i - 1)
                onehot(i, k).then_inc(S["onehot"], 1)

            batches(dve, pass1)

            dve.wait_ge(S["hist"], NBATCH)
            V.tensor_copy(tot[:, :], bank[7][:, 0:NB]).then_inc(S["tot_sb"], 1)
            dve.wait_ge(S["base_mm"], 1)
            V.tensor_scalar(bsum[:, :], bank[7][:, 64:64 + NB], float(GS - 1), None, ALU.add).then_inc(S["chain"], 1)
            dve.wait_ge(S["chain"], 6)
            V.tensor_copy(ngrp_i[:, :], bsum[:, :]).then_inc(S["chain"], 1)
            dve.wait_ge(S["chain"], 7)
            V.tensor_scalar(ngrp_i[:, :], ngrp_i[:, :], GSHIFT, None, ALU.logical_shift_right).then_inc(S["chain"], 1)
            dve.wait_ge(S["chain"], 8)
            V.tensor_copy(ngrp[:, :], ngrp_i[:, :]).then_inc(S["chain"], 1)
            dve.wait_ge(S["chain"], 9)
            V.tensor_tensor_scan(incl[:, :], ngrp[:, :], zrow[:, :], 0.0, ALU.add, ALU.add).then_inc(S["chain"], 1)
            dve.wait_ge(S["chain"], 10)
            V.tensor_tensor(excl[:, :], incl[:, :], ngrp[:, :], ALU.subtract).then_inc(S["chain"], 1)
            dve.wait_ge(S["chain"], 11)
            V.scalar_tensor_tensor(tot[:, :], excl[:, :], float(GS), bank[7][:, 128:128 + NB], ALU.mult, ALU.add)\
                .then_inc(S["base_ready"], 1)
            dve.wait_ge(S["base_ready"], 1)
            V.tensor_scalar(cnt[0][:, 0, :], tot[:, :], float(LEAD), None, ALU.add).then_inc(S["base_ready"], 1)
            dve.wait_ge(S["moments"], 2 * NB + 1)
            V.tensor_scalar(std[:, :], xsq[:, :], 1.0 / DIM, LN_EPS, ALU.mult, ALU.add).then_inc(S["lnchain"], 1)
            dve.wait_ge(S["lnchain"], 2)
            V.reciprocal(rstd[:, :], std[:, :]).then_inc(S["lnchain"], 1)
            dve.wait_ge(S["in_w"], 32)
            V.tensor_scalar(bias[:, 0:DH], bias[:, 0:DH], SCALE, None, ALU.mult).then_inc(S["lnchain"], 1)
            V.tensor_scalar(Wqkv_s[:, :, 0:DH], Wqkv_s[:, :, 0:DH], SCALE, None, ALU.mult).then_inc(S["lnchain"], 1)
            dve.wait_ge(S["lnchain"], 5)

            def normalize(t):
                ge(dve, S["xT_done"], t)
                V.tensor_scalar(xl[:, :], xs[:, bass.ds(t, 1), :].rearrange("p a d -> p (a d)"),
                                negmean[:, bass.ds(t, 1)], rstd[:, bass.ds(t, 1)],
                                ALU.add, ALU.mult).then_inc(S["normed"], 1)

            def projected(t):
                dve.wait_ge(S["qkv_done"], t + 1)
                ge(dve, S["kv_stored"], 32 * t)
                V.tensor_tensor(kvrow[:, :], bank[7][:, 2 * DH:2 * DH + DIM], bias[:, 2 * DH:2 * DH + DIM], ALU.add)
                V.tensor_tensor(qk32[:, :], bank[7][:, 0:2 * DH], bias[:, 0:2 * DH], ALU.add).then_inc(S["table_ready"], 1)

            def second_rest(t):
                dve.wait_ge(S["qkp1"], t + 1)
                V.tensor_tensor(qkres[:, :], qk32[:, :], qkp[:, 0, :], ALU.subtract).then_inc(S["qk_chain"], 1)

            def third_rest(t):
                dve.wait_ge(S["qkp2"], t + 1)
                V.tensor_tensor(qkp[:, 2, :], qkres[:, :], qkp[:, 1, :], ALU.subtract).then_inc(S["qkp3"], 1)

            def lo_onehot(i, k):
                ge(dve, S["loB_used"], i - 1)
                onehot(i, k).then_inc(S["loB_ready"], 1)

            def counts(i, k):
                dve.wait_ge(S["loB_used"], i + 1)
                ge(dve, S["lk_done"], i)
                for j in range(TB):
                    nxt = cnt[k][:, j + 1, :] if j + 1 < TB else cnt[1 - k][:, 0, :]
                    V.tensor_tensor(nxt, cnt[k][:, j, :], bank[k][:, j * NB:(j + 1) * NB], ALU.add).then_inc(S["cnt_ready"], 1)
                    dve.wait_ge(S["cnt_ready"], i * TB + (j + 1))

            def after_first_part(i, k):
                raw = ea_raw[:, bass.ds(i * (TB * NA), TB * NA)].rearrange("p (j a) -> p j a", a=NA)
                parts = recb[k][:, :, F_EA:RW].bitcast(BF16).rearrange("p j (b a) -> p j b a", a=AUG)
                dve.wait_ge(S["e1_ready"], i + 1)
                V.tensor_tensor(eres[k][:, :, :], raw, parts[:, :, 0, 0:NA], ALU.subtract).then_inc(S["eres_ready"], 1)

            def third_part(i, k):
                parts = recb[k][:, :, F_EA:RW].bitcast(BF16).rearrange("p j (b a) -> p j b a", a=AUG)
                dve.wait_ge(S["e2_ready"], i + 1)
                V.tensor_tensor(parts[:, :, 2, 0:NA], eres[k][:, :, :], parts[:, :, 1, 0:NA], ALU.subtract)\
                    .then_inc(S["e3_ready"], 1)

            def slots(i, k):
                dve.wait_ge(S["sbc_done"], i + 1)
                for j in range(TB):
                    col = s_f[:, i * TB + j:i * TB + j + 1] if isinstance(i, int) else s_f[:, bass.ds(i * TB + j, 1)]
                    V.scalar_tensor_tensor(same[:, j, :], bank[4 + j // 4][0:EP, (j % 4) * P:(j % 4) * P + EP], col,
                                           lower[0:EP, 0:EP], ALU.is_equal, ALU.mult,
                                           accum_out=within[:, j:j + 1]).then_inc(S["within_ready"], 1)
                dve.wait_ge(S["lk_done"], i + 1)
                V.tensor_tensor(picked[:, :, :], bank[6][0:EP, 0:TB * NB].rearrange("p (j a) -> p j a", a=NB),
                                hiA[:, bass.ds(i * TB, TB), :], ALU.mult).then_inc(S["pos_chain"], 1)
                dve.wait_ge(S["pos_chain"], 2 * i + 1)
                V.tensor_reduce(prior[:, :], picked[:, :, :], AX_X, ALU.add).then_inc(S["pos_chain"], 1)
                dve.wait_ge(S["pos_chain"], 2 * i + 2)
                dve.wait_ge(S["within_ready"], TB * (i + 1))
                ge(dve, S[f"scat{k}"], (i - k) * (8 * TB))
                V.tensor_tensor(pos[k][:, :], prior[:, :], within[:, :], ALU.add).then_inc(S["pos_ready"], 1)

            def pair(i):
                more = not isinstance(i, int) or i + 1 < NB
                after_first_part(2 * i, 0)
                lo_onehot(2 * i + 1, 1)
                third_part(2 * i, 0)
                if not isinstance(i, int) or i:
                    third_rest(i - 1)
                slots(2 * i, 0)
                counts(2 * i + 1, 1)
                projected(i)
                after_first_part(2 * i + 1, 1)
                if more:
                    lo_onehot(2 * i + 2, 0)
                third_part(2 * i + 1, 1)
                slots(2 * i + 1, 1)
                if more:
                    counts(2 * i + 2, 0)
                second_rest(i)
                if more:
                    normalize(i + 1)

            normalize(0)
            lo_onehot(0, 0)
            counts(0, 0)
            pair(0)
            with dve.Fori(1, NB - 1) as i:
                pair(i)
            pair(NB - 1)
            third_rest(NB - 1)

            gle = hiA[0:1, :, :].rearrange("p a n -> p (a n)")[:, 0:NG * NB].rearrange("p (g b) -> p g b", b=NB)
            V.tensor_tensor(gle, incl[0:1, None, :].to_broadcast([1, NG, NB]), gid[:, :, None].to_broadcast([1, NG, NB]), ALU.is_le).then_inc(S["chain"], 1)
            dve.wait_ge(S["chain"], 12)
            V.tensor_reduce(gblk[:, :], gle, AX_X, ALU.add).then_inc(S["chain"], 1)
            dve.wait_ge(S["chain"], 13)
            V.tensor_scalar(blk_i[:, :], gblk[:, :], float(NB - 1), None, ALU.min).then_inc(S["blk_ready"], 1)

            dve.wait_ge(S["in_small"], 64 * (STK // AUG))
            dve.wait_ge(S["recb_const"], 9)
            for n in range(PARTS):
                left = wraw if n == 0 else wres
                V.tensor_copy(wpart[n][:, :], left[:, :]).then_inc(S["wstk"], 1)
                dve.wait_ge(S["wstk"], 2 * n + 1)
                V.tensor_tensor(wres[:, :], left[:, :], wpart[n][:, :], ALU.subtract).then_inc(S["wstk"], 1)
                dve.wait_ge(S["wstk"], 2 * n + 2)
            V.tensor_scalar(wmask[:, 2:3], wmask[:, 0:1], -1.0, 1.0, ALU.mult, ALU.add).then_inc(S["wstk"], 1)
            V.tensor_tensor(wmask[:, 3:4], wmask[:, 0:1], wmask[:, 1:2], ALU.subtract).then_inc(S["wstk"], 1)
            dve.wait_ge(S["wstk"], 2 * PARTS + 2)
            V.tensor_scalar(wres[:, :], wpart[0][:, :], wmask[:, 2:3], None, ALU.mult).then_inc(S["wstk"], 1)
            dve.wait_ge(S["wstk"], 2 * PARTS + 3)
            V.scalar_tensor_tensor(wraw[:, :], wpart[1][:, :], wmask[:, 3:4], wres[:, :], ALU.mult, ALU.add).then_inc(S["wstk"], 1)
            dve.wait_ge(S["wstk"], 2 * PARTS + 4)
            V.scalar_tensor_tensor(Wrpe[:, :], wpart[2][:, :], wmask[:, 1:2], wraw[:, :], ALU.mult, ALU.add).then_inc(S["wstk"], 1)

            after_sort(dve)
            for n in range(RING):
                V.memset(pen[n][:, GS:GS + 1], 0.0)
            V.memset(dbuf[:, :], 0.0).then_inc(S["init_ready"], 1)
            dve.wait_ge(S["init_ready"], 4)

            def starts(g, k, i):
                dve.wait_ge(S[f"rec_ready{k}"], 32 * i + 32)
                ge(dve, S["tr_s"], g - 1)
                V.tensor_tensor(new[k % 2][:, 1:G], rec[k][:, 1:G, F_S], rec[k][:, 0:G - 1, F_S], ALU.not_equal)
                V.tensor_tensor(new[k % 2][:, 0:1], rec[k][:, 0, F_S:F_S + 1], before[k][:, :], ALU.not_equal).then_inc(S["new_ready"], 1)

            def products(g, k):
                dve.wait_ge(S["ke_ready"], g + 1)
                for a in range(2):
                    V.tensor_tensor(prod[:, 2 * a:2 * a + 2, :],
                                    bank[3 + a][:, :].rearrange("p (j c) -> p j c", c=2 * DH)[:, :, 0:DH],
                                    ke[:, 2 * a:2 * a + 2, :], ALU.mult).then_inc(S["prod_done"], 1)

            def scores(g, k):
                dve.wait_ge(S["prod_done"], 2 * g + 2)
                V.tensor_reduce(cc[k % 2][:, :, :].rearrange("p j h -> p (j h)"),
                                prod[:, :, :].rearrange("p j (h d) -> p (j h) d", d=D), AX_X, ALU.add).then_inc(S["c_ready"], 1)

            def maxima(g, k, i):
                dve.wait_ge(S["pen_ready"], g + 1)
                dve.wait_ge(S["ct_done"], g + 1)
                first = isinstance(g, int) and g == 0
                ahead = not isinstance(g, int) or g + 3 < NG
                before_it = fw[(k - 1) % 2][:, GS - 1:GS]
                V.tensor_tensor_scan(fw[k % 2][:, :], pen[k][:, 0:GS], bank[5][0:H, :],
                                     LOW if first else before_it, ALU.add, ALU.max).then_inc(S["fw_ready"], 1)
                if ahead:
                    starts(g + 3, (k + 3) % RING, i + (k + 3) // RING)
                V.tensor_scalar(goes_on[:, :], pen[k][:, 0:1], 0.0, None, ALU.is_equal)
                dve.wait_ge(S["fw_ready"], g + 1)
                ge(dve, S["smt_done"], g)
                V.tensor_tensor_scan(segm[:, GS - 1::-1], pen[k][:, GS:0:-1], fw[k % 2][:, GS - 1::-1],
                                     LOW, ALU.add, ALU.max).then_inc(S["sm_ready"], 1)
                if not first:
                    dve.wait_ge(S["sm_ready"], g + 1)
                    V.scalar_tensor_tensor(dbuf[:, 0:1], segm[:, 0:1], before_it, goes_on[:, :], ALU.subtract, ALU.mult)\
                        .then_inc(S["dbuf_ready"], 1)

            def shifts(g, k):
                dve.wait_ge(S["smt_done"], g + 1)
                V.tensor_tensor(diff[k][:, :, :].rearrange("p j h -> p (j h)"), cc[k % 2][:, :, :].rearrange("p j h -> p (j h)"),
                                bank[6][:, 0:G * H], ALU.subtract).then_inc(S["diff_ready"], 1)
                V.tensor_copy(dT[k][:, :], bank[6][:, G * H:G * H + H]).then_inc(S["dT_ready"], 1)

            def weighted(g, k):
                dve.wait_ge(S["w_exp"], g + 1)
                V.tensor_tensor(wv[k % 2][:, :, :, 0:DV],
                                kv[k][:, :, KW:KV].rearrange("p j (h d) -> p j h d", d=DV),
                                wv[k % 2][:, :, :, DV:DVA].to_broadcast([P, G, H, DV]), ALU.mult).then_inc(S["w_ready"], 1)

            def shrink(g, k):
                here = dve.value_load(blk_i[0:1, bass.ds(g, 1)], min_val=0, max_val=NB - 1)
                mine = acc[:, bass.ds(here * AW, AW)]
                dve.wait_ge(S["fac_ready"], g + 1)
                ge(dve, S["acc_done"], g)
                V.tensor_tensor(mine.rearrange("p (h d) -> p h d", d=DVA), mine.rearrange("p (h d) -> p h d", d=DVA),
                                fac[k][:, :, None].to_broadcast([P, H, DVA]), ALU.mult).then_inc(S["acc_scaled"], 1)
                return mine

            def accumulate(g, mine):
                dve.wait_ge(S["acc_scaled"], g + 1)
                dve.wait_ge(S["seg_done"], g + 1)
                V.tensor_tensor(mine, mine, bank[7][:, 0:AW], ALU.add).then_inc(S["acc_done"], 1)

            for n in range(RING - 1):
                starts(n, n, 0)
            products(0, 0)
            scores(0, 0)

            def step(g, k, i):
                inner = not isinstance(g, int)
                maxima(g, k, i)
                shifts(g, k)
                if inner or g + 1 < NG:
                    products(g + 1, (k + 1) % RING)
                if inner or g:
                    mine = shrink(g - 1, (k - 1) % RING)
                if inner or g + 1 < NG:
                    scores(g + 1, (k + 1) % RING)
                if inner or g:
                    accumulate(g - 1, mine)
                weighted(g, k)

            groups(dve, step)
            accumulate(NG - 1, shrink(NG - 1, RING - 1))

            dve.wait_ge(S["acc_done"], NG)
            dve.wait_ge(S["ex_small"], 16 * 4)

            def stepper(sem, turn, c, each):
                n = [0, 0]

                def did(ins):
                    n[0] += 1
                    ins.then_inc(sem, 1)

                def settle():
                    if isinstance(c, int):
                        dve.wait_ge(sem, c * each + n[0])
                    else:
                        wait_turn(dve, turn, [sem], steps=n[0] - n[1])
                    n[1] = n[0]

                return did, settle, n

            def norms(c):
                did, settle, n = stepper(S["prep"], prep_turn, c, PREP)

                def block_of(table, q):
                    return table[:, bass.ds(c * CB + q, 1), :].rearrange("p a d -> p (a d)")

                def moments(table):
                    for q in range(CB):
                        did(V.bn_stats(bst[:, q, :], block_of(table, q)))
                    settle()
                    for q in range(CB):
                        did(V.bn_aggr(cmv[:, q, :], bst[:, q, :]))
                    settle()
                    did(V.tensor_scalar(cstd[:, :], cmv[:, :, 1], LN_EPS, None, ALU.add))

                dve.wait_ge(S["residual"], 2 * c + 2)
                moments(xs)
                assert n[0] == HALF
                dve.wait_ge(S["prep_act"], 2 * c + 1)
                did(V.reciprocal(crstd[:, :], cstd[:, :]))
                settle()
                for q in range(CB):
                    did(V.tensor_scalar(block_of(hn, q), block_of(xs, q), cmv[:, q, 0:1], crstd[:, q:q + 1], ALU.subtract, ALU.mult))
                settle()
                moments(hn)
                dve.wait_ge(S["prep_act"], 2 * c + 2)
                did(V.reciprocal(crstd[:, :], cstd[:, :]))
                settle()
                for q in range(CB):
                    ins = V.tensor_scalar(block_of(hn, q), block_of(hn, q), cmv[:, q, 0:1], crstd[:, q:q + 1], ALU.subtract, ALU.mult)
                    if q + 1 < CB:
                        did(ins)
                    else:
                        ins.then_inc(S["norm_ready"], 1)
                dve.wait_ge(S["norm_ready"], c + 1)
                settle()
                assert n[0] == PREP, n[0]

            def router(c):
                did, settle, n = stepper(S["router"], router_turn, c, 2 * CB + 3)
                dve.wait_ge(S["logit_done"], c + 1)
                did(V.tensor_tensor(lg[:, :, :], bank[5][:, 0:CB * NX].rearrange("p (q e) -> p q e", e=NX),
                                    br_s[:, None, :].to_broadcast([P, CB, NX]), ALU.add))
                settle()
                for q in range(CB):
                    did(V.max(top[:, q, :], lg[:, q, :]))
                settle()
                for q in range(CB):
                    did(V.max_index(topi[:, q, :], top[:, q, :], lg[:, q, :]))
                settle()
                did(V.tensor_copy(tops[:, bass.ds(c * CB, CB), :], top[:, :, 0:TOP]))
                did(V.tensor_copy(topf[:, bass.ds(c * (CB * TOP), CB * TOP)].rearrange("p (q n) -> p q n", n=TOP), topi[:, :, 0:TOP]))
                settle()

            V.tensor_scalar(den[:, :], acc[:, :].rearrange("p (q d) -> p q d", d=DVA)[:, :, DV], DEN_EPS, None, ALU.add).then_inc(S["den"], 1)
            dve.wait_ge(S["den"], 1)
            V.reciprocal(den[:, :], den[:, :]).then_inc(S["den"], 1)
            norms(0)
            with dve.Fori(1, NCH) as c:
                norms(c)
                router(c - 1)
            router(NCH - 1)

            at = [0]

            def route(ins):
                at[0] += 1
                ins.then_inc(S["route"], 1)
                dve.wait_ge(S["route"], at[0])

            dve.wait_ge(S["rowc"], 7)
            route(V.tensor_tensor(hit[:, :, :], topf[:, None, :].to_broadcast([P, NX, NC]),
                                  iota[:, 0:NX, None].to_broadcast([P, NX, NC]), ALU.is_equal))
            route(V.tensor_tensor(e1[:, :], tops[:, :, 1], tops[:, :, 0], ALU.subtract))
            dve.wait_ge(S["route_pe"], 1)
            route(V.tensor_tensor_scan(upto[:, :, :].rearrange("p e c -> p (e c)"), inner1[:, :, :].rearrange("p e c -> p (e c)"),
                                       bank[6][:, 0:NX * NC], 0.0, ALU.mult, ALU.add))
            route(V.tensor_scalar(tiles_f[:, :], upto[:, :, NC - 1], float(P - 1), None, ALU.add))
            route(V.tensor_copy(tiles_i[:, :], tiles_f[:, :]))
            route(V.tensor_scalar(tiles_i[:, :], tiles_i[:, :], SHIFT, None, ALU.logical_shift_right))
            route(V.tensor_copy(tiles_f[:, :], tiles_i[:, :]))
            route(V.tensor_tensor_scan(tincl[:, :], tiles_f[:, :], tzero[:, :], 0.0, ALU.add, ALU.add))
            route(V.tensor_tensor(tbase[:, :], tincl[:, :], tiles_f[:, :], ALU.subtract))
            route(V.tensor_tensor(place[:, :, :].rearrange("p e c -> p (e c)"), upto[:, :, :].rearrange("p e c -> p (e c)"),
                                  bank[6][:, 0:NX * NC], ALU.subtract))
            route(V.tensor_tensor(place2[:, :, :].rearrange("p e c -> p (e c)"), place[:, :, :].rearrange("p e c -> p (e c)"),
                                  bank[7][:, 0:NX * NC], ALU.add))
            route(V.scalar_tensor_tensor(place[:, :, :], tbase[:, :, None].to_broadcast([P, NX, NC]), float(P), place2[:, :, :],
                                         ALU.mult, ALU.add))
            route(V.tensor_tensor(place2[:, :, :], place[:, :, :], hit[:, :, :], ALU.mult))
            route(V.tensor_reduce(slotf[:, :], place2[:, :, :].rearrange("p e c -> p c e"), AX_X, ALU.add))
            V.tensor_copy(slot[:, :], slotf[:, :]).then_inc(S["slot_ready"], 1)
            route(V.tensor_tensor(tle[:, :, :], tincl[0:BR, None, :].to_broadcast([BR, NT, NX]),
                                  iota[0:BR, 0:NT, None].to_broadcast([BR, NT, NX]), ALU.is_le))
            route(V.tensor_reduce(sel[:, :], tle[:, :, :], AX_X, ALU.add))
            route(V.tensor_scalar(texp[:, :], sel[:, :], float(NX - 1), None, ALU.min))
            route(V.tensor_copy(texp_i[:, :], texp[0:1, :]))
            route(V.scalar_tensor_tensor(rowexp[:, :], rowm[:, 0:1], float(-NX), row[:, :], ALU.mult, ALU.add))
            route(V.scalar_tensor_tensor(rowm[:, 2:3], rowm[:, 1:2], float(-NX), rowexp[:, :], ALU.mult, ALU.add))
            route(V.tensor_scalar(sel[:, :], texp[:, :], rowm[:, 2:3], None, ALU.is_equal))
            tiles_known = at[0]
            dve.wait_ge(S["hb_raw"], 16 * 2 * PARTS)
            left = hb
            for n in range(PARTS):
                route(V.tensor_copy(hbpart[n][:, :], left[:, :]))
                if n + 1 < PARTS:
                    route(V.tensor_tensor(hbres[n][:, :], left[:, :], hbpart[n][:, :], ALU.subtract))
                    left = hbres[n]
            route(V.tensor_tensor(rowm[:, 3:4], rowm[:, 0:1], rowm[:, 1:2], ALU.subtract))
            route(V.tensor_scalar(rowexp[:, :], rowm[:, 0:1], -1.0, 1.0, ALU.mult, ALU.add))
            route(V.tensor_scalar(hb[:, :], hbpart[0][:, :], rowexp[:, :], None, ALU.mult))
            route(V.scalar_tensor_tensor(hbres[0][:, :], hbpart[1][:, :], rowm[:, 3:4], hb[:, :], ALU.mult, ALU.add))
            route(V.scalar_tensor_tensor(hbst[:, :], hbpart[2][:, :], rowm[:, 1:2], hbres[0][:, :], ALU.mult, ALU.add))
            dve.wait_ge(S["route_act"], 1)
            route(V.tensor_scalar(w1[:, :], e1[:, :], 1.0, None, ALU.add))
            route(V.reciprocal(w0[:, :], w1[:, :]))
            route(V.tensor_tensor(w1[:, :], w0[:, :], e1[:, :], ALU.mult))
            assert at[0] == ROUTE, at[0]

            def choose(t, k):
                ge(dve, S["y_done"], t - TR + 1)
                V.tensor_copy(selw[k][:, :], sel[:, bass.ds(t, 1)].to_broadcast([BR, P])).then_inc(S["sel_ready"], 1)

            def copy_hidden(t, k):
                dve.wait_ge(S["th_done"], t + 1)
                ge(dve, S["y_done"], t - TR + 1)
                V.tensor_copy(hidT[k][:, :], bank[4][:, :]).then_inc(S["hT_copied"], 1)

            def copy_results(t, k, i):
                dve.wait_ge(S["y_done"], t + 1)
                ge(dve, S[f"stored{k}"], 16 * i)
                V.tensor_copy(yt[k][:, :], bank[5 + k][:, 0:DIM]).then_inc(S["y_copied"], 1)

            choose(0, 0)
            choose(1, 1)

            def results(t, k, i):
                copy_hidden(t, k)
                if not isinstance(t, int) or t + 2 < NT:
                    choose(t + 2, (k + 2) % TR)
                copy_results(t, k, i)

            tiles(dve, results)

            with dve.Fori(0, NCH) as c:
                for k in range(CB):
                    b = c * CB + k
                    xb = xs[:, bass.ds(b, 1), :].rearrange("p a d -> p (a d)")
                    dve.wait_ge(S[f"yg_ready{k}"], 16 * TOP * (c + 1))
                    V.scalar_tensor_tensor(xb, yg[k][:, 0, :], w0[:, bass.ds(b, 1)], xb, ALU.mult, ALU.add).then_inc(S["combined"], 1)
                    dve.wait_ge(S["combined"], TOP * b + 1)
                    V.scalar_tensor_tensor(xb, yg[k][:, 1, :], w1[:, bass.ds(b, 1)], xb, ALU.mult, ALU.add).then_inc(S["combined"], 1)

        @block.scalar
        def _(act):
            A = nc.scalar
            act.wait_ge(S["in_x"], 32)
            with act.Fori(0, NCH) as c:
                for t in (c * CB + q for q in range(CB)):
                    A.activation(kvrow[:, :], xs[:, bass.ds(t, 1), :].rearrange("p a d -> p (a d)"), ACT.Copy,
                                 accum_out=xsum[:, bass.ds(t, 1)]).then_inc(S["moments"], 1)
                    act.wait_ge(S["moments"], t + 1)
            A.activation(negmean[:, :], xsum[:, :], ACT.Copy, scale=-1.0 / DIM).then_inc(S["moments"], 1)
            act.wait_ge(S["moments"], NB + 1)
            with act.Fori(0, NCH) as c:
                for t in (c * CB + q for q in range(CB)):
                    A.activation(kvrow[:, :], xs[:, bass.ds(t, 1), :].rearrange("p a d -> p (a d)"), ACT.Square,
                                 bias=negmean[:, bass.ds(t, 1)], accum_out=xsq[:, bass.ds(t, 1)]).then_inc(S["moments"], 1)
                    act.wait_ge(S["moments"], t + NB + 2)
            act.wait_ge(S["lnchain"], 1)
            A.activation(std[:, :], std[:, :], ACT.Sqrt).then_inc(S["lnchain"], 1)

            def copy_xT(t):
                act.wait_ge(S["xT_done"], t + 1)
                ge(act, S["qkv_done"], t)
                A.activation(xlT[:, :], bank[3][:, 0:DIM], ACT.Copy).then_inc(S["xT_copied"], 1)

            def first_part(t):
                act.wait_ge(S["table_ready"], t + 1)
                ge(act, S["kv_stored"], 32 * t)
                ge(act, S["qtab_ready"], t)
                A.activation(qkp[:, 0, :], qk32[:, :], ACT.Copy).then_inc(S["qkp1"], 1)

            def second_part(t):
                act.wait_ge(S["qk_chain"], t + 1)
                A.activation(qkp[:, 1, :], qkres[:, :], ACT.Copy).then_inc(S["qkp2"], 1)

            def keep_queries(t):
                act.wait_ge(S["qkp3"], t + 1)
                A.activation(q_tab[:, bass.ds(t, 1), :, :].rearrange("p t a c -> p (t a) c"), qkp[:, :, 0:DH], ACT.Copy)\
                    .then_inc(S["qtab_ready"], 1)

            act.wait_ge(S["in_ea"], 32)
            act.wait_ge(S["recb_const"], 9)
            act.wait_ge(S["chain"], 5)

            def batch(i, k):
                ge(act, S[f"scat{k}"], (i - k) * (8 * TB))
                A.activation(recb[k][:, :, F_T:F_T + 1].rearrange("p j r -> p (j r)").bitcast(I32), t_i[:, bass.ds(i * TB, TB)], ACT.Copy)
                A.activation(recb[k][:, :, F_S:F_S + 1].rearrange("p j r -> p (j r)"), s_f[:, bass.ds(i * TB, TB)], ACT.Copy)
                A.activation(recb[k][:, :, F_B:F_B + 1].rearrange("p j r -> p (j r)"), b_f[:, bass.ds(i * TB, TB)], ACT.Copy, scale=-1.0)
                raw = ea_raw[:, bass.ds(i * (TB * NA), TB * NA)].rearrange("p (j a) -> p j a", a=NA)
                parts = recb[k][:, :, F_EA:RW].bitcast(BF16).rearrange("p j (b a) -> p j b a", a=AUG)
                for b in (0, 3, 5):
                    ins = A.activation(parts[:, :, b, 0:NA], raw, ACT.Copy)
                ins.then_inc(S["e1_ready"], 1)
                act.wait_ge(S["eres_ready"], i + 1)
                A.activation(parts[:, :, 1, 0:NA], eres[k][:, :, :], ACT.Copy).then_inc(S["e2_ready"], 1)
                A.activation(parts[:, :, 4, 0:NA], eres[k][:, :, :], ACT.Copy).then_inc(S["recb_ready"], 1)

            def turned_places(i, k):
                act.wait_ge(S["loB_used"], i + 1)
                ge(act, S["lk_done"], i - 1)
                A.activation(loBT[k][:, :, 0:EP], bank[2][:, :].bitcast(BF16).rearrange("p (j e) -> p j e", e=P)[:, :, 0:EP],
                             ACT.Copy).then_inc(S["loBT_ready"], 1)

            def pair(i):
                batch(2 * i, 0)
                if not isinstance(i, int) or i:
                    second_part(i - 1)
                copy_xT(i)
                turned_places(2 * i + 1, 1)
                if not isinstance(i, int) or i:
                    keep_queries(i - 1)
                batch(2 * i + 1, 1)
                if not isinstance(i, int) or i + 1 < NB:
                    turned_places(2 * i + 2, 0)
                first_part(i)

            turned_places(0, 0)
            pair(0)
            with act.Fori(1, NB - 1) as i:
                pair(i)
            pair(NB - 1)
            second_part(NB - 1)
            keep_queries(NB - 1)

            def onehots(g, k, i):
                act.wait_ge(S[f"rec_ready{k}"], 32 * i + 32)
                ge(act, S["oh_ready"], g)
                ge(act, S["tr_oh"], g - 1)
                ge(act, S["oh32_ready"], g - 1)
                for j in range(G):
                    ins = A.activation(away[:, j, :], iota[:, :], ACT.Abs, bias=rec[k][:, j, F_B:F_B + 1])
                ins.then_inc(S["away_ready"], 1)
                act.wait_ge(S["away_ready"], g + 1)
                A.activation(oh[k % 2][:, :, :], away[:, :, :], ACT.Relu, scale=-1.0, bias=1.0).then_inc(S["oh_ready"], 1)

            def turned(g, k):
                act.wait_ge(S["tr_oh"], g + 1)
                ge(act, S["qk_done"], g - 1)
                A.activation(ohT[k % 2][:, :], bank[0][:, :].bitcast(BF16)[:, 0:GS], ACT.Copy).then_inc(S["oht_copied"], 1)
                act.wait_ge(S["tr_ea"], g + 1)
                A.activation(eaT[k % 2][:, :], bank[1][0:STK, :].bitcast(BF16)[:, 0:GS], ACT.Copy).then_inc(S["eat_copied"], 1)
                act.wait_ge(S["tr_s"], g + 1)
                ge(act, S["sm_ready"], g - RING + 1)
                A.activation(pen[k][:, 0:GS], bank[2][0:H, :], ACT.Copy, scale=LOW).then_inc(S["pen_ready"], 1)
                ge(act, S["seg_done"], g - RING + 1)
                A.activation(oh32[k][:, :, :], oh[k % 2][:, :, :], ACT.Copy).then_inc(S["oh32_ready"], 1)

            def keys(g, k):
                act.wait_ge(S["qk_done"], g + 1)
                ge(act, S["prod_done"], 2 * g)
                for a in range(2):
                    ins = A.activation(ke[:, 2 * a:2 * a + 2, :],
                                       bank[3 + a][:, :].rearrange("p (j c) -> p j c", c=2 * DH)[:, :, DH:2 * DH], ACT.Copy)
                ins.then_inc(S["ke_ready"], 1)

            def exps(g, k):
                act.wait_ge(S["diff_ready"], g + 1)
                ge(act, S["seg_done"], g - 1)
                A.activation(wv[k % 2][:, :, :, DV], diff[k][:, :, :], ACT.Exp).then_inc(S["w_exp"], 1)

            def factor(g, k):
                act.wait_ge(S["f_done"], g + 1)
                A.activation(fac[k][:, :], bank[6][:, 0:H], ACT.Exp, scale=-1.0).then_inc(S["fac_ready"], 1)

            act.wait_ge(S["init_ready"], 4)
            onehots(0, 0, 0)
            onehots(1, 1, 0)
            turned(0, 0)
            onehots(2, 2, 0)
            turned(1, 1)
            keys(0, 0)
            onehots(3, 3, 0)
            turned(2, 2)
            keys(1, 1)

            def step(g, k, i):
                inner = not isinstance(g, int)
                exps(g, k)
                if inner or g + RING < NG:
                    onehots(g + RING, k, i + 1)
                factor(g, k)
                if inner or g + 3 < NG:
                    turned(g + 3, (k + 3) % RING)
                if inner or g + 2 < NG:
                    keys(g + 2, (k + 2) % RING)

            groups(act, step)

            act.wait_ge(S["ex_small"], 16 * 4)

            def roots(c):
                for n in range(2):
                    act.wait_ge(S["prep"], c * PREP + (HALF if n == 0 else PREP - CB))
                    A.activation(cstd[:, :], cstd[:, :], ACT.Sqrt).then_inc(S["prep_act"], 1)

            def normed_turned(c):
                act.wait_ge(S["hnT_done"], c + 1)
                ge(act, S["logit_done"], c)
                for k in range(KD):
                    A.activation(xnT[:, k, 0:4 * P], bank[k][:, :], ACT.Identity, scale=gamT[:, k:k + 1], bias=betT[:, k:k + 1])
                    ins = A.activation(xnT[:, k, 4 * P:CB * P], bank[2][:, k * P:(k + 1) * P], ACT.Identity,
                                       scale=gamT[:, k:k + 1], bias=betT[:, k:k + 1])
                ins.then_inc(S["xnT_ready"], 1)

            roots(0)
            normed_turned(0)
            with act.Fori(1, NCH) as c:
                roots(c)
                normed_turned(c)
            act.wait_ge(S["route"], 2)
            A.activation(e1[:, :], e1[:, :], ACT.Exp).then_inc(S["route_act"], 1)

            def copy_tile(t, k):
                act.wait_ge(S["tx_done"], t + 1)
                ge(act, S["h_done"], t - TR + 1)
                for a in range(KD):
                    ins = A.activation(xtT[k][:, a, :], bank[0][:, a * P:(a + 1) * P], ACT.Identity,
                                       scale=gamT[:, a:a + 1], bias=betT[:, a:a + 1])
                ins.then_inc(S["xt_copied"], 1)

            def gelu(t, k):
                act.wait_ge(S["h_done"], t + 1)
                ge(act, S["th_done"], t - TR + 1)
                A.activation(hid[k][:, :], bank[1 + k][:, :], ACT.Gelu).then_inc(S["gelu_done"], 1)

            copy_tile(0, 0)
            copy_tile(1, 1)
            gelu(0, 0)

            def activate(t, k, i):
                inner = not isinstance(t, int)
                if inner or t + 1 < NT:
                    gelu(t + 1, (k + 1) % TR)
                if inner or t + 2 < NT:
                    copy_tile(t + 2, (k + 2) % TR)

            tiles(act, activate)

        @block.tensor
        def _(pe):
            T = nc.tensor
            maxima_turn = pe.alloc_register("maxima_turn")
            pe.reg_mov(maxima_turn, RING + 1)
            pe.wait_ge(S["a_ready"], 4)

            def histogram(i, k):
                pe.wait_ge(S["onehot"], i + 1)
                for j in range(TB):
                    mm = T.matmul(bank[7][:, 0:NB], loB[k][:, j, :],
                                  hiA[:, bass.ds(i * TB + j, 1), :].rearrange("p a n -> p (a n)"),
                                  start=(isinstance(i, int) and i == 0 and j == 0),
                                  stop=(isinstance(i, int) and i == NBATCH - 1 and j == TB - 1), skip_group_check=True)
                mm.then_inc(S["hist"], 1)

            batches(pe, histogram)
            pe.wait_ge(S["consts"], 9)
            pe.wait_ge(S["tot_sb"], 1)
            T.matmul(bank[7][:, 64:64 + NB], ones[:, :], tot[:, :], start=True, stop=True, skip_group_check=True)
            T.matmul(bank[7][:, 128:128 + NB], upper[:, :], tot[:, :], start=True, stop=True,
                     skip_group_check=True).then_inc(S["base_mm"], 1)

            pe.wait_ge(S["in_w"], 32)

            def turn_x(t):
                pe.wait_ge(S["normed"], t + 1)
                ge(pe, S["xT_copied"], t)
                for a in range(KD):
                    mm = T.transpose(bank[3][:, a * P:(a + 1) * P], xl[:, a * P:(a + 1) * P], ident[:, :])
                mm.then_inc(S["xT_done"], 1)

            def project(t):
                pe.wait_ge(S["xT_copied"], t + 1)
                ge(pe, S["table_ready"], t)
                for a in range(KD):
                    mm = T.matmul(bank[7][:, :], xlT[:, a * P:(a + 1) * P], Wqkv_s[:, a, :],
                                  start=(a == 0), stop=(a == KD - 1))
                mm.then_inc(S["qkv_done"], 1)

            pe.wait_ge(S["identb_ready"], 1)
            pe.wait_ge(S["base_ready"], 2)

            def tile_counts(i, k):
                pe.wait_ge(S["loB_ready"], i + 1)
                ge(pe, S["cnt_ready"], (i - 1) * TB)
                ge(pe, S["loBT_ready"], i)
                for j in range(TB):
                    T.matmul(bank[k][:, j * NB:(j + 1) * NB], loB[k][:, j, :],
                             hiA[:, bass.ds(i * TB + j, 1), :].rearrange("p a n -> p (a n)"),
                             start=True, stop=True, skip_group_check=True)
                for j in range(TB):
                    mm = T.transpose(bank[2][:, :].bitcast(BF16)[:, j * P:j * P + EP], loB[k][:, j, :], identb[0:EP, 0:EP])
                mm.then_inc(S["loB_used"], 1)

            def spread_sources(i, k):
                ge(pe, S["within_ready"], i * TB)
                for j in range(TB):
                    for n in range(2):
                        mm = T.matmul(bank[4 + j // 4][0:EP, (j % 4) * P:(j % 4) * P + EP],
                                      srcb[:, bass.ds(i * TB + j, 1), n].to_broadcast([EP, EP]), identb[0:EP, 0:EP],
                                      start=(n == 0), stop=(n == 1), skip_group_check=True)
                mm.then_inc(S["sbc_done"], 1)

            def look_up(i, k):
                pe.wait_ge(S["loBT_ready"], i + 1)
                pe.wait_ge(S["cnt_ready"], (i + 1) * TB)
                ge(pe, S["pos_chain"], 2 * i)
                for j in range(TB):
                    mm = T.matmul(bank[6][0:EP, j * NB:(j + 1) * NB], loBT[k][:, j, 0:EP], cnt[k][:, j, :],
                                  start=True, stop=True, skip_group_check=True)
                mm.then_inc(S["lk_done"], 1)

            def pair(i):
                more = not isinstance(i, int) or i + 1 < NB
                look_up(2 * i, 0)
                tile_counts(2 * i + 1, 1)
                project(i)
                spread_sources(2 * i + 1, 1)
                look_up(2 * i + 1, 1)
                if more:
                    tile_counts(2 * i + 2, 0)
                    spread_sources(2 * i + 2, 0)
                    turn_x(i + 1)

            turn_x(0)
            tile_counts(0, 0)
            spread_sources(0, 0)
            pair(0)
            with pe.Fori(1, NB - 1) as i:
                pair(i)
            pair(NB - 1)

            after_sort(pe)
            pe.wait_ge(S["wstk"], 2 * PARTS + 5)
            pe.wait_ge(S["blk_ready"], 1)
            pe.wait_ge(S["qtab_ready"], NB)

            def turn_edges(g, k, i):
                pe.wait_ge(S["oh_ready"], g + 1)
                ge(pe, S["oht_copied"], g)
                for j in range(G):
                    mm = T.transpose(bank[0][:, :].bitcast(BF16)[:, j * P:(j + 1) * P], oh[k % 2][:, j, :], identb[:, :])
                mm.then_inc(S["tr_oh"], 1)
                pe.wait_ge(S[f"rec_ready{k}"], 32 * i + 32)
                ge(pe, S["eat_copied"], g)
                for j in range(G):
                    mm = T.transpose(bank[1][0:STK, :].bitcast(BF16)[:, j * P:(j + 1) * P], rec[k][:, j, F_EA:RW].bitcast(BF16),
                                     identb[:, :])
                mm.then_inc(S["tr_ea"], 1)
                pe.wait_ge(S["new_ready"], g + 1)
                ge(pe, S["pen_ready"], g)
                for j in range(G):
                    mm = T.matmul(bank[2][0:H, j::G], new[k % 2][:, j:j + 1].to_broadcast([P, H]), identb[:, :],
                                  start=True, stop=True, skip_group_check=True)
                mm.then_inc(S["tr_s"], 1)

            def queries_keys(g, k, i):
                here = pe.value_load(blk_i[0:1, bass.ds(g, 1)], min_val=0, max_val=NB - 1)
                pe.wait_ge(S["oht_copied"], g + 1)
                pe.wait_ge(S["eat_copied"], g + 1)
                pe.wait_ge(S[f"kv_ready{k}"], (16 * G) * i + 16 * G)
                ge(pe, S["prod_done"], 2 * g)
                for j in range(G):
                    o = bank[3 + j // 2][:, (j % 2) * 2 * DH:(j % 2 + 1) * 2 * DH]
                    T.matmul(o, eaT[k % 2][:, j * P:(j + 1) * P], Wrpe[:, :], start=True, stop=False, skip_group_check=True)
                    for a in range(PARTS):
                        T.matmul(o[:, 0:DH], ohT[k % 2][:, j * P:(j + 1) * P],
                                 q_tab[:, bass.ds(here, 1), a, :].rearrange("p b c -> p (b c)"), start=False, stop=False,
                                 skip_group_check=True)
                    for a in range(PARTS):
                        mm = T.matmul(o[:, DH:2 * DH], identb[:, :], kv[k][:, j, 0:KW].bitcast(BF16)[:, a * DH:(a + 1) * DH],
                                      start=False, stop=(a == PARTS - 1), skip_group_check=True)
                mm.then_inc(S["qk_done"], 1)

            def turn_scores(g, k):
                pe.wait_ge(S["c_ready"], g + 1)
                ge(pe, S["fw_ready"], g)
                for j in range(G):
                    mm = T.transpose(bank[5][0:H, j::G], cc[k % 2][:, j, :], ident[:, :])
                mm.then_inc(S["ct_done"], 1)

            def turn_maxima(g, k):
                if isinstance(g, int):
                    pe.wait_ge(S["sm_ready"], g + 1)
                    ge(pe, S["dbuf_ready"], g)
                    ge(pe, S["fac_ready"], g)
                else:
                    wait_turn(pe, maxima_turn, [S["sm_ready"]], [(S["dbuf_ready"], g), (S["fac_ready"], g)])
                for j in range(G):
                    T.transpose(bank[6][:, j * H:(j + 1) * H], segm[:, j::G], ident[0:H, 0:H])
                T.transpose(bank[6][:, G * H:(G + 1) * H], dbuf[:, :], ident[0:H, 0:H]).then_inc(S["smt_done"], 1)

            def growth(g, k):
                pe.wait_ge(S["dT_ready"], g + 1)
                pe.wait_ge(S["oh32_ready"], g + 1)
                T.matmul(bank[6][:, 0:H], oh32[k][:, 0, :], dT[k][:, :], start=True, stop=True,
                         skip_group_check=True).then_inc(S["f_done"], 1)

            def segment_sums(g, k):
                pe.wait_ge(S["w_ready"], g + 1)
                ge(pe, S["acc_done"], g)
                for j in range(G):
                    mm = T.matmul(bank[7][:, 0:AW], oh32[k][:, j, :], wv[k % 2][:, j, :, :].rearrange("p h d -> p (h d)"),
                                  start=(j == 0), stop=(j == G - 1))
                mm.then_inc(S["seg_done"], 1)

            turn_edges(0, 0, 0)
            turn_edges(1, 1, 0)
            queries_keys(0, 0, 0)
            turn_edges(2, 2, 0)
            turn_scores(0, 0)
            queries_keys(1, 1, 0)

            def step(g, k, i):
                inner = not isinstance(g, int)
                turn_maxima(g, k)
                if inner or g:
                    segment_sums(g - 1, (k - 1) % RING)
                growth(g, k)
                if inner or g + 3 < NG:
                    turn_edges(g + 3, (k + 3) % RING, i + (k + 3) // RING)
                if inner or g + 1 < NG:
                    turn_scores(g + 1, (k + 1) % RING)
                if inner or g + 2 < NG:
                    queries_keys(g + 2, (k + 2) % RING, i + (k + 2) // RING)

            groups(pe, step)
            segment_sums(NG - 1, RING - 1)

            pe.wait_ge(S["acc_done"], NG)
            pe.wait_ge(S["ex_small"], 16 * 4)

            def turn_normed(c):
                pe.wait_ge(S["norm_ready"], c + 1)
                ge(pe, S["xnT_ready"], c)
                for k in range(KD):
                    for q in range(CB):
                        o = bank[k][:, q * P:(q + 1) * P] if q < 4 else bank[2][:, k * P:(k + 1) * P]
                        mm = T.transpose(o, hn[:, c * CB + q, k * P:(k + 1) * P], ident[:, :])
                mm.then_inc(S["hnT_done"], 1)

            def logits(c):
                pe.wait_ge(S["xnT_ready"], c + 1)
                ge(pe, S["router"], (c - 1) * (2 * CB + 3) + 1)
                for q in range(CB):
                    for k in range(KD):
                        mm = T.matmul(bank[5][:, q * NX:(q + 1) * NX], xnT[:, k, q * P:(q + 1) * P], Wr_s[:, k, :],
                                      start=(k == 0), stop=(k == KD - 1), skip_group_check=True)
                mm.then_inc(S["logit_done"], 1)

            for c in range(NCH):
                turn_normed(c)
                logits(c)

            pe.wait_ge(S["route"], 1)
            T.matmul(bank[6][:, 0:NX * NC], ones[:, :], hit[:, :, :].rearrange("p e c -> p (e c)"), start=True, stop=True)
            T.matmul(bank[7][:, 0:NX * NC], upper[:, :], hit[:, :, :].rearrange("p e c -> p (e c)"), start=True, stop=True)\
                .then_inc(S["route_pe"], 1)
            pe.wait_ge(S["ex_w"], 16 * (KD + MH))
            pe.wait_ge(S["route"], ROUTE)

            def turn_tile(t, k, i):
                pe.wait_ge(S[f"xt_ready{k}"], 16 * i + 16)
                ge(pe, S["xt_copied"], t)
                for a in range(KD):
                    mm = T.transpose(bank[0][:, a * P:(a + 1) * P], xt[k][:, a * P:(a + 1) * P], ident[:, :])
                mm.then_inc(S["tx_done"], 1)

            def expert_of(t):
                return pe.value_load(texp_i[0:1, bass.ds(t, 1)], min_val=0, max_val=NX - 1)

            def hidden(t, k):
                ex = expert_of(t)
                pe.wait_ge(S["xt_copied"], t + 1)
                pe.wait_ge(S["sel_ready"], t + 1)
                ge(pe, S["gelu_done"], t - TR + 1)
                T.matmul(bank[1 + k][:, :], selw[k][:, :], hbst[:, 0:HID], start=True, stop=False)
                for a in range(KD):
                    mm = T.matmul(bank[1 + k][:, :], xtT[k][:, a, :], W1s[:, a, bass.ds(ex * HID, HID)],
                                  start=False, stop=(a == KD - 1))
                mm.then_inc(S["h_done"], 1)

            def turn_hidden(t, k):
                pe.wait_ge(S["gelu_done"], t + 1)
                ge(pe, S["hT_copied"], t)
                for m in range(MH):
                    mm = T.transpose(bank[4][:, m * P:(m + 1) * P], hid[k][:, m * P:(m + 1) * P], ident[:, :])
                mm.then_inc(S["th_done"], 1)

            def output(t, k):
                ex = expert_of(t)
                pe.wait_ge(S["hT_copied"], t + 1)
                ge(pe, S["y_copied"], t - TR + 1)
                T.matmul(bank[5 + k][:, 0:DIM], selw[k][:, :], hbst[:, HID:HB], start=True, stop=False)
                for m in range(MH):
                    mm = T.matmul(bank[5 + k][:, 0:DIM], hidT[k][:, m * P:(m + 1) * P], W2s[:, m, bass.ds(ex * DIM, DIM)],
                                  start=False, stop=(m == MH - 1))
                mm.then_inc(S["y_done"], 1)

            turn_tile(0, 0, 0)
            turn_tile(1, 1, 0)
            hidden(0, 0)

            def multiply(t, k, i):
                inner = not isinstance(t, int)
                turn_hidden(t, k)
                if inner or t + 1 < NT:
                    hidden(t + 1, (k + 1) % TR)
                if inner or t + 2 < NT:
                    turn_tile(t + 2, (k + 2) % TR, i + (k + 2) // TR)
                output(t, k)

            tiles(pe, multiply)


INPUTS = ['x', 'src', 'dst', 'edge_attr_18', 'L0_gnn_Wqkv', 'L0_gnn_bqkv', 'L0_gnn_Wk_rpe', 'L0_gnn_bk_rpe',
          'L0_gnn_Wq_rpe', 'L0_gnn_bq_rpe', 'L0_ffn_gamma', 'L0_ffn_beta', 'L0_ffn_Wr', 'L0_ffn_br', 'L0_ffn_W1',
          'L0_ffn_b1', 'L0_ffn_W2', 'L0_ffn_b2']


def kernel(**inputs):
    import numpy as _np
    import concourse.bacc as _bacc
    from concourse import mybir as _mybir
    from concourse.bass_utils import run_bass_kernel_spmd as _run

    nc = _bacc.Bacc("TRN2", target_bir_lowering=False, num_devices=1)
    arrays, args = {}, []
    for name in INPUTS:
        a = _np.ascontiguousarray(inputs[name])
        arrays[f"in_{name}"] = a
        args.append(nc.dram_tensor(f"in_{name}", a.shape, _mybir.dt.from_np(a.dtype), kind="ExternalInput").ap())
    shape = tuple(inputs['x'].shape)
    args.append(nc.dram_tensor("out_x", shape, _mybir.dt.from_np(_np.dtype("float32")), kind="ExternalOutput").ap())
    gnn_ffn(nc, *args)
    r = _run(nc, [arrays], core_ids=[0])
    return r.results[0]["out_x"]
```
